# Optimizing a Trainium2 kernel written in Bass

```python
import numpy as np
import jax
import jax.numpy as jnp

def _softmax(x, axis=-1):
    return jax.nn.softmax(x, axis=axis)

def _gelu(x):
    return jax.nn.gelu(x, approximate=True)

def _silu(x):
    return jax.nn.silu(x)

def _sigmoid(x):
    return jax.nn.sigmoid(x)

def _layernorm(x, axis=-1, eps=1e-05):
    m = jnp.mean(x, axis=axis, keepdims=True)
    v = jnp.var(x, axis=axis, keepdims=True)
    return (x - m) / jnp.sqrt(v + eps)

def _scatter_add(tgt, idx, src, axis=0):
    return tgt.at[idx].add(src)

def _segment_sum(src, seg, n):
    return jax.ops.segment_sum(src, seg, n)
kernel_name = 'mk_early_fusion_d1_tok_img768_r4_c45caa'

def setup_inputs(seed: int=0):
    np.random.seed(seed)
    _w = jnp.asarray

    def _rec_inputs():
        import jax
        import jax.numpy as jnp
        _rk = jax.random.key(seed)
        x = -0.00016672 + 0.999947 * jax.random.normal(jax.random.fold_in(_rk, 1), (8, 3, 96, 96), jnp.float32)
        txt = -3.52942e-05 + 0.577782 * jax.random.normal(jax.random.fold_in(_rk, 2), (8, 128, 192), jnp.float32)
        return (x, txt)
    x, txt = _rec_inputs()

    def _L0_tok_setup():
        import jax, jax.numpy as jnp
        import numpy as np
        P1, P2 = (16, 16)
        EMBED = 192

        def _patchify(images):
            B, C, H, W = images.shape
            h, w = (H // P1, W // P2)
            x = images.reshape(B, C, h, P1, w, P2)
            x = x.transpose(0, 2, 4, 3, 5, 1)
            return x.reshape(B, h * w, P1 * P2 * C)
        key = jax.random.key(seed)
        k1, k2, k3 = jax.random.split(key, 3)
        B, C, H, W = (64, 3, 96, 96)
        images = jax.random.normal(k1, (B, C, H, W), dtype=jnp.float32)
        patch_dim = P1 * P2 * C
        bound = 1.0 / np.sqrt(patch_dim)
        W_lin = jax.random.uniform(k2, (EMBED, patch_dim), minval=-bound, maxval=bound, dtype=jnp.float32)
        b_lin = jax.random.uniform(k3, (EMBED,), minval=-bound, maxval=bound, dtype=jnp.float32)
        return {'images': images, 'W_lin': W_lin, 'b_lin': b_lin}
    _L0_tok_all = _L0_tok_setup()
    _L0_tok_in = {k: v for k, v in _L0_tok_all.items() if k in ('W_lin', 'b_lin')}
    del _L0_tok_all

    def _L0_attn_setup():
        import jax, jax.numpy as jnp
        import numpy as np
        NUM_HEADS = 12
        BITS_W = 8
        BITS_A = 8
        BITS_S = 4
        EPS = 1.1920928955078125e-07

        def fq_weight(w):
            qmin, qmax = (-2 ** (BITS_W - 1), 2 ** (BITS_W - 1) - 1)
            mn = jnp.minimum(w.min(axis=1, keepdims=True), 0.0)
            mx = jnp.maximum(w.max(axis=1, keepdims=True), 0.0)
            scale = jnp.maximum((mx - mn) / float(qmax - qmin), EPS)
            zp = qmin - jnp.round(mn / scale)
            wq = jnp.clip(jnp.round(w / scale) + zp, qmin, qmax)
            return (wq - zp) * scale

        def fq_act(x):
            qmin, qmax = (-2 ** (BITS_A - 1), 2 ** (BITS_A - 1) - 1)
            mn = jnp.minimum(x.min(), 0.0)
            mx = jnp.maximum(x.max(), 0.0)
            scale = jnp.maximum((mx - mn) / float(qmax - qmin), EPS)
            zp = qmin - jnp.round(mn / scale)
            xq = jnp.clip(jnp.round(x / scale) + zp, qmin, qmax)
            return ((xq - zp) * scale, scale)

        def int_log_softmax(x, scale):
            x_int = x / scale
            x_int = x_int - x_int.max(axis=-1, keepdims=True)
            x0, n = (-0.6931, 30)
            x0_int = jnp.floor(x0 / scale)
            x_int = jnp.maximum(x_int, n * x0_int)
            q = jnp.floor(x_int / x0_int)
            r = x_int - x0_int * q
            c0 = 0.35815147
            b_int = jnp.floor(0.96963238 / c0 / scale)
            c_int = jnp.floor(1.0 / c0 / (scale * scale))
            z = r * (r + b_int) + c_int
            exp_int = jnp.clip(jnp.floor(z * jnp.exp2(n - q)), 0.0, None)
            exp_sum = exp_int.sum(axis=-1, keepdims=True)
            sm = jnp.round(exp_sum / exp_int)
            big = jnp.floor(jnp.log2(sm))
            big = jnp.where(sm - jnp.exp2(big) >= jnp.exp2(big - 1.0), big + 1.0, big)
            mask = big >= float(2 ** BITS_S)
            qlog = jnp.clip(big, 0.0, float(2 ** BITS_S - 1))
            return jnp.where(mask, 0.0, jnp.exp2(-qlog))
        key = jax.random.key(seed)
        ks = jax.random.split(key, 5)
        B, N, C = (16, 577, 192)
        return {'x': jax.random.normal(ks[0], (B, N, C), jnp.float32), 'w_qkv': jax.random.normal(ks[1], (3 * C, C), jnp.float32) * 0.02, 'b_qkv': jax.random.normal(ks[2], (3 * C,), jnp.float32) * 0.02, 'w_proj': jax.random.normal(ks[3], (C, C), jnp.float32) * 0.02, 'b_proj': jax.random.normal(ks[4], (C,), jnp.float32) * 0.02}
    _L0_attn_all = _L0_attn_setup()
    _L0_attn_in = {k: v for k, v in _L0_attn_all.items() if k in ('w_qkv', 'b_qkv', 'w_proj', 'b_proj')}
    del _L0_attn_all

    def _L0_ffn_setup():
        import jax, jax.numpy as jnp
        import numpy as np
        CAPACITY_FACTOR = 1.25
        key = jax.random.key(seed)
        ks = jax.random.split(key, 5)
        B, S, D, F, E = (8, 512, 192, 768, 8)
        return {'x': jax.random.normal(ks[0], (B, S, D), jnp.float32), 'switch_w': jax.random.normal(ks[1], (D, E), jnp.float32) * 0.02, 'switch_b': jnp.zeros((E,), jnp.float32), 'w1': jax.random.normal(ks[2], (E, D, F), jnp.float32) * 0.02, 'b1': jnp.zeros((E, F), jnp.float32), 'w2': jax.random.normal(ks[3], (E, F, D), jnp.float32) * 0.02, 'b2': jnp.zeros((E, D), jnp.float32)}
    _L0_ffn_all = _L0_ffn_setup()
    _L0_ffn_in = {k: v for k, v in _L0_ffn_all.items() if k in ('switch_w', 'switch_b', 'w1', 'b1', 'w2', 'b2')}
    del _L0_ffn_all
    return {'x': x, 'txt': txt, 'L0_tok_W_lin': _L0_tok_in['W_lin'], 'L0_tok_b_lin': _L0_tok_in['b_lin'], 'L0_attn_w_qkv': _L0_attn_in['w_qkv'], 'L0_attn_b_qkv': _L0_attn_in['b_qkv'], 'L0_attn_w_proj': _L0_attn_in['w_proj'], 'L0_attn_b_proj': _L0_attn_in['b_proj'], 'L0_ffn_switch_w': _L0_ffn_in['switch_w'], 'L0_ffn_switch_b': _L0_ffn_in['switch_b'], 'L0_ffn_w1': _L0_ffn_in['w1'], 'L0_ffn_b1': _L0_ffn_in['b1'], 'L0_ffn_w2': _L0_ffn_in['w2'], 'L0_ffn_b2': _L0_ffn_in['b2']}

def reference(x, txt, L0_tok_W_lin, L0_tok_b_lin, L0_attn_w_qkv, L0_attn_b_qkv, L0_attn_w_proj, L0_attn_b_proj, L0_ffn_switch_w, L0_ffn_switch_b, L0_ffn_w1, L0_ffn_b1, L0_ffn_w2, L0_ffn_b2):
    import jax
    import jax.numpy as jnp

    def _L0_tok_ref(images, W_lin, b_lin):
        import jax, jax.numpy as jnp
        import numpy as np
        P1, P2 = (16, 16)
        EMBED = 192

        def _patchify(images):
            B, C, H, W = images.shape
            h, w = (H // P1, W // P2)
            x = images.reshape(B, C, h, P1, w, P2)
            x = x.transpose(0, 2, 4, 3, 5, 1)
            return x.reshape(B, h * w, P1 * P2 * C)
        patches = _patchify(images)
        return jnp.einsum('bnd,ed->bne', patches, W_lin) + b_lin

    def _L0_attn_ref(x, w_qkv, b_qkv, w_proj, b_proj):
        import jax, jax.numpy as jnp
        import numpy as np
        NUM_HEADS = 12
        BITS_W = 8
        BITS_A = 8
        BITS_S = 4
        EPS = 1.1920928955078125e-07

        def fq_weight(w):
            qmin, qmax = (-2 ** (BITS_W - 1), 2 ** (BITS_W - 1) - 1)
            mn = jnp.minimum(w.min(axis=1, keepdims=True), 0.0)
            mx = jnp.maximum(w.max(axis=1, keepdims=True), 0.0)
            scale = jnp.maximum((mx - mn) / float(qmax - qmin), EPS)
            zp = qmin - jnp.round(mn / scale)
            wq = jnp.clip(jnp.round(w / scale) + zp, qmin, qmax)
            return (wq - zp) * scale

        def fq_act(x):
            qmin, qmax = (-2 ** (BITS_A - 1), 2 ** (BITS_A - 1) - 1)
            mn = jnp.minimum(x.min(), 0.0)
            mx = jnp.maximum(x.max(), 0.0)
            scale = jnp.maximum((mx - mn) / float(qmax - qmin), EPS)
            zp = qmin - jnp.round(mn / scale)
            xq = jnp.clip(jnp.round(x / scale) + zp, qmin, qmax)
            return ((xq - zp) * scale, scale)

        def int_log_softmax(x, scale):
            x_int = x / scale
            x_int = x_int - x_int.max(axis=-1, keepdims=True)
            x0, n = (-0.6931, 30)
            x0_int = jnp.floor(x0 / scale)
            x_int = jnp.maximum(x_int, n * x0_int)
            q = jnp.floor(x_int / x0_int)
            r = x_int - x0_int * q
            c0 = 0.35815147
            b_int = jnp.floor(0.96963238 / c0 / scale)
            c_int = jnp.floor(1.0 / c0 / (scale * scale))
            z = r * (r + b_int) + c_int
            exp_int = jnp.clip(jnp.floor(z * jnp.exp2(n - q)), 0.0, None)
            exp_sum = exp_int.sum(axis=-1, keepdims=True)
            sm = jnp.round(exp_sum / exp_int)
            big = jnp.floor(jnp.log2(sm))
            big = jnp.where(sm - jnp.exp2(big) >= jnp.exp2(big - 1.0), big + 1.0, big)
            mask = big >= float(2 ** BITS_S)
            qlog = jnp.clip(big, 0.0, float(2 ** BITS_S - 1))
            return jnp.where(mask, 0.0, jnp.exp2(-qlog))
        B, N, C = x.shape
        H = NUM_HEADS
        hd = C // H
        attn_scale = hd ** (-0.5)
        y = x @ fq_weight(w_qkv).T + b_qkv
        y, _ = fq_act(y)
        qkv = y.reshape(B, N, 3, H, hd).transpose(2, 0, 3, 1, 4)
        q, k, v = (qkv[0], qkv[1], qkv[2])
        attn = jnp.einsum('bhnd,bhmd->bhnm', q, k) * attn_scale
        attn, s_attn = fq_act(attn)
        attn = int_log_softmax(attn, s_attn)
        o = jnp.einsum('bhnm,bhmd->bhnd', attn, v)
        o = o.transpose(0, 2, 1, 3).reshape(B, N, C)
        o, _ = fq_act(o)
        o = o @ fq_weight(w_proj).T + b_proj
        o, _ = fq_act(o)
        return o

    def _L0_ffn_ref(x, switch_w, switch_b, w1, b1, w2, b2):
        import jax, jax.numpy as jnp
        import numpy as np
        CAPACITY_FACTOR = 1.25
        B, S, D = x.shape
        E = w1.shape[0]
        xf = x.reshape(-1, D)
        N = xf.shape[0]
        capacity = int(CAPACITY_FACTOR * N / E)
        probs = jax.nn.softmax(xf @ switch_w + switch_b, axis=-1)
        prob_max = jnp.max(probs, axis=-1)
        routes = jnp.argmax(probs, axis=-1)
        sort_idx = jnp.lexsort((-prob_max, routes))
        counts = jnp.bincount(routes, length=E)
        starts = jnp.concatenate([jnp.zeros((1,), counts.dtype), jnp.cumsum(counts)[:-1]])
        rank_sorted = jnp.arange(N) - starts[routes[sort_idx]]
        rank = jnp.zeros((N,), jnp.int32).at[sort_idx].set(rank_sorted.astype(jnp.int32))
        keep = rank < capacity
        dest_e = jnp.where(keep, routes, E)
        dest_c = jnp.where(keep, rank, 0)
        buf = jnp.zeros((E + 1, capacity, D), xf.dtype).at[dest_e, dest_c].set(xf)
        h = jax.nn.gelu(jnp.einsum('ecd,edf->ecf', buf[:E], w1) + b1[:, None, :], approximate=False)
        o = jnp.einsum('ecf,efd->ecd', h, w2) + b2[:, None, :]
        y_exp = o[routes, dest_c]
        y = jnp.where(keep[:, None], y_exp, xf)
        out = y * prob_max[:, None]
        return out.reshape(B, S, D)
    h = _L0_tok_ref(x, L0_tok_W_lin, L0_tok_b_lin)
    h = jnp.concatenate([h, txt], axis=1)
    h = h + _L0_attn_ref(_layernorm(h, axis=-1), L0_attn_w_qkv, L0_attn_b_qkv, L0_attn_w_proj, L0_attn_b_proj)
    h = h + _L0_ffn_ref(_layernorm(h, axis=-1), L0_ffn_switch_w, L0_ffn_switch_b, L0_ffn_w1, L0_ffn_b1, L0_ffn_w2, L0_ffn_b2)
    return h

_drawn_inputs = setup_inputs


def setup_inputs(seed=0):
    import zlib

    import numpy as np

    out = dict(_drawn_inputs(seed))
    spreads = {'L0_ffn_switch_b': (0.0, 0.1), 'L0_ffn_b1': (0.0, 0.8), 'L0_ffn_b2': (0.0, 0.1)}
    factors = {'L0_tok_b_lin': 2.722, 'L0_attn_w_qkv': 3.17, 'L0_attn_b_qkv': 3.427}
    for name, (base, spread) in spreads.items():
        noise = np.random.default_rng([zlib.crc32(name.encode()), seed]).standard_normal(out[name].shape)
        drawn = base * np.exp(spread * noise) if base else spread * noise
        out[name] = jnp.asarray(drawn.astype(out[name].dtype))
    for name, factor in factors.items():
        out[name] = (out[name] * factor).astype(out[name].dtype)
    return out
```

```python
import concourse.bass as bass
from concourse import mybir
from contextlib import ExitStack

B, CH, IMG, PATCH = 8, 3, 96, 16
D = 192
NIMG = (IMG // PATCH) ** 2
NTXT = 128
N = NIMG + NTXT
TOK = B * N
P = 128
T = -(-TOK // P)
LAST = TOK - (T - 1) * P
PD = CH * PATCH * PATCH
KC = PD // P
H, HD = 12, 16
HG, HQ = 3, 4
DC = D // 2
QKV = 3 * D
EXP, F = 8, 768
CAP = int(1.25 * TOK / EXP)
SLOTS = CAP + CAP % 2
HALF = SLOTS // 2
FC = F // P
KR = N - P
EB = 3
ET = -(-B // EB)
EPS = 1.1920928955078125e-07
LNEPS = 1e-5
MAGIC = 1.5 * 2.0 ** 23
PSCALE = 2.0 ** 111
RSCALE = (4.0 / 3.0) * (1.0 - 2.0 ** -9 * (1.0 - 2.0 ** -9)) * 2.0 ** 112


def rows(t):
    return P if t < T - 1 else LAST


def first_batch(t):
    return P * t // N


def batches(t):
    return (P * t + rows(t) - 1) // N - first_batch(t) + 1


def pieces(b, lo, hi):
    out, n = [], lo
    while n < hi:
        at = N * b + n
        k = min(hi - n, P - at % P)
        out.append((at // P, at % P, n, k))
        n += k
    return out


C_ID, C_PAR, C_SEL, C_LOW, C_BSEL, C_EXP = 0, P, P + TOK, P + TOK + HG * N, 2 * P + TOK + HG * N, 2 * P + TOK + HG * N + 2 * T
C_END = C_EXP + T * EXP


def fusion_kernel(nc, x, wlin, blin, txt, wqkv, bqkv, bproj, sww, swb, w1, b1, w2, b2, consts, out):
    f32, bf16, i16, u16, u32 = (mybir.dt.float32, mybir.dt.bfloat16, mybir.dt.int16, mybir.dt.uint16,
                                mybir.dt.uint32)
    ALU = mybir.AluOpType
    ACT = mybir.ActivationFunctionType
    AX = mybir.AxisListType

    ctx = ExitStack()
    with ctx:
        def sb(name, shape, dt=f32):
            return ctx.enter_context(nc.sbuf_tensor(name, shape, dt))[:]

        def sem(name):
            return ctx.enter_context(nc.semaphore(name))

        def dram(name, shape, dt):
            return nc.dram_tensor(name, shape, dt, kind="Internal").ap()

        v_dram = dram("v_dram", (TOK, D), bf16)
        slots_in = dram("slots_in", (EXP * SLOTS, D), f32)
        slots_out = dram("slots_out", (EXP * SLOTS, D), f32)

        UW = H * N
        HE = 2
        cst = sb("cst", [P, C_END])
        ident = cst[:, C_ID:C_ID + P]
        parity = cst[:, C_PAR:C_PAR + TOK]
        lower = cst[:, C_LOW:C_LOW + P]
        batch_sel = cst[:, C_BSEL:C_BSEL + 2 * T].rearrange("p (t b) -> p t b", b=2)
        expert_no = cst[:, C_EXP:C_EXP + T * EXP].rearrange("p (t e) -> p t e", e=EXP)
        ident_b = sb("ident_b", [P, P], bf16)
        sel_b = sb("sel_b", [P, HG * N], bf16)
        h = sb("h", [P, T, D])
        xT = sb("xT", [DC, 2, TOK])
        wprojT = sb("wprojT", [DC, 2, D], bf16)
        proj_scale = sb("proj_scale", [P, D])
        bproj_b = sb("bproj_b", [P, D])
        swb_b = sb("swb_b", [P, EXP])
        sww_s = sb("sww_s", [DC, 2, EXP])
        probsT = sb("probsT", [P, 16, P], bf16)
        b1_s = sb("b1_s", [P, EXP, FC])
        b2_s = sb("b2_s", [EXP, D])
        stat = sb("stat", [P, T, 6])
        mv = sb("mv", [P, T, 2])
        var = sb("var", [P, T])
        std = sb("std", [P, T])
        rstd = sb("rstd", [P, T])
        ymax = sb("ymax", [P, T])
        ymin = sb("ymin", [P, T])
        rmax = sb("rmax", [P, T * H])
        gcol = sb("gcol", [P, 2])
        gred = sb("gred", [P, 2])
        sc = sb("sc", [P, 64])
        S = sb("S", [P, 2, H])
        lg = sb("lg", [P, 6, T, EXP])
        onehot = sb("onehot", [P, T, EXP], bf16)
        rt = sb("rt", [P, 8, T])
        slot = sb("slot", [P, T], u32)
        w1_a = sb("w1_a", [DC, HE, 2, F])
        w2_a = sb("w2_a", [P, HE, FC, D])

        def cutter(name, words):
            whole, at = sb(name, [P, words]), [0]

            def cut(n, dt=f32):
                if n is None:
                    at[0] = 0
                    return None
                assert at[0] + n <= words, (name, at, n)
                v = whole[:, at[0]:at[0] + n]
                at[0] += n
                return v if dt == f32 else v.bitcast(dt)
            return cut

        cut = cutter("attn", 3 * HG * TOK // 2 + 2 * B * D // 2 + T * P // 2)
        qT = cut(HG * TOK // 2, bf16).rearrange("p (g n) -> p g n", g=HG)
        kT = cut(HG * TOK // 2, bf16).rearrange("p (g n) -> p g n", g=HG)
        kpair = cut(HG * (B - 1) * N // 2, bf16).rearrange("p (g n) -> p g n", g=HG)
        vmain = cut(B * D // 2, bf16).rearrange("p (b u d) -> p b u d", b=B, u=H)
        vrest = cut(B * D // 2, bf16).rearrange("p (b j c) -> p b j c", b=B, j=HQ)
        nbT = cut(T * P // 2, bf16)
        cut(None)
        G = cut(T * TOK // 2, bf16).rearrange("p (t n) -> p t n", n=TOK)
        cut(None)
        xeT = cut(2 * 2 * SLOTS).rearrange("p (k c n) -> p k c n", k=2, c=2)
        hT = cut(2 * FC * SLOTS).rearrange("p (k f n) -> p k f n", k=2, f=FC)
        oe = cut(2 * 2 * D).rearrange("p (k a d) -> p k a d", k=2, a=2)

        NB2 = EXP - HE
        cut = cutter("region", 18432)
        xn = cut(T * D).rearrange("p (t d) -> p t d", d=D)
        y = cut(T * QKV).rearrange("p (t c) -> p t c", c=QKV)
        yint = cut(T * QKV // 2, i16).rearrange("p (t c) -> p t c", c=QKV)
        emb_w = cut(KC * D).rearrange("p (c e) -> p c e", e=D)
        blin_b = cut(D)
        emb = cut(ET * D).rearrange("p (t e) -> p t e", e=D)
        wall = cut(8 * D).rearrange("p (g i) -> p g i", g=8)[0:DC]
        wdeq = cut(8 * D).rearrange("p (g i) -> p g i", g=8)[0:DC]
        bqkv_b = cut(QKV)
        wqkvT = cut(2 * QKV).rearrange("p (c o) -> p c o", c=2)[0:DC]
        qk2 = y.rearrange("p t c -> p (t c)")[:, 0:T * 2 * D].bitcast(bf16).rearrange("p (t k c) -> p t k c", t=T, k=2 * HG)
        cut(None)
        bufs = {}
        for k in range(2):
            for n, words, dt in (("m", UW // 2, i16), ("q", UW // 2, i16), ("r", UW // 2, i16), ("pw", UW // 2, i16),
                                 ("x", UW // 2, u16), ("w", UW, f32), ("e", UW, f32)):
                bufs[n, k] = cut(words, dt)
        cut(None)
        w1_b = cut(NB2 * 2 * F).rearrange("p (e c f) -> p e c f", e=NB2, c=2)
        w2_b = cut(NB2 * FC * D).rearrange("p (e c d) -> p e c d", e=NB2, c=FC)
        cut = cutter("share", EXP * 2 * D)
        patches = cut(KC * B * NIMG).rearrange("p (c n) -> p c n", c=KC)
        cut(None)
        oT = cut(TOK, bf16).rearrange("p (c n) -> p c n", c=2)[0:DC]
        cut(None)
        prow = cut(TOK)
        cnt = cut(TOK)[0:EXP]
        cut(None)
        xe = cut(EXP * 2 * D).rearrange("p (e a d) -> p e a d", e=EXP, a=2)
        cut = cutter("obuf", T * D)
        obuf_w = cut(T * D)
        obuf = obuf_w.rearrange("p (t d) -> p t d", d=D)
        cut(None)
        nm = cut(T * H)
        nb = cut(T * H)
        nb2 = cut(T * H)
        nb3 = cut(T * H)
        parts = [cut(T * H // 2, bf16) for _ in range(3)]
        nb_parts = cut(T * P // 2, bf16).rearrange("p (t c) -> p t c", c=P)
        cut = cutter("xf", T * D)
        xf = cut(T * D).rearrange("p (t d) -> p t d", d=D)
        cut(None)
        oint = cut(T * D // 2, i16).rearrange("p (t d) -> p t d", d=D)
        obf = cut(T * D // 2, bf16).rearrange("p (t d) -> p t d", d=D)
        tie = sb("tie", [P, P], bf16)
        wst = sb("wst", [DC, 8, 8])
        wproj_n = sb("wproj_n", [DC, 2, D], bf16)
        ps = ctx.enter_context(nc.psum_tensor("ps", [P, 8 * 512], f32))

        def bank(k, n=1):
            return ps[:, 512 * k:512 * (k + n)]

        def bankb(k, n=1):
            return ps[:, 512 * k:512 * (k + n)].bitcast(bf16)

        def w1_of(e):
            return w1_a[:, e] if e < HE else w1_b[0:DC, e - HE]

        def w2_of(e):
            return w2_a[:, e] if e < HE else w2_b[:, e - HE]

        names = ("cst_in emb_in w_in bias_in txt_in h_in ffn_in ffn_in2 zeroed v_out v_in v_zero xe_in oe_out0 oe_out1 scat gath stored "
                 "pool_zero emb_mm emb_sb var_ok std_ok xn_ok xnT_mm xT_ok wdeq_ok wproj_ok wT_mm wT_ok qkv_mm y_ok g_col g_T qkv_int "
                 "qT_mm kT_mm q_ok k_ok pair_ok s0_mm s0_read nb_ok nbT_mm nbT_ok s_mm m_ok r_ok w_ok e_ok inv_ok p_ok "
                 "pT_mm pT_ok o_mm o_ok obf_ok oT_mm oT_ok pr_mm y2_ok xf_ok lg_mm lg_ok ex_ok p_col prow_mm prow_ok "
                 "cmp_ok cnt_mm cnt_ok cntT_mm slot_ok xeT_mm xeT_ok h_mm h_ok oe_mm oe_ok out_ok dve_order act_order cst_b").split()
        s = {n: sem(n) for n in names}

        block = ctx.enter_context(nc.Block())
        text = [(b, pc) for b in range(B) for pc in pieces(b, NIMG, N)]
        image = [(b, pc) for b in range(B) for pc in pieces(b, 0, NIMG)]

        @block.sync
        def _(sp):
            def load(dst, src, what):
                sp.dma_start(dst, src).then_inc(s[what], 16)

            load(patches, x, "emb_in")
            load(emb_w, wlin, "emb_in")
            load(blin_b, blin.partition_broadcast(P), "emb_in")
            load(cst[:, :], consts, "cst_in")
            load(bqkv_b, bqkv.partition_broadcast(P), "bias_in")
            load(bproj_b[:, :], bproj.partition_broadcast(P), "bias_in")
            load(swb_b[:, :], swb.partition_broadcast(P), "bias_in")
            load(sww_s[:, :, :], sww, "bias_in")
            sp.wait_ge(s["pool_zero"], 2)
            for b, (t, r, n, k) in text:
                load(h[r:r + k, t, :], txt[b, n - NIMG:n - NIMG + k, :], "txt_in")
            for a in range(2):
                load(slots_in.rearrange("(a p) d -> p a d", p=HALF)[:, 8 * a:8 * a + 8, :], obuf[0:HALF, 0:8, :], "zeroed")
            load(w1_a[:, :, :, :], w1[:, 0:HE], "ffn_in")
            load(w2_a[:, :, :, :], w2[:, 0:HE], "ffn_in")
            load(b1_s[:, :, :], b1, "ffn_in")
            load(b2_s[:, :], b2, "ffn_in")
            sp.wait_ge(s["qkv_int"], 3)
            vint = yint.bitcast(bf16)
            load(v_dram[0:(T - 1) * P, :].rearrange("(t p) c -> p t c", p=P), vint[:, 0:T - 1, 2 * D:], "v_out")
            load(v_dram[(T - 1) * P:, :], vint[0:LAST, T - 1, 2 * D:], "v_out")
            sp.wait_ge(s["v_out"], 32)
            vb = v_dram.rearrange("(b n) c -> n b c", n=N)
            load(vmain.rearrange("p b u d -> p b (u d)"), vb[0:P], "v_in")
            sp.wait_ge(s["v_zero"], 1)
            for b in range(B):
                for g in range(HG):
                    load(vrest[KR * g:KR * (g + 1), b, :, HD * g:HD * (g + 1)],
                         vb[P:N, b, :].rearrange("n (j g d) -> n j g d", j=HQ, g=HG)[:, :, g, :], "v_in")
            sp.wait_ge(s["p_ok"], T)
            sp.wait_ge(s["inv_ok"], T)
            sp.wait_ge(s["pT_mm"], T)
            load(w1_b[0:DC], w1[:, HE:], "ffn_in2")
            load(w2_b, w2[:, HE:], "ffn_in2")
            sp.wait_ge(s["scat"], 16 * T)
            for e in range(EXP):
                load(xe[0:HALF, e], slots_in[e * SLOTS:(e + 1) * SLOTS, :].rearrange("(a p) d -> p a d", a=2), "xe_in")
            for e in range(EXP):
                sp.wait_ge(s["oe_ok"], e + 1)
                load(slots_out[e * SLOTS:(e + 1) * SLOTS, :].rearrange("(a p) d -> p a d", a=2), oe[0:HALF, e % 2],
                     ("oe_out0", "oe_out1")[e % 2])
            for t in range(T):
                sp.wait_ge(s["out_ok"], t + 1)
                load(out[P * t:P * t + rows(t), :], h[0:rows(t), t, :], "stored")
            sp.wait_ge(s["stored"], 16 * T)

        @block.gpsimd
        def _(pool):
            pool.memset(obuf_w, 0.0).then_inc(s["pool_zero"], 1)
            pool.memset(h[:, T - 1, :], 0.0).then_inc(s["pool_zero"], 1)
            pool.memset(y[:, T - 1, :], 0.0).then_inc(s["pool_zero"], 1)
            pool.memset(lg[:, :, :, :], 0.0).then_inc(s["pool_zero"], 1)
            pool.memset(onehot[:, :, :], 0.0).then_inc(s["pool_zero"], 1)
            pool.memset(rmax[:, :], 0.0).then_inc(s["pool_zero"], 1)
            pool.memset(vrest, 0.0).then_inc(s["v_zero"], 1)
            pool.wait_ge(s["zeroed"], 32)
            pool.wait_ge(s["slot_ok"], 1)
            pool.wait_ge(s["xf_ok"], T)
            for t in range(T):
                pool.indirect_dma_start(out=slots_in, out_offset=bass.IndirectOffsetOnAxis(ap=slot[0:rows(t), t:t + 1], axis=0),
                                        in_=xf[0:rows(t), t, :], in_offset=None, bounds_check=EXP * SLOTS - 1,
                                        oob_is_err=False).then_inc(s["scat"], 16)
            pool.wait_ge(s["oe_out0"], 16 * (EXP // 2))
            pool.wait_ge(s["oe_out1"], 16 * (EXP // 2))
            pool.wait_ge(s["scat"], 16 * T)
            for t in range(T):
                pool.indirect_dma_start(out=xf[0:rows(t), t, :], out_offset=None, in_=slots_out,
                                        in_offset=bass.IndirectOffsetOnAxis(ap=slot[0:rows(t), t:t + 1], axis=0),
                                        bounds_check=EXP * SLOTS - 1, oob_is_err=False).then_inc(s["gath"], 16)

        def scores_of(t):
            b, R = first_batch(t), rows(t)
            for j in range(HQ):
                for g in range(HG):
                    rws = slice(32 * j, 32 * j + 32)
                    keys = (kpair if batches(t) == 2 else kT)[rws, g, N * b:N * (b + 1)]
                    qs = qT[rws, g, P * t:P * t + R]
                    if t < T - 1:
                        yield j, g, slice(0, P), slice(N * g, N * (g + 1)), qs, keys
                    else:
                        yield 0, g, rws, slice(N * g, N * (g + 1)), qs, keys

        def scores_view(t, k):
            if t < T - 1:
                return bank(k, 4).rearrange("p (a c) -> p a c", a=4)[:, :, 0:HG * N]
            return bank(k)[:, 0:HG * N]

        def units(t):
            return H if t < T - 1 else HG

        @block.tensor
        def _(pe):
            mm = nc.tensor.matmul
            tr = nc.tensor.transpose
            pe.wait_ge(s["emb_in"], 48)
            for j in range(ET):
                n = min(EB, B - EB * j) * NIMG
                for c in range(KC):
                    last = mm(bank(j)[0:n, 0:D], patches[:, c, EB * NIMG * j:EB * NIMG * j + n], emb_w[:, c, :],
                              start=(c == 0), stop=(c == KC - 1))
                last.then_inc(s["emb_mm"], 1)
            pe.wait_ge(s["wdeq_ok"], 1)
            pe.wait_ge(s["cst_in"], 16)
            for c in range(2):
                for o in range(6):
                    last = tr(bank(3 + 2 * c + o // 3)[0:DC, DC * (o % 3):DC * (o % 3 + 1)],
                              wdeq[:, o, DC * c:DC * (c + 1)], ident[0:DC, 0:DC])
            last.then_inc(s["wT_mm"], 1)
            pe.wait_ge(s["wproj_ok"], 1)
            pe.wait_ge(s["cst_b"], 2)
            for c in range(2):
                for o in range(2):
                    tr(bankb(7)[0:DC, D * c + DC * o:D * c + DC * (o + 1)], wproj_n[:, o, DC * c:DC * (c + 1)],
                       ident_b[0:DC, 0:DC])
            for o in range(2):
                last = tr(bank(7)[:, 256 + DC * o:256 + DC * (o + 1)], wst[:, 6 + o, 2:3].to_broadcast([DC, P]),
                          ident[0:DC, 0:DC])
            last.then_inc(s["wT_mm"], 1)
            pe.wait_ge(s["wT_ok"], 3)
            def turn(t, src, ready):
                R = rows(t)
                pe.wait_ge(s[ready[0]], ready[1])
                for c in range(2):
                    last = tr(bank(t % 2)[0:DC, P * c:P * c + R], src[0:R, t, DC * c:DC * (c + 1)], ident[0:R, 0:R])
                last.then_inc(s["xnT_mm"], 1)

            def qkv(t):
                R = rows(t)
                pe.wait_ge(s["xT_ok"], t + 1)
                if t >= 3:
                    pe.wait_ge(s["y_ok"], t - 2)
                for a in range(2):
                    for c in range(2):
                        last = mm(bank(2 + 2 * (t % 3) + a)[0:R, 0:QKV // 2], xT[:, c, P * t:P * t + R],
                                  wqkvT[:, c, QKV // 2 * a:QKV // 2 * (a + 1)], start=(c == 0), stop=(c == 1))
                last.then_inc(s["qkv_mm"], 1)

            for t in range(T + 1):
                if t < T:
                    if t >= 2:
                        pe.wait_ge(s["xT_ok"], t - 1)
                    turn(t, xn, ("xn_ok", t + 1))
                if t >= 1:
                    qkv(t - 1)

            def global_stat(n):
                pe.wait_ge(s["g_col"], n)
                for a in range(2):
                    last = tr(bank(7)[:, P * a:P * (a + 1)], gcol[:, a:a + 1].to_broadcast([P, P]), ident)
                last.then_inc(s["g_T"], 1)

            global_stat(1)
            pe.wait_ge(s["qkv_int"], 3)
            for t in range(T):
                R = rows(t)
                for k, name, ok in ((0, "qT_mm", "q_ok"), (1, "kT_mm", "k_ok")):
                    if t >= 2:
                        pe.wait_ge(s[ok], t - 1)
                    for g in range(HG):
                        last = tr(bankb(2 * k + t % 2)[:, P * g:P * g + R], qk2[0:R, t, HG * k + g, :], ident_b[0:R, 0:R])
                    last.then_inc(s[name], 1)
            pe.wait_ge(s["pair_ok"], 1)
            for t in range(T):
                if t >= 2:
                    pe.wait_ge(s["s0_read"], t - 1)
                for j, g, prt, col, qs, keys in scores_of(t):
                    last = mm(bank(4 * (t % 2) + j)[prt, col], qs, keys, start=True, stop=True)
                last.then_inc(s["s0_mm"], 1)
            global_stat(2)
            pe.wait_ge(s["nb_ok"], 1)
            for t in range(T):
                last = tr(bankb(4, 2)[:, P * t:P * (t + 1)], nb_parts[:, t, :], ident_b)
            last.then_inc(s["nbT_mm"], 1)
            pe.wait_ge(s["nbT_ok"], 1)

            def scores(t):
                if t >= 1:
                    pe.wait_ge(s["m_ok"], t)
                if t < T - 1:
                    for j in range(HQ):
                        mm(bank(j)[:, 0:HG * N], nbT[32 * j:32 * j + 3 * HG, P * t:P * (t + 1)],
                           sel_b[32 * j:32 * j + 3 * HG, :], start=True, stop=True)
                        for jj, g, prt, col, qs, keys in scores_of(t):
                            if jj == j:
                                last = mm(bank(j)[prt, col], qs, keys, start=False, stop=True, skip_group_check=True)
                else:
                    mm(bank(0)[:, 0:HG * N], nbT[0:3 * HG, P * t:P * (t + 1)], sel_b[0:3 * HG, :], start=True, stop=True)
                    for _, g, prt, col, qs, keys in scores_of(t):
                        last = mm(bank(0)[prt, col], qs, keys, start=False, stop=True, skip_group_check=True)
                last.then_inc(s["s_mm"], 1)

            def turn_probs(t):
                pe.wait_ge(s["p_ok"], t + 1)
                if t >= 1:
                    pe.wait_ge(s["pT_ok"], t)
                pr, n0 = bufs["q", t % 2].bitcast(bf16), P * units(t)
                for u in range(units(t)):
                    tr(bankb(4, 2)[:, P * u:P * (u + 1)], pr[:, P * u:P * (u + 1)], ident_b)
                for j in range(units(t) // HG):
                    last = tr(bankb(4, 2)[0:HG * KR, P * (H + j):P * (H + j + 1)], pr[:, n0 + HG * KR * j:n0 + HG * KR * (j + 1)],
                              ident_b)
                last.then_inc(s["pT_mm"], 1)

            def attend(t):
                b, nb_, R = first_batch(t), batches(t), rows(t)
                pe.wait_ge(s["pT_ok"], t + 1)
                if t == 0:
                    pe.wait_ge(s["v_in"], 16 * (1 + HG * B))
                if t >= 2:
                    pe.wait_ge(s["o_ok"], t - 1)
                o = bank(6 + t % 2)[0:R, 0:nb_ * D].rearrange("p (b c) -> p b c", b=nb_)
                for j in range(HQ):
                    if t < T - 1:
                        rest, main = probsT[0:HG * KR, H + j, :], [probsT[:, HG * j + g, :] for g in range(HG)]
                    else:
                        qs = slice(LAST * j, LAST * (j + 1))
                        rest, main = probsT[0:HG * KR, H, qs], [probsT[:, g, qs] for g in range(HG)]
                    mm(o[:, :, HG * HD * j:HG * HD * (j + 1)], rest, vrest[0:HG * KR, b:b + nb_, j, :],
                       start=True, stop=True)
                    for g in range(HG):
                        u = HG * j + g
                        last = mm(o[:, :, HD * u:HD * (u + 1)], main[g], vmain[:, b:b + nb_, u, :],
                                  start=False, stop=True, skip_group_check=True)
                last.then_inc(s["o_mm"], 1)

            scores(0)
            for i in range(T + 2):
                if i + 1 < T:
                    scores(i + 1)
                if i >= 2:
                    turn_probs(i - 2)
                    attend(i - 2)
            global_stat(3)
            pe.wait_ge(s["obf_ok"], 1)
            for t in range(T + 1):
                if t < T:
                    R = rows(t)
                    if t >= 2:
                        pe.wait_ge(s["oT_ok"], t - 1)
                    for c in range(2):
                        last = tr(bankb(t % 2)[0:DC, P * c:P * c + R], obf[0:R, t, DC * c:DC * (c + 1)], ident_b[0:R, 0:R])
                    last.then_inc(s["oT_mm"], 1)
                if t >= 1:
                    u, R = t - 1, rows(t - 1)
                    pe.wait_ge(s["oT_ok"], u + 1)
                    if u >= 4:
                        pe.wait_ge(s["y2_ok"], u - 3)
                    for c in range(2):
                        last = mm(bank(2 + u % 4)[0:R, 0:D], oT[:, c, P * u:P * u + R], wprojT[:, c, :],
                                  start=(c == 0), stop=(c == 1))
                    last.then_inc(s["pr_mm"], 1)
            global_stat(4)
            for t in range(T + 1):
                if t < T:
                    pe.wait_ge(s["xT_ok"], T + max(t - 1, 0))
                    turn(t, xf, ("xf_ok", t + 1))
                if t >= 1:
                    u, R = t - 1, rows(t - 1)
                    pe.wait_ge(s["xT_ok"], T + u + 1)
                    for c in range(2):
                        last = mm(bank(2)[0:R, EXP * u:EXP * (u + 1)], xT[:, c, P * u:P * u + R], sww_s[:, c, :],
                                  start=(c == 0), stop=(c == 1))
            last.then_inc(s["lg_mm"], 1)
            pe.wait_ge(s["p_col"], 1)
            for t in range(T):
                R = rows(t)
                last = tr(bank(3, 3)[:, P * t:P * t + R], rt[0:R, 2, t:t + 1].to_broadcast([R, P]), ident[0:R, 0:R])
            last.then_inc(s["prow_mm"], 1)
            for t in range(T):
                R = rows(t)
                pe.wait_ge(s["cmp_ok"], t + 1)
                for c in range(3):
                    w = min(512, TOK - 512 * c)
                    last = mm(bank(c)[0:EXP, 0:w], onehot[0:R, t, :], G[0:R, t, 512 * c:512 * c + w],
                              start=(t == 0), stop=(t == T - 1))
            last.then_inc(s["cnt_mm"], 1)
            pe.wait_ge(s["cnt_ok"], 1)
            for t in range(T):
                R = rows(t)
                last = tr(bank(6)[0:R, EXP * t:EXP * (t + 1)], cnt[:, P * t:P * t + R], ident[0:EXP, 0:EXP])
            last.then_inc(s["cntT_mm"], 1)

            def expert_in(e):
                pe.wait_ge(s["xe_in"], 16 * EXP)
                if e >= 1:
                    pe.wait_ge(s["xeT_ok"], e)
                for c in range(2):
                    for a in range(2):
                        last = tr(bank(0)[0:DC, SLOTS * c + HALF * a:SLOTS * c + HALF * (a + 1)],
                                  xe[0:HALF, e, a, DC * c:DC * (c + 1)], ident[0:HALF, 0:HALF])
                last.then_inc(s["xeT_mm"], 1)
                pe.wait_ge(s["xeT_ok"], e + 1)
                if e == 0:
                    pe.wait_ge(s["ffn_in"], 64)
                if e == HE:
                    pe.wait_ge(s["ffn_in2"], 32)
                for f in range(FC):
                    if e >= 2 and f % 2 == 0:
                        pe.wait_ge(s["h_ok"], 3 * (e - 2) + f // 2 + 1)
                    for c in range(2):
                        last = mm(bank(2 + 3 * (e % 2) + f // 2)[:, SLOTS * (f % 2):SLOTS * (f % 2 + 1)],
                                  w1_of(e)[:, c, P * f:P * (f + 1)], xeT[0:DC, e % 2, c, :], start=(c == 0), stop=(c == 1))
                    if f % 2:
                        last.then_inc(s["h_mm"], 1)

            def expert_out(e):
                pe.wait_ge(s["h_ok"], 3 * (e + 1))
                if e >= 1:
                    pe.wait_ge(s["oe_ok"], e)
                for a in range(2):
                    o = bank(1)[0:HALF, D * a:D * (a + 1)]
                    mm(o, ident[0:EXP, e:e + 1].to_broadcast([EXP, HALF]), b2_s[:, :], start=True, stop=False)
                    for f in range(FC):
                        last = mm(o, hT[:, e % 2, f, HALF * a:HALF * (a + 1)], w2_of(e)[:, f, :],
                                  start=False, stop=(f == FC - 1))
                last.then_inc(s["oe_mm"], 1)

            expert_in(0)
            for e in range(EXP):
                if e + 1 < EXP:
                    expert_in(e + 1)
                expert_out(e)

        @block.scalar
        def _(act):
            A = nc.scalar.activation
            act.dma_start(wall, wqkv).then_inc(s["w_in"], 16)
            for j in range(ET):
                act.wait_ge(s["emb_sb"], j + 1)
                for b, (t, r, n, k) in image:
                    if b // EB == j:
                        at = NIMG * (b % EB) + n
                        act.dma_start(h[r:r + k, t, :], emb[at:at + k, j, :]).then_inc(s["h_in"], 16)
            act.wait_ge(s["wT_mm"], 1)
            for c in range(2):
                A(wqkvT[:, c, :].rearrange("p (a o) -> p a o", a=2),
                  bank(3 + 2 * c, 2).rearrange("p (a o) -> p a o", a=2)[0:DC, :, 0:QKV // 2], ACT.Copy).then_inc(s["wT_ok"], 1)
            act.wait_ge(s["wT_mm"], 2)
            A(wprojT[:, :, :].rearrange("p c o -> p (c o)"), bankb(7)[0:DC, 0:2 * D], ACT.Copy).then_inc(s["wT_ok"], 1)
            A(proj_scale[:, :], bank(7)[:, 256:256 + D], ACT.Copy).then_inc(s["wT_ok"], 1)
            act.wait_ge(s["var_ok"], 1)
            A(std[:, :], var[:, :], ACT.Sqrt).then_inc(s["std_ok"], 1)

            def keep_turned(t, n):
                R = rows(t)
                act.wait_ge(s["xnT_mm"], n + 1)
                A(xT[:, :, P * t:P * t + R], bank(t % 2)[0:DC, 0:2 * P].rearrange("p (c n) -> p c n", c=2)[:, :, 0:R],
                  ACT.Copy).then_inc(s["xT_ok"], 1)

            for t in range(T):
                keep_turned(t, t)
            act.wait_ge(s["cst_in"], 16)
            for t in range(T):
                act.wait_ge(s["kT_mm"], t + 1)
                lo = P * t
                for b in range(first_batch(t), first_batch(t) + batches(t)):
                    hi = min(N * (b + 1), P * t + rows(t))
                    last = A(kT[:, :, lo:hi],
                             bankb(2 + t % 2)[:, 0:HG * P].rearrange("p (g n) -> p g n", g=HG)[:, :, lo - P * t:hi - P * t],
                             ACT.Copy, scale=parity[:, N * b:N * b + 1])
                    lo = hi
                last.then_inc(s["k_ok"], 1)
            act.wait_ge(s["nbT_mm"], 1)
            A(nbT, bankb(4, 2)[:, 0:T * P], ACT.Copy).then_inc(s["nbT_ok"], 1)

            def distance(t):
                act.wait_ge(s["s_mm"], t + 1)
                if t == 0:
                    act.wait_ge(s["v_out"], 32)
                if t >= 2:
                    act.wait_ge(s["r_ok"], t - 1)
                m = bufs["m", t % 2][:, 0:units(t) * N]
                if t < T - 1:
                    m = m.rearrange("p (a c) -> p a c", a=4)
                A(m, scores_view(t, 0), ACT.Copy, scale=sc[:, 20:21]).then_inc(s["m_ok"], 1)

            def square(t):
                act.wait_ge(s["r_ok"], t + 1)
                if t >= 2:
                    act.wait_ge(s["e_ok"], t - 1)
                n = units(t) * N
                A(bufs["w", t % 2][:, 0:n], bufs["r", t % 2][:, 0:n], ACT.Square, bias=sc[:, 27:28]).then_inc(s["w_ok"], 1)

            def invert(t):
                act.wait_ge(s["e_ok"], t + 1)
                e = bufs["e", t % 2][:, 0:units(t) * N]
                A(e, e, ACT.Ln).then_inc(s["act_order"], 1)
                act.wait_ge(s["act_order"], t + 1)
                A(e, e, ACT.Exp, scale=-1.0).then_inc(s["inv_ok"], 1)

            def keep_probs(t):
                act.wait_ge(s["pT_mm"], t + 1)
                if t >= 1:
                    act.wait_ge(s["o_mm"], t)
                n, k = units(t), units(t) // HG
                A(probsT[:, 0:n, :].rearrange("p u n -> p (u n)"), bankb(4, 2)[:, 0:P * n], ACT.Copy)
                A(probsT[0:HG * KR, H:H + k, :].rearrange("p u n -> p (u n)"),
                  bankb(4, 2)[0:HG * KR, P * H:P * (H + k)], ACT.Copy).then_inc(s["pT_ok"], 1)

            distance(0)
            for i in range(T + 2):
                if i + 1 < T:
                    distance(i + 1)
                if i < T:
                    square(i)
                if 1 <= i <= T:
                    invert(i - 1)
                if i >= 2:
                    keep_probs(i - 2)
            for t in range(T):
                R = rows(t)
                act.wait_ge(s["oT_mm"], t + 1)
                A(oT[:, :, P * t:P * t + R], bankb(t % 2)[0:DC, 0:2 * P].rearrange("p (c n) -> p c n", c=2)[:, :, 0:R],
                  ACT.Copy).then_inc(s["oT_ok"], 1)
            act.wait_ge(s["var_ok"], 2)
            A(std[:, :], var[:, :], ACT.Sqrt).then_inc(s["std_ok"], 1)
            for t in range(T):
                keep_turned(t, T + t)
            act.wait_ge(s["lg_ok"], 1)
            A(lg[:, 3, :, :], lg[:, 2, :, :], ACT.Exp).then_inc(s["ex_ok"], 1)
            act.wait_ge(s["prow_mm"], 1)
            A(prow, bank(3, 3)[:, 0:TOK], ACT.Copy).then_inc(s["prow_ok"], 1)
            act.wait_ge(s["cnt_mm"], 1)
            A(cnt, bank(0, 3)[0:EXP, 0:TOK], ACT.Copy).then_inc(s["cnt_ok"], 1)
            for e in range(EXP):
                for f in range(FC):
                    if f % 2 == 0:
                        act.wait_ge(s["h_mm"], 3 * e + f // 2 + 1)
                        if e >= 2:
                            act.wait_ge(s["oe_mm"], e - 1)
                    last = A(hT[:, e % 2, f, :], bank(2 + 3 * (e % 2) + f // 2)[:, SLOTS * (f % 2):SLOTS * (f % 2 + 1)],
                             ACT.Gelu, bias=b1_s[:, e, f:f + 1])
                    if f % 2:
                        last.then_inc(s["h_ok"], 1)

        @block.vector
        def _(dve):
            v = nc.vector
            made = {n: 0 for n in names}

            def done(ins, what="dve_order"):
                made[what] += 1
                ins.then_inc(s[what], 1)
                dve.wait_ge(s[what], made[what])

            dve.wait_ge(s["w_in"], 16)
            W = [wst[:, :, k:k + 1].squeeze(2) if False else wst[:, :, k] for k in range(8)]
            done(v.tensor_reduce(W[0], wall, AX.X, ALU.max))
            done(v.tensor_reduce(W[1], wall, AX.X, ALU.min, negate=True))
            done(v.tensor_scalar(wst[:, :, 0:2], wst[:, :, 0:2], 0.0, None, ALU.max))
            done(v.tensor_tensor(W[2], W[0], W[1], ALU.add))
            done(v.tensor_scalar(W[2], W[2], 1.0 / 255.0, EPS, ALU.mult, ALU.max))
            done(v.reciprocal(W[3], W[2]))
            done(v.tensor_tensor(W[4], W[1], W[3], ALU.mult))
            done(v.tensor_scalar(W[4], W[4], -1.0, MAGIC, ALU.mult, ALU.add))
            done(v.tensor_scalar(W[4], W[4], 255.0 - MAGIC, None, ALU.add))
            for o in range(8):
                v.tensor_scalar(wdeq[:, o, :], wall[:, o, :], wst[:, o, 3:4], MAGIC, ALU.mult, ALU.add).then_inc(s["dve_order"], 1)
                made["dve_order"] += 1
            dve.wait_ge(s["dve_order"], made["dve_order"])
            for o in range(6):
                v.tensor_scalar(wdeq[:, o, :], wdeq[:, o, :], MAGIC, wst[:, o, 4:5], ALU.subtract, ALU.min).then_inc(s["dve_order"], 1)
                made["dve_order"] += 1
            for o in range(2):
                last = v.tensor_scalar(wproj_n[:, o, :], wdeq[:, 6 + o, :], MAGIC, wst[:, 6 + o, 4:5], ALU.subtract, ALU.min)
            last.then_inc(s["wproj_ok"], 1)
            dve.wait_ge(s["dve_order"], made["dve_order"])
            for o in range(6):
                last2 = v.tensor_scalar(wdeq[:, o, :], wdeq[:, o, :], wst[:, o, 2:3], None, ALU.mult)
            last2.then_inc(s["wdeq_ok"], 1)
            dve.wait_ge(s["cst_in"], 16)
            v.tensor_copy(ident_b[:, :], ident).then_inc(s["cst_b"], 1)
            v.tensor_copy(sel_b[:, :], cst[:, C_SEL:C_SEL + HG * N]).then_inc(s["cst_b"], 1)
            for j in range(ET):
                n = min(EB, B - EB * j) * NIMG
                dve.wait_ge(s["emb_mm"], j + 1)
                v.tensor_tensor(emb[0:n, j, :], bank(j)[0:n, 0:D], blin_b[0:n], ALU.add).then_inc(s["emb_sb"], 1)

            def layer_norm(dst, ok):
                for t in range(T):
                    v.bn_stats(stat[:, t, :], h[:, t, :]).then_inc(s["dve_order"], 1)
                    made["dve_order"] += 1
                dve.wait_ge(s["dve_order"], made["dve_order"])
                for t in range(T):
                    v.bn_aggr(mv[:, t, :], stat[:, t, :]).then_inc(s["dve_order"], 1)
                    made["dve_order"] += 1
                dve.wait_ge(s["dve_order"], made["dve_order"])
                v.tensor_scalar(var[:, :], mv[:, :, 1], LNEPS, None, ALU.add).then_inc(s["var_ok"], 1)
                made["std_ok"] += 1
                dve.wait_ge(s["std_ok"], made["std_ok"])
                done(v.reciprocal(rstd[:, :], std[:, :]))
                for t in range(T):
                    v.tensor_scalar(dst[:, t, :], h[:, t, :], mv[:, t, 0:1], rstd[:, t:t + 1],
                                    ALU.subtract, ALU.mult).then_inc(s[ok], 1)

            dve.wait_ge(s["txt_in"], 16 * len(text))
            dve.wait_ge(s["h_in"], 16 * len(image))
            layer_norm(xn, "xn_ok")
            dve.wait_ge(s["bias_in"], 64)
            dve.wait_ge(s["pool_zero"], 6)
            for t in range(T):
                R = rows(t)
                dve.wait_ge(s["qkv_mm"], t + 1)
                done(v.tensor_tensor(y[0:R, t, :].rearrange("p (a c) -> p a c", a=2),
                                     bank(2 + 2 * (t % 3), 2).rearrange("p (a c) -> p a c", a=2)[0:R, :, 0:QKV // 2],
                                     bqkv_b[0:R].rearrange("p (a c) -> p a c", a=2), ALU.add), "y_ok")
                v.tensor_reduce(ymax[:, t:t + 1], y[:, t, :], AX.X, ALU.max).then_inc(s["dve_order"], 1)
                v.tensor_reduce(ymin[:, t:t + 1], y[:, t, :], AX.X, ALU.min).then_inc(s["dve_order"], 1)
                made["dve_order"] += 2
            dve.wait_ge(s["dve_order"], made["dve_order"])

            def quantiser(at, kappa, mx, mn, ax):
                done(v.tensor_reduce(gcol[:, 0:1], mx, ax, ALU.max))
                done(v.tensor_reduce(gcol[:, 1:2], mn, ax, ALU.min, negate=True), "g_col")
                made["g_T"] += 1
                dve.wait_ge(s["g_T"], made["g_T"])
                done(v.tensor_reduce(gred[:, :], bank(7)[:, 0:2 * P].rearrange("p (a n) -> p a n", a=2), AX.X, ALU.max))
                done(v.tensor_scalar(gred[:, :], gred[:, :], 0.0, None, ALU.max))
                c = [sc[:, at + k:at + k + 1] for k in range(4)]
                done(v.tensor_tensor(c[0], gred[:, 0:1], gred[:, 1:2], ALU.add))
                if kappa is not None:
                    done(v.tensor_scalar(c[0], c[0], kappa, None, ALU.mult))
                done(v.tensor_scalar(c[0], c[0], 1.0 / 255.0, EPS, ALU.mult, ALU.max))
                done(v.reciprocal(c[3], c[0]))
                if kappa is not None:
                    done(v.tensor_scalar(c[1], c[3], kappa, None, ALU.mult))
                else:
                    done(v.tensor_copy(c[1], c[3]))
                done(v.tensor_tensor(c[2], gred[:, 1:2], c[1], ALU.mult))
                done(v.tensor_scalar(c[2], c[2], -1.0, MAGIC, ALU.mult, ALU.add))
                done(v.tensor_scalar(c[2], c[2], 255.0 - MAGIC, None, ALU.add))

            quantiser(0, None, ymax[:, :], ymin[:, :], AX.X)
            done(v.tensor_scalar(yint, y, sc[:, 1:2], sc[:, 2:3], ALU.mult, ALU.min))
            for a in range(2):
                v.tensor_copy(qk2.rearrange("p t k (j a d) -> p t (k j) a d", j=HQ, a=2)[:, :, :, a, :],
                              yint[:, :, 0:2 * D].rearrange("p t (x d) -> p t x d", d=HD)).then_inc(s["qkv_int"], 1)
            v.tensor_copy(yint.bitcast(bf16)[:, :, 2 * D:], yint[:, :, 2 * D:]).then_inc(s["qkv_int"], 1)
            for t in range(T):
                R = rows(t)
                dve.wait_ge(s["qT_mm"], t + 1)
                v.tensor_tensor(qT[:, :, P * t:P * t + R],
                                bankb(t % 2)[:, 0:HG * P].rearrange("p (g n) -> p g n", g=HG)[:, :, 0:R],
                                parity[:, P * t:P * t + R].unsqueeze(1).to_broadcast([P, HG, R]), ALU.mult).then_inc(s["q_ok"], 1)
            dve.wait_ge(s["q_ok"], T)
            dve.wait_ge(s["k_ok"], T)
            v.tensor_tensor(kpair, kT[:, :, 0:(B - 1) * N], kT[:, :, N:B * N], ALU.add).then_inc(s["pair_ok"], 1)
            for t in range(T):
                dve.wait_ge(s["s0_mm"], t + 1)
                view = scores_view(t, 4 * (t % 2))
                full = view.rearrange("p a (g n) -> p a g n", g=HG) if t < T - 1 else view.rearrange("p (g n) -> p g n", g=HG)
                mx = rmax[:, H * t:H * t + units(t)]
                v.tensor_reduce(mx.rearrange("p (a g) -> p a g", a=4) if t < T - 1 else mx, full, AX.X, ALU.max)
                v.tensor_reduce(ymin[:, t:t + 1], view, AX.XY if t < T - 1 else AX.X, ALU.min).then_inc(s["s0_read"], 1)
            dve.wait_ge(s["s0_read"], T)
            sy = sc[:, 0:1]
            done(v.tensor_scalar(sc[:, 8:9], sy, sy, 0.25, ALU.mult, ALU.mult))
            quantiser(4, sc[:, 8:9], rmax[:, :], ymin[:, :], AX.X)
            rs = sc[:, 7:8]
            C0 = 0.35815147
            done(v.tensor_scalar(sc[:, 12:13], rs, -0.6931, None, ALU.mult))
            done(v.tensor_scalar(sc[:, 13:14], rs, 0.96963238 / C0, None, ALU.mult))
            done(v.tensor_scalar(sc[:, 14:15], rs, rs, 1.0 / C0, ALU.mult, ALU.mult))
            done(v.tensor_scalar(sc[:, 15:18], sc[:, 12:15], MAGIC, -MAGIC, ALU.add, ALU.add))
            done(v.tensor_tensor(sc[:, 30:33], sc[:, 15:18], sc[:, 12:15], ALU.is_gt))
            done(v.tensor_tensor(sc[:, 15:18], sc[:, 15:18], sc[:, 30:33], ALU.subtract))
            done(v.tensor_scalar(sc[:, 20:21], sc[:, 5:6], -1.0, None, ALU.mult))
            done(v.tensor_scalar(sc[:, 21:22], sc[:, 15:16], -1.0, None, ALU.mult))
            done(v.reciprocal(sc[:, 22:23], sc[:, 21:22]))
            done(v.tensor_scalar(sc[:, 23:24], sc[:, 22:23], 0.5, -0.5, ALU.mult, ALU.add))
            done(v.tensor_scalar(sc[:, 24:25], sc[:, 21:22], 30.0, None, ALU.mult))
            done(v.tensor_scalar(sc[:, 27:28], sc[:, 16:17], 0.5, None, ALU.mult))
            done(v.tensor_scalar(sc[:, 28:29], sc[:, 27:28], sc[:, 27:28], -1.0, ALU.mult, ALU.mult))
            done(v.tensor_tensor(sc[:, 28:29], sc[:, 28:29], sc[:, 17:18], ALU.add))
            done(v.reciprocal(sc[:, 29:30], sc[:, 20:21]))
            dve.wait_ge(s["zeroed"], 32)
            done(v.tensor_scalar(nm, rmax[:, :], sc[:, 5:6], MAGIC, ALU.mult, ALU.add))
            done(v.tensor_scalar(nm, nm, MAGIC, sc[:, 6:7], ALU.subtract, ALU.min))
            done(v.tensor_scalar(nb, nm, sc[:, 29:30], None, ALU.mult))
            done(v.tensor_copy(parts[0], nb))
            done(v.tensor_tensor(nb2, nb, parts[0], ALU.subtract))
            done(v.tensor_copy(parts[1], nb2))
            done(v.tensor_tensor(nb3, nb2, parts[1], ALU.subtract))
            done(v.tensor_copy(parts[2], nb3))
            for k in range(3):
                last = v.tensor_copy(nb_parts.rearrange("p t (j c) -> p t j c", j=HQ)[:, :, :, k:k + 7:3],
                                     parts[k].rearrange("p (t j g) -> p t j g", j=HQ, g=HG))
            last.then_inc(s["nb_ok"], 1)

            def split(t):
                k, n = t % 2, units(t) * N
                m, q, r, pw = (bufs[x, k][:, 0:n] for x in ("m", "q", "r", "pw"))
                dve.wait_ge(s["m_ok"], t + 1)
                if t >= 2:
                    dve.wait_ge(s["w_ok"], t - 1)
                if t >= 4:
                    dve.wait_ge(s["pT_mm"], t - 3)
                done(v.tensor_scalar(m, m, 0.0, sc[:, 24:25], ALU.max, ALU.min))
                done(v.tensor_scalar(q, m, sc[:, 22:23], sc[:, 23:24], ALU.mult, ALU.add))
                v.tensor_scalar(pw, q, -128.0, 127.0 * 128.0, ALU.mult, ALU.add)
                done(v.tensor_scalar(r, q, sc[:, 21:22], None, ALU.mult))
                done(v.tensor_tensor(r, r, m, ALU.subtract), "r_ok")

            def exps(t):
                k = t % 2
                dve.wait_ge(s["w_ok"], t + 1)
                for u in range(units(t)):
                    ks = slice(N * u, N * (u + 1))
                    last = v.scalar_tensor_tensor(bufs["e", k][:, ks], bufs["w", k][:, ks], sc[:, 28:29],
                                                  bufs["pw", k].bitcast(bf16)[:, ks], ALU.add, ALU.mult,
                                                  accum_out=S[:, k, u:u + 1])
                done(last, "e_ok")

            def probs(t):
                k, n = t % 2, units(t) * N
                dve.wait_ge(s["inv_ok"], t + 1)
                x = bufs["x", k]
                for u in range(units(t)):
                    ks = slice(N * u, N * (u + 1))
                    last = v.tensor_scalar(x[:, ks], bufs["e", k][:, ks], S[:, k, u:u + 1], None, ALU.mult)
                done(last)
                done(v.tensor_scalar(x[:, 0:n].bitcast(bf16), x[:, 0:n], RSCALE, None, ALU.mult))
                xi = x[:, 0:n].bitcast(i16).rearrange("p (u n) -> p u n", n=N)
                p = bufs["q", k]
                u = units(t)
                for dst, ks in ((p[:, 0:P * u], slice(0, P)), (p[:, P * u:N * u], slice(P, N))):
                    last = v.tensor_scalar(dst.rearrange("p (u n) -> p u n", u=u), xi[:, :, ks], 0x7F80, 0x7F80,
                                           ALU.bitwise_xor, ALU.bitwise_and)
                done(last, "p_ok")

            def keep_out(t):
                R = rows(t)
                dve.wait_ge(s["o_mm"], t + 1)
                o = bank(6 + t % 2)[0:R]
                if batches(t) == 1:
                    done(v.tensor_scalar(obuf[0:R, t, :], o[:, 0:D], batch_sel[0:R, t, 0:1], None, ALU.mult), "o_ok")
                else:
                    done(v.tensor_scalar(obuf[0:R, t, :], o[:, 0:D], batch_sel[0:R, t, 0:1], None, ALU.mult))
                    done(v.scalar_tensor_tensor(obuf[0:R, t, :], o[:, D:2 * D], batch_sel[0:R, t, 1:2], obuf[0:R, t, :],
                                                ALU.mult, ALU.add), "o_ok")

            for i in range(T + 3):
                if i < T:
                    split(i)
                if 1 <= i <= T:
                    exps(i - 1)
                if 2 <= i <= T + 1:
                    probs(i - 2)
                if i == 2:
                    done(v.memset(obuf[:, T - 1, :], 0.0))
                if i >= 3:
                    keep_out(i - 3)
            quantiser(36, sy, obuf_w, obuf_w, AX.X)
            done(v.tensor_scalar(oint, obuf, sc[:, 37:38], sc[:, 38:39], ALU.mult, ALU.min))
            done(v.tensor_copy(obf, oint), "obf_ok")
            done(v.tensor_scalar(proj_scale[:, :], proj_scale[:, :], sc[:, 36:37], None, ALU.mult))
            for t in range(T):
                R = rows(t)
                dve.wait_ge(s["pr_mm"], t + 1)
                done(v.tensor_tensor(obuf[0:R, t, :], bank(2 + t % 4)[0:R, 0:D], proj_scale[0:R, :], ALU.mult), "y2_ok")
                done(v.tensor_tensor(obuf[0:R, t, :], obuf[0:R, t, :], bproj_b[0:R, :], ALU.add))
            quantiser(44, None, obuf_w, obuf_w, AX.X)
            dve.wait_ge(s["oT_mm"], T)
            done(v.tensor_scalar(oint, obuf, sc[:, 45:46], sc[:, 46:47], ALU.mult, ALU.min))
            done(v.scalar_tensor_tensor(h[:, :, :], oint, sc[:, 44:45], h[:, :, :], ALU.mult, ALU.add))
            layer_norm(xf, "xf_ok")
            dve.wait_ge(s["lg_mm"], 1)
            L = [lg[:, k, :, :] for k in range(6)]

            def wide(col):
                return rt[:, col, :].unsqueeze(2).to_broadcast([P, T, EXP])

            for t0, t1, R in ((0, T - 1, P), (T - 1, T, LAST)):
                done(v.tensor_tensor(L[0][0:R, t0:t1], bank(2)[0:R, EXP * t0:EXP * t1].rearrange("p (t e) -> p t e", e=EXP),
                                     swb_b[0:R, :].unsqueeze(1).to_broadcast([R, t1 - t0, EXP]), ALU.add))
            done(v.tensor_reduce(rt[:, 0, :], L[0], AX.X, ALU.max))
            done(v.tensor_tensor(L[2], L[0], wide(0), ALU.subtract), "lg_ok")
            done(v.tensor_tensor(L[1], L[0], wide(0), ALU.is_equal))
            done(v.scalar_tensor_tensor(L[4], L[1], -float(EXP), expert_no, ALU.mult, ALU.add))
            done(v.tensor_reduce(rt[:, 3, :], L[4], AX.X, ALU.min))
            for t0, t1, R in ((0, T - 1, P), (T - 1, T, LAST)):
                done(v.tensor_tensor(onehot[0:R, t0:t1, :], L[4][0:R, t0:t1],
                                     rt[0:R, 3, t0:t1].unsqueeze(2).to_broadcast([R, t1 - t0, EXP]), ALU.is_equal))
            dve.wait_ge(s["ex_ok"], 1)
            done(v.tensor_reduce(rt[:, 1, :], L[3], AX.X, ALU.add))
            done(v.reciprocal(rt[:, 2, :], rt[:, 1, :]), "p_col")
            dve.wait_ge(s["prow_ok"], 1)
            for t in range(T):
                R = rows(t)
                p = rt[0:R, 2, t:t + 1]
                lo, hi = P * t, P * t + R
                if lo:
                    v.tensor_scalar(G[0:R, t, 0:lo], prow[0:R, 0:lo], p, None, ALU.is_lt)
                if hi < TOK:
                    v.tensor_scalar(G[0:R, t, hi:], prow[0:R, hi:], p, None, ALU.is_le)
                done(v.tensor_scalar(G[0:R, t, lo:hi], prow[0:R, lo:hi], p, None, ALU.is_lt))
                done(v.scalar_tensor_tensor(tie[0:R, 0:R], prow[0:R, lo:hi], p, lower[0:R, 0:R], ALU.is_equal, ALU.mult))
                done(v.tensor_tensor(G[0:R, t, lo:hi], G[0:R, t, lo:hi], tie[0:R, 0:R], ALU.add), "cmp_ok")
            dve.wait_ge(s["cntT_mm"], 1)
            for t0, t1, R in ((0, T - 1, P), (T - 1, T, LAST)):
                done(v.tensor_tensor(L[5][0:R, t0:t1], bank(6)[0:R, EXP * t0:EXP * t1].rearrange("p (t e) -> p t e", e=EXP),
                                     onehot[0:R, t0:t1, :], ALU.mult))
            done(v.tensor_reduce(rt[:, 4, :], L[5], AX.X, ALU.add))
            done(v.tensor_scalar(rt[:, 5, :], rt[:, 4, :], float(CAP), 1e6, ALU.is_ge, ALU.mult))
            done(v.tensor_scalar(rt[:, 6, :], rt[:, 3, :], float(EXP), float(SLOTS), ALU.add, ALU.mult))
            done(v.tensor_tensor(rt[:, 5, :], rt[:, 5, :], rt[:, 4, :], ALU.add))
            done(v.tensor_tensor(slot[:, :], rt[:, 5, :], rt[:, 6, :], ALU.add), "slot_ok")
            for e in range(EXP + 1):
                if e < EXP:
                    dve.wait_ge(s["xeT_mm"], e + 1)
                    if e >= 2:
                        dve.wait_ge(s["h_mm"], 3 * (e - 1))
                    v.tensor_copy(xeT[0:DC, e % 2], bank(0)[0:DC, 0:2 * SLOTS].rearrange("p (c n) -> p c n", c=2)
                                  ).then_inc(s["xeT_ok"], 1)
                if e >= 1:
                    u = e - 1
                    dve.wait_ge(s["oe_mm"], u + 1)
                    if u >= 2:
                        dve.wait_ge(s[("oe_out0", "oe_out1")[u % 2]], 16 * (u // 2))
                    v.tensor_copy(oe[0:HALF, u % 2], bank(1)[0:HALF, 0:2 * D].rearrange("p (a d) -> p a d", a=2)
                                  ).then_inc(s["oe_ok"], 1)
            dve.wait_ge(s["gath"], 16 * T)
            for t in range(T):
                R = rows(t)
                v.scalar_tensor_tensor(h[0:R, t, :], xf[0:R, t, :], rt[0:R, 2, t:t + 1], h[0:R, t, :],
                                       ALU.mult, ALU.add).then_inc(s["out_ok"], 1)


def constants():
    import numpy as np
    c = np.zeros((P, C_END), np.float32)
    p = np.arange(P)
    c[p, C_ID + p] = 1.0
    tok = np.arange(TOK)
    c[:, C_PAR:C_PAR + TOK] = ((p[:, None] // HD) % 2 == (tok[None, :] // N) % 2)
    for j in range(HQ):
        for g in range(HG):
            for k in range(3):
                c[32 * j + 3 * g + k, C_SEL + N * g:C_SEL + N * (g + 1)] = 1.0
    c[:, C_LOW:C_LOW + P] = p[:, None] < p[None, :]
    for t in range(T):
        b = np.minimum((P * t + p) // N, B - 1)
        c[:, C_BSEL + 2 * t] = (b == first_batch(t)) * PSCALE
        c[:, C_BSEL + 2 * t + 1] = (b != first_batch(t)) * PSCALE
    c[:, C_EXP:] = np.tile(np.arange(EXP), T)[None, :]
    return c


def kernel(x, txt, L0_tok_W_lin, L0_tok_b_lin, L0_attn_w_qkv, L0_attn_b_qkv, L0_attn_w_proj, L0_attn_b_proj,
           L0_ffn_switch_w, L0_ffn_switch_b, L0_ffn_w1, L0_ffn_b1, L0_ffn_w2, L0_ffn_b2):
    import numpy as np
    import concourse.bacc as bacc
    from concourse.bass_utils import run_bass_kernel_spmd

    hp = IMG // PATCH
    a = {}
    xs = np.asarray(x).reshape(B, CH, hp, PATCH, hp, PATCH).transpose(3, 5, 1, 0, 2, 4)
    a["x"] = xs.reshape(KC, P, B * NIMG).transpose(1, 0, 2)
    a["wlin"] = np.asarray(L0_tok_W_lin).T.reshape(KC, P, D).transpose(1, 0, 2)
    a["blin"] = np.asarray(L0_tok_b_lin)
    a["txt"] = np.asarray(txt)
    order = np.arange(D).reshape(HG, HQ, HD).transpose(1, 0, 2).reshape(-1)
    wq = np.asarray(L0_attn_w_qkv)
    bq = np.asarray(L0_attn_b_qkv)
    rows_ = np.concatenate([np.arange(2 * D), 2 * D + order])
    wq = np.concatenate([wq[rows_], np.asarray(L0_attn_w_proj)[:, order]], 0)
    a["wqkv"] = wq.reshape(8, DC, D).transpose(1, 0, 2)
    a["bqkv"] = bq[rows_]
    a["bproj"] = np.asarray(L0_attn_b_proj)
    a["sww"] = np.asarray(L0_ffn_switch_w).reshape(2, DC, EXP).transpose(1, 0, 2)
    a["swb"] = np.asarray(L0_ffn_switch_b)
    a["w1"] = np.asarray(L0_ffn_w1).reshape(EXP, 2, DC, F).transpose(2, 0, 1, 3)
    a["b1"] = np.asarray(L0_ffn_b1).reshape(EXP, FC, P).transpose(2, 0, 1)
    a["w2"] = np.asarray(L0_ffn_w2).reshape(EXP, FC, P, D).transpose(2, 0, 1, 3)
    a["b2"] = np.asarray(L0_ffn_b2)
    a["consts"] = constants()
    a = {k: np.ascontiguousarray(v) for k, v in a.items()}
    nc = bacc.Bacc("TRN2", target_bir_lowering=False, num_devices=1)
    ins = {k: nc.dram_tensor(k + "_dram", v.shape, mybir.dt.from_np(v.dtype), kind="ExternalInput").ap() for k, v in a.items()}
    out = nc.dram_tensor("out_dram", (TOK, D), mybir.dt.float32, kind="ExternalOutput").ap()
    fusion_kernel(nc, out=out, **ins)
    r = run_bass_kernel_spmd(nc, [{k + "_dram": v for k, v in a.items()}], core_ids=[0])
    return r.results[0]["out_dram"].reshape(B, N, D)
```

```python
import concourse.bass as bass
from concourse import mybir
from contextlib import ExitStack

B, CH, IMG, PATCH = 8, 3, 96, 16
D = 192
NIMG = (IMG // PATCH) ** 2
NTXT = 128
N = NIMG + NTXT
TOK = B * N
P = 128
T = -(-TOK // P)
LAST = TOK - (T - 1) * P
PD = CH * PATCH * PATCH
KC = PD // P
H, HD = 12, 16
HG, HQ = 3, 4
DC = D // 2
QKV = 3 * D
EXP, F = 8, 768
CAP = int(1.25 * TOK / EXP)
SLOTS = CAP + CAP % 2
SD = 2 * D + 2
NOBODY = 1e6
HALF = SLOTS // 2
FC = F // P
KR = N - P
EB = 3
ET = -(-B // EB)
EPS = 1.1920928955078125e-07
LNEPS = 1e-5
MAGIC = 1.5 * 2.0 ** 23
PSCALE = 2.0 ** 111
RSCALE = (4.0 / 3.0) * (1.0 - 2.0 ** -9 * (1.0 - 2.0 ** -9)) * 2.0 ** 112


LNT = ((0, EB * N // P), (EB * N // P, 2 * EB * N // P), (2 * EB * N // P, T))
assert ET == 3
TH = T // 2 + 1
TQ = T // 2 + 1
PB = P * TQ // N - 1


YT = (0, 2, 4, 6, 8)
Y2T = tuple(t + 1 for t in YT[1:])


def rows(t):
    return P if t < T - 1 else LAST


def first_batch(t):
    return P * t // N


def batches(t):
    return (P * t + rows(t) - 1) // N - first_batch(t) + 1


def pieces(b, lo, hi):
    out, n = [], lo
    while n < hi:
        at = N * b + n
        k = min(hi - n, P - at % P)
        out.append((at // P, at % P, n, k))
        n += k
    return out


C_ID, C_PAR, C_SEL, C_LOW, C_BSEL, C_EXP = 0, P, P + TOK, P + TOK + HG * N, 2 * P + TOK + HG * N, 2 * P + TOK + HG * N + 2 * T
C_TOK = C_EXP + T * EXP
C_END = C_TOK + T


def fusion_kernel(nc, x, wlin, blin, txt, wqkv, bqkv, bproj, sww, swb, w1, b1, w2, b2, consts, out):
    f32, bf16, i16, u16, u32 = (mybir.dt.float32, mybir.dt.bfloat16, mybir.dt.int16, mybir.dt.uint16,
                                mybir.dt.uint32)
    ALU = mybir.AluOpType
    ACT = mybir.ActivationFunctionType
    AX = mybir.AxisListType

    ctx = ExitStack()
    with ctx:
        def sb(name, shape, dt=f32):
            return ctx.enter_context(nc.sbuf_tensor(name, shape, dt))[:]

        def sem(name):
            return ctx.enter_context(nc.semaphore(name))

        def dram(name, shape, dt):
            return nc.dram_tensor(name, shape, dt, kind="Internal").ap()

        v_dram = dram("v_dram", (TOK, D), bf16)
        slots = dram("slots", (EXP * SLOTS, SD), f32)

        UW = H * N
        HE = 2
        cst = sb("cst", [P, C_END])
        ident = cst[:, C_ID:C_ID + P]
        parity = cst[:, C_PAR:C_PAR + TOK]
        lower = cst[:, C_LOW:C_LOW + P]
        batch_sel = cst[:, C_BSEL:C_BSEL + 2 * T].rearrange("p (t b) -> p t b", b=2)
        expert_no = cst[:, C_EXP:C_EXP + T * EXP].rearrange("p (t e) -> p t e", e=EXP)
        token_no = cst[:, C_TOK:C_END]
        ident_b = sb("ident_b", [P, P], bf16)
        sel_b = sb("sel_b", [P, HG * N], bf16)
        xs = sb("xs", [P, T, SD])
        xf, h = xs[:, :, 0:D], xs[:, :, D:2 * D]
        xT = sb("xT", [DC, 2, TOK])
        wprojT = sb("wprojT", [DC, 2, D], bf16)
        proj_scale = sb("proj_scale", [P, D])
        bproj_b = sb("bproj_b", [P, D])
        swb_b = sb("swb_b", [P, EXP])
        sww_s = sb("sww_s", [DC, 2, EXP])
        probsT = sb("probsT", [P, 16, P], bf16)
        b1_s = sb("b1_s", [P, EXP, FC])
        stat = sb("stat", [P, T, 6])
        mv = sb("mv", [P, T, 2])
        var = sb("var", [P, T])
        std = sb("std", [P, T])
        rstd = sb("rstd", [P, T])
        ymax = sb("ymax", [P, T])
        ymin = sb("ymin", [P, T])
        rmax = sb("rmax", [P, T * H])
        gcol = sb("gcol", [P, 2])
        gred = sb("gred", [P, 2])
        sc = sb("sc", [P, 64])
        S = sb("S", [P, 2, H])
        lg = sb("lg", [P, 6, T, EXP])
        onehot = sb("onehot", [P, T, EXP], bf16)
        rt = sb("rt", [P, 8, T])
        slot = sb("slot", [P, T], u32)
        whose = sb("whose", [HALF, EXP, 2], u32)
        empty = sb("empty", [HALF, SD])
        ones = sb("ones", [1, P])
        zeros = sb("zeros", [P, T * EXP], bf16)
        w1_a = sb("w1_a", [DC, HE, 2, F])
        w2_a = sb("w2_a", [P, HE, FC, D])

        def cutter(name, words):
            whole, at = sb(name, [P, words]), [0]

            def cut(n, dt=f32):
                if n is None:
                    at[0] = 0
                    return None
                assert at[0] + n <= words, (name, at, n)
                v = whole[:, at[0]:at[0] + n]
                at[0] += n
                return v if dt == f32 else v.bitcast(dt)
            return cut

        cut = cutter("attn", 3 * HG * TOK // 2 + 2 * B * D // 2 + T * P // 2)
        qT = cut(HG * TOK // 2, bf16).rearrange("p (g n) -> p g n", g=HG)
        kT = cut(HG * TOK // 2, bf16).rearrange("p (g n) -> p g n", g=HG)
        kpair = cut(HG * (B - 1) * N // 2, bf16).rearrange("p (g n) -> p g n", g=HG)
        vmain = cut(B * D // 2, bf16).rearrange("p (b u d) -> p b u d", b=B, u=H)
        vrest = cut(B * D // 2, bf16).rearrange("p (b j c) -> p b j c", b=B, j=HQ)
        nbT = cut(T * P // 2, bf16)
        cut(None)
        G = cut(T * TOK // 2, bf16).rearrange("p (t n) -> p t n", n=TOK)
        cut(None)
        xeT = cut(2 * 2 * SLOTS).rearrange("p (k c n) -> p k c n", k=2, c=2)
        hT = cut(2 * FC * SLOTS).rearrange("p (k f n) -> p k f n", k=2, f=FC)
        oe = cut(2 * 2 * D).rearrange("p (k a d) -> p k a d", k=2, a=2)

        NB2 = EXP - HE
        cut = cutter("region", 18432)
        xn = cut(T * D).rearrange("p (t d) -> p t d", d=D)
        y = cut(T * QKV).rearrange("p (t c) -> p t c", c=QKV)
        yint = cut(T * QKV // 2, i16).rearrange("p (t c) -> p t c", c=QKV)
        emb_w = cut(KC * D).rearrange("p (c e) -> p c e", e=D)
        blin_b = cut(D)
        emb = cut(ET * D).rearrange("p (t e) -> p t e", e=D)
        wall = cut(8 * D).rearrange("p (g i) -> p g i", g=8)[0:DC]
        wdeq = cut(8 * D).rearrange("p (g i) -> p g i", g=8)[0:DC]
        bqkv_b = cut(QKV)
        wqkvT = cut(2 * QKV).rearrange("p (c o) -> p c o", c=2)[0:DC]
        qk2 = y.rearrange("p t c -> p (t c)")[:, 0:T * 2 * D].bitcast(bf16).rearrange("p (t k c) -> p t k c", t=T, k=2 * HG)
        cut(None)
        bufs = {}
        for k in range(2):
            for n, words, dt in (("m", UW // 2, i16), ("q", UW // 2, i16), ("r", UW // 2, i16), ("pw", UW // 2, i16),
                                 ("x", UW // 2, u16), ("w", UW, f32), ("e", UW, f32)):
                bufs[n, k] = cut(words, dt)
        cut(None)
        w1_b = cut(NB2 * 2 * F).rearrange("p (e c f) -> p e c f", e=NB2, c=2)
        b2_s = cut(EXP * D).rearrange("p (e d) -> p e d", e=EXP)
        w2_b = cut(NB2 * FC * D).rearrange("p (e c d) -> p e c d", e=NB2, c=FC)
        cut = cutter("share", EXP * 2 * SD)
        patches = cut(KC * B * NIMG).rearrange("p (c n) -> p c n", c=KC)
        cut(None)
        oT = cut(TOK, bf16).rearrange("p (c n) -> p c n", c=2)[0:DC]
        y2int, oint = (cut(T * D // 2, i16).rearrange("p (t d) -> p t d", d=D) for _ in range(2))
        obf = cut(T * D // 2, bf16).rearrange("p (t d) -> p t d", d=D)
        cut(None)
        prow = cut(TOK)
        cut(None)
        xe = cut(EXP * 2 * SD).rearrange("p (e a d) -> p e a d", e=EXP, a=2)
        cut = cutter("obuf", T * D)
        obuf_w = cut(T * D)
        obuf = obuf_w.rearrange("p (t d) -> p t d", d=D)
        cut(None)
        nm = cut(T * H)
        nb = cut(T * H)
        nb2 = cut(T * H)
        nb3 = cut(T * H)
        parts = [cut(T * H // 2, bf16) for _ in range(3)]
        nb_parts = cut(T * P // 2, bf16).rearrange("p (t c) -> p t c", c=P)
        tie = probsT.rearrange("p u n -> p (u n)")[:, 0:TOK]
        wst = sb("wst", [DC, 8, 8])
        wproj_n = probsT.rearrange("p u n -> p (u n)")[0:DC, 0:2 * D].rearrange("p (a d) -> p a d", a=2)
        ps = ctx.enter_context(nc.psum_tensor("ps", [P, 8 * 512], f32))

        def bank(k, n=1):
            return ps[:, 512 * k:512 * (k + n)]

        def bankb(k, n=1):
            return ps[:, 512 * k:512 * (k + n)].bitcast(bf16)

        def w1_of(e):
            return w1_a[:, e] if e < HE else w1_b[0:DC, e - HE]

        def w2_of(e):
            return w2_a[:, e] if e < HE else w2_b[:, e - HE]

        names = ("yint_ok v_int h_in0 h_in1 h_in2 xe_first oe_read cst_in emb_in w_in bias_in txt_in h_in ffn_in ffn_in2 zeroed v_out v_in v_zero xe_in oe_out0 oe_out1 scat stored "
                 "pool_zero emb_mm emb_sb var_ok std_ok xn_ok xnT_mm xT_ok wdeq_ok wproj_ok wT_mm wT_ok qkv_mm y_ok g_col g_T copy_a copy_b "
                 "qT_mm kT_mm q_ok k_ok pair_ok s0_mm s0_read nb_ok nbT_mm nbT_ok s_mm m_ok r_ok w_ok e_ok inv_ok p_ok "
                 "pT_mm pT_ok o_mm o_ok obf_ok oT_mm oT_ok pr_mm y2_ok xf_ok lg_mm lg_ok ex_ok p_col prow_mm prow_ok "
                 "cmp_ok cnt_mm slot_ok xeT_mm xeT_ok h_mm h_ok oe_mm oe_ok out_ok dve_order act_order cst_b pool_made q_done pw_ok y2_sum o_first nb_free half_b k_at qx_done x_done pow_done tie_ok lt_ok le_ok whose_ok").split()
        s = {n: sem(n) for n in names}

        block = ctx.enter_context(nc.Block())
        text = [(b, pc) for b in range(B) for pc in pieces(b, NIMG, N)]
        image = [(b // EB, NIMG * (b % EB) + pc[2], pc) for b in range(B) for pc in pieces(b, 0, NIMG)]

        def units(t):
            return H if t < T - 1 else HG

        @block.sync
        def _(sp):
            def load(dst, src, what):
                sp.dma_start(dst, src).then_inc(s[what], 16)

            load(patches, x, "emb_in")
            load(emb_w, wlin, "emb_in")
            load(blin_b[0:1], blin.partition_broadcast(1), "emb_in")
            load(cst[:, :], consts, "cst_in")
            load(bqkv_b, bqkv.partition_broadcast(P), "bias_in")
            load(bproj_b[:, :], bproj.partition_broadcast(P), "bias_in")
            load(swb_b[:, :], swb.partition_broadcast(P), "bias_in")
            load(sww_s[:, :, :], sww, "bias_in")
            sp.wait_ge(s["pool_zero"], 1)
            for b, (t, r, n, k) in text:
                load(h[r:r + k, t, :], txt[b, n - NIMG:n - NIMG + k, :], "txt_in")
            for j, n, (t, r, m, k) in image:
                sp.wait_ge(s["emb_sb"], j + 1)
                load(h[r:r + k, t, :], emb[n:n + k, j, :], ("h_in0", "h_in1", "h_in2")[j])
            sp.wait_ge(s["pool_zero"], 8)
            load(slots.rearrange("(p a) d -> p a d", p=HALF), empty.unsqueeze(1).to_broadcast([HALF, EXP * SLOTS // HALF, SD]), "zeroed")
            load(w1_a[:, :, :, :], w1[:, 0:HE], "ffn_in")
            load(w2_a[:, :, :, :], w2[:, 0:HE], "ffn_in")
            load(b1_s[:, :, :], b1, "ffn_in")
            sp.wait_ge(s["v_int"], 1)
            vint = yint.bitcast(bf16)
            load(v_dram[0:(T - 1) * P, :].rearrange("(t p) c -> p t c", p=P), vint[:, 0:T - 1, 2 * D:], "v_out")
            load(v_dram[(T - 1) * P:, :], vint[0:LAST, T - 1, 2 * D:], "v_out")
            sp.wait_ge(s["v_out"], 32)
            vb = v_dram.rearrange("(b n) c -> n b c", n=N)
            load(vmain.rearrange("p b u d -> p b (u d)"), vb[0:P], "v_in")
            sp.wait_ge(s["v_zero"], 2)
            for b in range(B):
                for g in range(HG):
                    load(vrest[KR * g:KR * (g + 1), b, :, HD * g:HD * (g + 1)],
                         vb[P:N, b, :].rearrange("n (j g d) -> n j g d", j=HQ, g=HG)[:, :, g, :], "v_in")
            sp.wait_ge(s["p_ok"], 2 * T)
            sp.wait_ge(s["inv_ok"], T)
            sp.wait_ge(s["pT_mm"], T)
            load(w1_b[0:DC], w1[:, HE:], "ffn_in2")
            load(w2_b, w2[:, HE:], "ffn_in2")
            load(b2_s, b2.partition_broadcast(P), "ffn_in2")
            for t in range(T):
                sp.wait_ge(s["out_ok"], t + 1)
                load(out[P * t:P * t + rows(t), :], obuf[0:rows(t), t, :], "stored")
            sp.wait_ge(s["scat"], 16 * T)
            for e in range(EXP):
                load(xe[0:HALF, e], slots[e * SLOTS:(e + 1) * SLOTS, :].rearrange("(a p) d -> p a d", a=2),
                     "xe_first" if e == 0 else "xe_in")

        @block.gpsimd
        def _(pool):
            pool.memset(h[:, T - 1, :], 0.0).then_inc(s["pool_zero"], 1)
            pool.memset(ones, 1.0).then_inc(s["pool_zero"], 1)
            pool.memset(y[:, T - 1, :], 0.0).then_inc(s["pool_zero"], 1)
            pool.memset(lg, 0.0).then_inc(s["pool_zero"], 1)
            pool.memset(onehot, 0.0).then_inc(s["pool_zero"], 1)
            pool.memset(rmax, 0.0).then_inc(s["pool_zero"], 1)
            pool.memset(zeros, 0.0).then_inc(s["pool_zero"], 1)
            pool.memset(empty, 0.0).then_inc(s["pool_made"], 1)
            pool.wait_ge(s["pool_made"], 1)
            pool.memset(empty[:, 2 * D:2 * D + 1], NOBODY).then_inc(s["pool_zero"], 1)
            pool.memset(vrest, 0.0).then_inc(s["v_zero"], 1)
            pool.memset(obuf_w, 0.0).then_inc(s["v_zero"], 1)
            for t in range(T):
                R = rows(t)
                pool.wait_ge(s["y2_ok"], t + 1)
                pool.tensor_tensor(obuf[0:R, t, :], obuf[0:R, t, :], bproj_b[0:R, :], ALU.add).then_inc(s["y2_sum"], 1)
            pool.wait_ge(s["zeroed"], 16)
            pool.wait_ge(s["xf_ok"], T + 2)
            for t in range(T):
                if t == 0 or t == TH:
                    pool.wait_ge(s["slot_ok"], 1 if t == 0 else 2)
                pool.indirect_dma_start(out=slots, out_offset=bass.IndirectOffsetOnAxis(ap=slot[0:rows(t), t:t + 1], axis=0),
                                        in_=xs[0:rows(t), t, :], in_offset=None, bounds_check=EXP * SLOTS - 1,
                                        oob_is_err=False).then_inc(s["scat"], 16)
            pool.wait_ge(s["stored"], 16 * T)
            pool.wait_ge(s["whose_ok"], 1)
            for e in range(EXP):
                pool.wait_ge(s["oe_ok"], 2 * (e + 1))
                for a in range(2):
                    pool.indirect_dma_start(out=out, out_offset=bass.IndirectOffsetOnAxis(ap=whose[0:HALF, e, a:a + 1], axis=0),
                                            in_=oe[0:HALF, e % 2, a, :], in_offset=None, bounds_check=TOK - 1,
                                            oob_is_err=False).then_inc(s[("oe_out0", "oe_out1")[e % 2]], 16)
            pool.wait_ge(s["oe_out0"], 16 * EXP)
            pool.wait_ge(s["oe_out1"], 16 * EXP)

        def compares(half):
            a, b = ((0, P * TH), (P * TH, TOK))[half]
            for t in range(T):
                end = P * t + rows(t)
                if end > a:
                    yield "lt", t, a, min(b, end)
                if end < b:
                    yield "le", t, max(a, end), b
                if t >= 1 and a <= P * (t - 1) < b:
                    yield "tie", t - 1, P * (t - 1), end - rows(t)
            if a <= P * (T - 1) < b:
                yield "tie", T - 1, P * (T - 1), TOK

        def scores_of(t):
            b, R = first_batch(t), rows(t)
            for j in range(HQ):
                for g in range(HG):
                    rws = slice(32 * j, 32 * j + 32)
                    keys = (kpair if batches(t) == 2 else kT)[rws, g, N * b:N * (b + 1)]
                    qs = qT[rws, g, P * t:P * t + R]
                    if t < T - 1:
                        yield j, g, slice(0, P), slice(N * g, N * (g + 1)), qs, keys
                    else:
                        yield 0, g, rws, slice(N * g, N * (g + 1)), qs, keys

        def scores_view(t, k):
            if t < T - 1:
                return bank(k, 4).rearrange("p (a c) -> p a c", a=4)[:, :, 0:HG * N]
            return bank(k)[:, 0:HG * N]

        @block.tensor
        def _(pe):
            mm = nc.tensor.matmul
            tr = nc.tensor.transpose
            pe.wait_ge(s["emb_in"], 48)
            for j in range(ET):
                n = min(EB, B - EB * j) * NIMG
                if j == 0:
                    pe.wait_ge(s["pool_zero"], 2)
                mm(bank(j)[0:n, 0:D], ones[:, 0:n], blin_b[0:1, :], start=True, stop=False)
                for c in range(KC):
                    last = mm(bank(j)[0:n, 0:D], patches[:, c, EB * NIMG * j:EB * NIMG * j + n], emb_w[:, c, :],
                              start=False, stop=(c == KC - 1))
                last.then_inc(s["emb_mm"], 1)
            pe.wait_ge(s["wdeq_ok"], 1)
            pe.wait_ge(s["cst_in"], 16)
            for c in range(2):
                for o in range(6):
                    last = tr(bank(3 + 2 * c + o // 3)[0:DC, DC * (o % 3):DC * (o % 3 + 1)],
                              wdeq[:, o, DC * c:DC * (c + 1)], ident[0:DC, 0:DC])
            last.then_inc(s["wT_mm"], 1)
            pe.wait_ge(s["wproj_ok"], 1)
            pe.wait_ge(s["cst_b"], 2)
            for c in range(2):
                for o in range(2):
                    tr(bankb(7)[0:DC, D * c + DC * o:D * c + DC * (o + 1)], wproj_n[:, o, DC * c:DC * (c + 1)],
                       ident_b[0:DC, 0:DC])
            for o in range(2):
                last = tr(bank(7)[:, 256 + DC * o:256 + DC * (o + 1)], wst[:, 6 + o, 2:3].to_broadcast([DC, P]),
                          ident[0:DC, 0:DC])
            last.then_inc(s["wT_mm"], 1)
            pe.wait_ge(s["wT_ok"], 3)
            def turn(t, src, ready, banks=(0, 1)):
                R = rows(t)
                pe.wait_ge(s[ready[0]], ready[1])
                for c in range(2):
                    last = tr(bank(banks[t % len(banks)])[0:DC, P * c:P * c + R], src[0:R, t, DC * c:DC * (c + 1)], ident[0:R, 0:R])
                last.then_inc(s["xnT_mm"], 1)

            def qkv(t):
                R = rows(t)
                pe.wait_ge(s["xT_ok"], t + 1)
                if t >= 3:
                    pe.wait_ge(s["y_ok"], t - 2)
                for a in range(2):
                    for c in range(2):
                        last = mm(bank(2 + 2 * (t % 3) + a)[0:R, 0:QKV // 2], xT[:, c, P * t:P * t + R],
                                  wqkvT[:, c, QKV // 2 * a:QKV // 2 * (a + 1)], start=(c == 0), stop=(c == 1))
                last.then_inc(s["qkv_mm"], 1)

            for t in range(T + 1):
                if t < T:
                    if t >= 2:
                        pe.wait_ge(s["xT_ok"], t - 1)
                    turn(t, xn, ("xn_ok", t + 1))
                if t >= 1:
                    qkv(t - 1)

            def global_stat(n):
                pe.wait_ge(s["g_col"], n)
                for a in range(2):
                    last = tr(bank(7)[:, P * a:P * (a + 1)], gcol[:, a:a + 1].to_broadcast([P, P]), ident)
                last.then_inc(s["g_T"], 1)

            global_stat(1)
            for t in range(T):
                R = rows(t)
                pe.wait_ge(s["copy_a"], 1 if t < TQ else 2)
                pe.wait_ge(s["copy_b"], 1 if t < TQ else 2)
                for k, name, ok in ((0, "qT_mm", "q_ok"), (1, "kT_mm", "k_ok")):
                    if t >= 2:
                        pe.wait_ge(s[ok], t - 1)
                    for g in range(HG):
                        last = tr(bankb(2 * k + t % 2)[:, P * g:P * g + R], qk2[0:R, t, HG * k + g, :], ident_b[0:R, 0:R])
                    last.then_inc(s[name], 1)
            for t in range(T):
                R = rows(t)
                pe.wait_ge(s["pair_ok"], 1 if t < TQ - 1 else 2)
                if t == 1:
                    pe.wait_ge(s["q_ok"], T)
                    pe.wait_ge(s["k_ok"], T)
                if t >= 2:
                    pe.wait_ge(s["s0_read"], t - 1)
                for j, g, prt, col, qs, keys in scores_of(t):
                    last = mm(bank(4 * ((t + 1) % 2) + j)[prt, col], qs, keys, start=True, stop=True)
                last.then_inc(s["s0_mm"], 1)
            global_stat(2)
            pe.wait_ge(s["nb_ok"], 1)
            for t in range(T):
                last = tr(bankb(4, 2)[:, P * t:P * (t + 1)], nb_parts[:, t, :], ident_b)
            last.then_inc(s["nbT_mm"], 1)
            pe.wait_ge(s["nbT_ok"], 1)

            def scores(t):
                if t >= 1:
                    pe.wait_ge(s["m_ok"], t)
                if t < T - 1:
                    for j in range(HQ):
                        mm(bank(j)[:, 0:HG * N], nbT[32 * j:32 * j + 3 * HG, P * t:P * (t + 1)],
                           sel_b[32 * j:32 * j + 3 * HG, :], start=True, stop=True)
                        for jj, g, prt, col, qs, keys in scores_of(t):
                            if jj == j:
                                last = mm(bank(j)[prt, col], qs, keys, start=False, stop=True, skip_group_check=True)
                else:
                    mm(bank(0)[:, 0:HG * N], nbT[0:3 * HG, P * t:P * (t + 1)], sel_b[0:3 * HG, :], start=True, stop=True)
                    for _, g, prt, col, qs, keys in scores_of(t):
                        last = mm(bank(0)[prt, col], qs, keys, start=False, stop=True, skip_group_check=True)
                last.then_inc(s["s_mm"], 1)

            def turn_probs(t):
                pe.wait_ge(s["p_ok"], 2 * (t + 1))
                if t >= 1:
                    pe.wait_ge(s["pT_ok"], t)
                pr, n0 = bufs["q", t % 2].bitcast(bf16), P * units(t)
                for u in range(units(t)):
                    tr(bankb(4, 2)[:, P * u:P * (u + 1)], pr[:, P * u:P * (u + 1)], ident_b)
                for j in range(units(t) // HG):
                    last = tr(bankb(4, 2)[0:HG * KR, P * (H + j):P * (H + j + 1)], pr[:, n0 + HG * KR * j:n0 + HG * KR * (j + 1)],
                              ident_b)
                last.then_inc(s["pT_mm"], 1)

            def attend(t):
                b, nb_, R = first_batch(t), batches(t), rows(t)
                pe.wait_ge(s["pT_ok"], t + 1)
                if t == 0:
                    pe.wait_ge(s["v_in"], 16 * (1 + HG * B))
                if t >= 2:
                    pe.wait_ge(s["o_ok"], t - 1)
                o = bank(6 + t % 2)[0:R, 0:nb_ * D].rearrange("p (b c) -> p b c", b=nb_)
                for j in range(HQ):
                    if t < T - 1:
                        rest, main = probsT[0:HG * KR, H + j, :], [probsT[:, HG * j + g, :] for g in range(HG)]
                    else:
                        qs = slice(LAST * j, LAST * (j + 1))
                        rest, main = probsT[0:HG * KR, H, qs], [probsT[:, g, qs] for g in range(HG)]
                    mm(o[:, :, HG * HD * j:HG * HD * (j + 1)], rest, vrest[0:HG * KR, b:b + nb_, j, :],
                       start=True, stop=True)
                    for g in range(HG):
                        u = HG * j + g
                        last = mm(o[:, :, HD * u:HD * (u + 1)], main[g], vmain[:, b:b + nb_, u, :],
                                  start=False, stop=True, skip_group_check=True)
                last.then_inc(s["o_mm"], 1)

            scores(0)
            for i in range(T + 4):
                if i + 1 < T:
                    scores(i + 1)
                if i >= 4:
                    attend(i - 4)
                if 3 <= i < T + 3:
                    turn_probs(i - 3)
            global_stat(3)
            pe.wait_ge(s["obf_ok"], 1)
            for t in range(T + 1):
                if t < T:
                    R = rows(t)
                    if t >= 2:
                        pe.wait_ge(s["oT_ok"], t - 1)
                    for c in range(2):
                        last = tr(bankb(t % 2)[0:DC, P * c:P * c + R], obf[0:R, t, DC * c:DC * (c + 1)], ident_b[0:R, 0:R])
                    last.then_inc(s["oT_mm"], 1)
                if t >= 1:
                    u, R = t - 1, rows(t - 1)
                    pe.wait_ge(s["oT_ok"], u + 1)
                    if u >= 4:
                        pe.wait_ge(s["y2_ok"], u - 3)
                    for c in range(2):
                        last = mm(bank(2 + u % 4)[0:R, 0:D], oT[:, c, P * u:P * u + R], wprojT[:, c, :],
                                  start=(c == 0), stop=(c == 1))
                    last.then_inc(s["pr_mm"], 1)
            global_stat(4)
            for t in range(T + 1):
                if t < T:
                    pe.wait_ge(s["xT_ok"], T + max(t - 3, 0))
                    turn(t, xf, ("xf_ok", t + 1), (0, 1, 3, 4))
                if t >= 1:
                    u, R = t - 1, rows(t - 1)
                    pe.wait_ge(s["xT_ok"], T + u + 1)
                    for c in range(2):
                        last = mm(bank(2)[0:R, EXP * u:EXP * (u + 1)], xT[:, c, P * u:P * u + R], sww_s[:, c, :],
                                  start=(c == 0), stop=(c == 1))
            last.then_inc(s["lg_mm"], 1)
            pe.wait_ge(s["p_col"], 1)
            for t in range(T):
                R = rows(t)
                last = tr(bank(3, 3)[:, P * t:P * t + R], rt[0:R, 2, t:t + 1].to_broadcast([R, P]), ident[0:R, 0:R])
            last.then_inc(s["prow_mm"], 1)
            for half in range(2):
                mm(bank(6 + half)[:, 0:T * EXP], ident_b, zeros, start=True, stop=True)
            n = 0
            for half in range(2):
                todo = [t for _, t, _, _ in compares(half)]
                for t in range(T):
                    R = rows(t)
                    pe.wait_ge(s["cmp_ok"], n + len(todo) - todo[::-1].index(t))
                    for i in range((0, TH)[half], (TH, T)[half]):
                        last = mm(bank(6 + half)[0:rows(i), EXP * i:EXP * (i + 1)], G[0:R, t, P * i:P * i + rows(i)],
                                  onehot[0:R, t, :], start=False, stop=True, skip_group_check=True)
                last.then_inc(s["cnt_mm"], 1)
                n += len(todo)

            def expert_turn(e):
                if e <= 1:
                    pe.wait_ge(s["xe_first" if e == 0 else "xe_in"], 16 if e == 0 else 16 * (EXP - 1))
                if e >= 1:
                    pe.wait_ge(s["xeT_ok"], e)
                for c in range(2):
                    for a in range(2):
                        last = tr(bank(0)[0:DC, SLOTS * c + HALF * a:SLOTS * c + HALF * (a + 1)],
                                  xe[0:HALF, e, a, DC * c:DC * (c + 1)], ident[0:HALF, 0:HALF])
                last.then_inc(s["xeT_mm"], 1)

            def expert_in(e):
                pe.wait_ge(s["xeT_ok"], e + 1)
                if e == 0:
                    pe.wait_ge(s["ffn_in"], 48)
                if e == HE:
                    pe.wait_ge(s["ffn_in2"], 48)
                for f in range(FC):
                    if e >= 2 and f % 2 == 0:
                        pe.wait_ge(s["h_ok"], 3 * (e - 2) + f // 2 + 1)
                    for c in range(2):
                        last = mm(bank(2 + 3 * (e % 2) + f // 2)[:, SLOTS * (f % 2):SLOTS * (f % 2 + 1)],
                                  w1_of(e)[:, c, P * f:P * (f + 1)], xeT[0:DC, e % 2, c, :], start=(c == 0), stop=(c == 1))
                    if f % 2:
                        last.then_inc(s["h_mm"], 1)

            def expert_out(e):
                pe.wait_ge(s["h_ok"], 3 * (e + 1))
                if e >= 1:
                    pe.wait_ge(s["oe_read"], e)
                for a in range(2):
                    o = bank(1)[0:HALF, D * a:D * (a + 1)]
                    for f in range(FC):
                        last = mm(o, hT[:, e % 2, f, HALF * a:HALF * (a + 1)], w2_of(e)[:, f, :],
                                  start=(f == 0), stop=(f == FC - 1))
                last.then_inc(s["oe_mm"], 1)

            expert_turn(0)
            expert_in(0)
            expert_turn(1)
            for e in range(EXP):
                if e + 1 < EXP:
                    expert_in(e + 1)
                if e + 2 < EXP:
                    expert_turn(e + 2)
                expert_out(e)

        @block.scalar
        def _(act):
            A = nc.scalar.activation
            act.dma_start(wall, wqkv).then_inc(s["w_in"], 16)
            for j in range(ET):
                n = min(EB, B - EB * j) * NIMG
                act.wait_ge(s["emb_mm"], j + 1)
                A(emb[0:n, j, :], bank(j)[0:n, 0:D], ACT.Copy).then_inc(s["emb_sb"], 1)

            def deviation(c, n):
                t0, t1 = LNT[c]
                act.wait_ge(s["var_ok"], n + 1)
                A(std[:, t0:t1], var[:, t0:t1], ACT.Sqrt).then_inc(s["std_ok"], 1)

            deviation(0, 0)
            act.wait_ge(s["wT_mm"], 1)
            for c in range(2):
                A(wqkvT[:, c, :].rearrange("p (a o) -> p a o", a=2),
                  bank(3 + 2 * c, 2).rearrange("p (a o) -> p a o", a=2)[0:DC, :, 0:QKV // 2], ACT.Copy).then_inc(s["wT_ok"], 1)
            act.wait_ge(s["wT_mm"], 2)
            A(wprojT[:, :, :].rearrange("p c o -> p (c o)"), bankb(7)[0:DC, 0:2 * D], ACT.Copy).then_inc(s["wT_ok"], 1)
            A(proj_scale[:, :], bank(7)[:, 256:256 + D], ACT.Copy).then_inc(s["wT_ok"], 1)
            deviation(1, 1)

            def keep_turned(t, n, banks=(0, 1)):
                R = rows(t)
                act.wait_ge(s["xnT_mm"], n + 1)
                A(xT[:, :, P * t:P * t + R], bank(banks[t % len(banks)])[0:DC, 0:2 * P].rearrange("p (c n) -> p c n", c=2)[:, :, 0:R],
                  ACT.Copy).then_inc(s["xT_ok"], 1)

            for t in range(T):
                if t == 2:
                    deviation(2, 2)
                keep_turned(t, t)
            for n, (t0, t1) in enumerate(((0, TQ), (TQ, T))):
                act.wait_ge(s["yint_ok"], n + 1)
                A(qk2.rearrange("p t k (j a d) -> p t (k j) a d", j=HQ, a=2)[:, t0:t1, :, 1, :],
                  yint[:, t0:t1, 0:2 * D].rearrange("p t (x d) -> p t x d", d=HD), ACT.Copy).then_inc(s["copy_b"], 1)
            act.wait_ge(s["cst_in"], 16)
            for t in range(T):
                act.wait_ge(s["kT_mm"], t + 1)
                lo = P * t
                for b in range(first_batch(t), first_batch(t) + batches(t)):
                    hi = min(N * (b + 1), P * t + rows(t))
                    last = A(kT[:, :, lo:hi],
                             bankb(2 + t % 2)[:, 0:HG * P].rearrange("p (g n) -> p g n", g=HG)[:, :, lo - P * t:hi - P * t],
                             ACT.Copy, scale=parity[:, N * b:N * b + 1])
                    lo = hi
                last.then_inc(s["k_ok"], 1)
            A(yint.bitcast(bf16)[:, :, 2 * D:], yint[:, :, 2 * D:], ACT.Copy).then_inc(s["v_int"], 1)
            act.wait_ge(s["nbT_mm"], 1)
            A(nbT, bankb(4, 2)[:, 0:T * P], ACT.Copy).then_inc(s["nbT_ok"], 1)

            act.preload_act_table_set("natural_log_exp_and_others")

            def distance(t):
                act.wait_ge(s["s_mm"], t + 1)
                if t == 0:
                    act.wait_ge(s["k_at"], 1)
                    act.wait_ge(s["v_out"], 32)
                if t >= 2:
                    act.wait_ge(s["r_ok"], t - 1)
                m = bufs["m", t % 2][:, 0:units(t) * N]
                if t < T - 1:
                    m = m.rearrange("p (a c) -> p a c", a=4)
                A(m, scores_view(t, 0), ACT.Relu, scale=sc[:, 5:6], bias=sc[:, 24:25]).then_inc(s["m_ok"], 1)

            def square(t):
                act.wait_ge(s["r_ok"], t + 1)
                if t == 0:
                    act.wait_ge(s["half_b"], 1)
                if t >= 2:
                    act.wait_ge(s["e_ok"], t - 1)
                n = units(t) * N
                A(bufs["w", t % 2][:, 0:n], bufs["r", t % 2][:, 0:n], ACT.Square, bias=sc[:, 26:27]).then_inc(s["w_ok"], 1)

            def invert(t):
                act.wait_ge(s["e_ok"], t + 1)
                e = bufs["e", t % 2][:, 0:units(t) * N]
                A(e, e, ACT.Ln).then_inc(s["act_order"], 1)
                act.wait_ge(s["act_order"], t + 1)
                A(e, e, ACT.Exp, scale=-1.0).then_inc(s["inv_ok"], 1)

            def keep_probs(t):
                act.wait_ge(s["pT_mm"], t + 1)
                if t >= 1:
                    act.wait_ge(s["o_mm"], t)
                n, k = units(t), units(t) // HG
                A(probsT[:, 0:n, :].rearrange("p u n -> p (u n)"), bankb(4, 2)[:, 0:P * n], ACT.Copy)
                A(probsT[0:HG * KR, H:H + k, :].rearrange("p u n -> p (u n)"),
                  bankb(4, 2)[0:HG * KR, P * H:P * (H + k)], ACT.Copy).then_inc(s["pT_ok"], 1)

            def first_of_out(t):
                R = rows(t)
                act.wait_ge(s["o_mm"], t + 1)
                A(obuf[0:R, t, :], bank(6 + t % 2)[0:R, 0:D], ACT.Copy, scale=batch_sel[0:R, t, 0:1]).then_inc(s["o_first"], 1)

            act.wait_ge(s["nb_free"], 1)
            distance(0)
            for i in range(T + 4):
                if i + 1 < T:
                    distance(i + 1)
                if i >= 4:
                    first_of_out(i - 4)
                if 3 <= i < T + 3:
                    keep_probs(i - 3)
                if i < T:
                    square(i)
                if 1 <= i <= T:
                    invert(i - 1)
            for t in range(T):
                R = rows(t)
                act.wait_ge(s["oT_mm"], t + 1)
                A(oT[:, :, P * t:P * t + R], bankb(t % 2)[0:DC, 0:2 * P].rearrange("p (c n) -> p c n", c=2)[:, :, 0:R],
                  ACT.Copy).then_inc(s["oT_ok"], 1)
            deviation(0, 3)
            for t in range(T):
                if t == 1:
                    deviation(1, 4)
                if t == LNT[1][0] + 1:
                    deviation(2, 5)
                keep_turned(t, T + t, (0, 1, 3, 4))
            act.wait_ge(s["lg_ok"], 1)
            A(lg[:, 3, :, :], lg[:, 2, :, :], ACT.Exp).then_inc(s["ex_ok"], 1)
            act.wait_ge(s["prow_mm"], 1)
            A(prow, bank(3, 3)[:, 0:TOK], ACT.Copy).then_inc(s["prow_ok"], 1)
            for e in range(EXP):
                for f in range(FC):
                    if f % 2 == 0:
                        act.wait_ge(s["h_mm"], 3 * e + f // 2 + 1)
                        if e >= 2:
                            act.wait_ge(s["oe_mm"], e - 1)
                    last = A(hT[:, e % 2, f, :], bank(2 + 3 * (e % 2) + f // 2)[:, SLOTS * (f % 2):SLOTS * (f % 2 + 1)],
                             ACT.Gelu, bias=b1_s[:, e, f:f + 1])
                    if f % 2:
                        last.then_inc(s["h_ok"], 1)

        @block.vector
        def _(dve):
            v = nc.vector
            made = {n: 0 for n in names}

            def done(ins, what="dve_order"):
                made[what] += 1
                ins.then_inc(s[what], 1)
                dve.wait_ge(s[what], made[what])

            dve.wait_ge(s["w_in"], 16)
            W = [wst[:, :, k] for k in range(5)]
            done(v.tensor_reduce(W[0], wall, AX.X, ALU.max))
            done(v.tensor_reduce(W[1], wall, AX.X, ALU.min, negate=True))
            done(v.tensor_scalar(wst[:, :, 0:2], wst[:, :, 0:2], 0.0, None, ALU.max))
            done(v.tensor_tensor(W[2], W[0], W[1], ALU.add))
            done(v.tensor_scalar(W[2], W[2], 1.0 / 255.0, EPS, ALU.mult, ALU.max))
            done(v.reciprocal(W[3], W[2]))
            done(v.tensor_tensor(W[4], W[1], W[3], ALU.mult))
            done(v.tensor_scalar(W[4], W[4], -1.0, MAGIC, ALU.mult, ALU.add))
            done(v.tensor_scalar(W[4], W[4], 255.0 - MAGIC, None, ALU.add))
            for o in range(8):
                v.tensor_scalar(wdeq[:, o, :], wall[:, o, :], wst[:, o, 3:4], MAGIC, ALU.mult, ALU.add).then_inc(s["dve_order"], 1)
                made["dve_order"] += 1
            dve.wait_ge(s["dve_order"], made["dve_order"])
            for o in range(6):
                v.tensor_scalar(wdeq[:, o, :], wdeq[:, o, :], MAGIC, wst[:, o, 4:5], ALU.subtract, ALU.min).then_inc(s["dve_order"], 1)
                made["dve_order"] += 1
            for o in range(2):
                last = v.tensor_scalar(wproj_n[:, o, :], wdeq[:, 6 + o, :], MAGIC, wst[:, 6 + o, 4:5], ALU.subtract, ALU.min)
            last.then_inc(s["wproj_ok"], 1)
            dve.wait_ge(s["dve_order"], made["dve_order"])
            for o in range(6):
                last2 = v.tensor_scalar(wdeq[:, o, :], wdeq[:, o, :], wst[:, o, 2:3], None, ALU.mult)
            last2.then_inc(s["wdeq_ok"], 1)
            dve.wait_ge(s["cst_in"], 16)
            v.tensor_copy(ident_b[:, :], ident).then_inc(s["cst_b"], 1)
            v.tensor_copy(sel_b[:, :], cst[:, C_SEL:C_SEL + HG * N]).then_inc(s["cst_b"], 1)

            def layer_norm(dst, ok, t0, t1):
                for t in range(t0, t1):
                    v.bn_stats(stat[:, t, :], h[:, t, :]).then_inc(s["dve_order"], 1)
                made["dve_order"] += t1 - t0
                dve.wait_ge(s["dve_order"], made["dve_order"])
                for t in range(t0, t1):
                    v.bn_aggr(mv[:, t, :], stat[:, t, :]).then_inc(s["dve_order"], 1)
                made["dve_order"] += t1 - t0
                dve.wait_ge(s["dve_order"], made["dve_order"])
                v.tensor_scalar(var[:, t0:t1], mv[:, t0:t1, 1], LNEPS, None, ALU.add).then_inc(s["var_ok"], 1)
                made["std_ok"] += 1
                dve.wait_ge(s["std_ok"], made["std_ok"])
                done(v.reciprocal(rstd[:, t0:t1], std[:, t0:t1]))
                for t in range(t0, t1):
                    v.tensor_scalar(dst[:, t, :], h[:, t, :], mv[:, t, 0:1], rstd[:, t:t + 1],
                                    ALU.subtract, ALU.mult).then_inc(s[ok], 1)

            def qkv_out(t):
                R = rows(t)
                dve.wait_ge(s["qkv_mm"], t + 1)
                done(v.tensor_tensor(y[0:R, t, :].rearrange("p (a c) -> p a c", a=2),
                                     bank(2 + 2 * (t % 3), 2).rearrange("p (a c) -> p a c", a=2)[0:R, :, 0:QKV // 2],
                                     bqkv_b[0:R].rearrange("p (a c) -> p a c", a=2), ALU.add), "y_ok")
                v.tensor_reduce(ymax[:, t:t + 1], y[:, t, :], AX.X, ALU.max).then_inc(s["dve_order"], 1)
                v.tensor_reduce(ymin[:, t:t + 1], y[:, t, :], AX.X, ALU.min).then_inc(s["dve_order"], 1)
                made["dve_order"] += 2

            dve.wait_ge(s["txt_in"], 16 * len(text))
            dve.wait_ge(s["pool_zero"], 7)
            dve.wait_ge(s["bias_in"], 64)
            dve.wait_ge(s["h_in0"], 16 * sum(im[0] == 0 for im in image))
            layer_norm(xn, "xn_ok", *LNT[0])
            dve.wait_ge(s["h_in1"], 16 * sum(im[0] == 1 for im in image))
            layer_norm(xn, "xn_ok", *LNT[1])
            dve.wait_ge(s["h_in2"], 16 * sum(im[0] == 2 for im in image))
            layer_norm(xn, "xn_ok", *LNT[2])
            for t in range(T):
                qkv_out(t)
            dve.wait_ge(s["dve_order"], made["dve_order"])

            def quantiser(at, mx, mn, kappa=None, kappa255=None):
                dve.wait_ge(s["dve_order"], made["dve_order"])
                done(v.tensor_reduce(gcol[:, 0:1], mx, AX.X, ALU.max))
                done(v.tensor_reduce(gcol[:, 1:2], mn, AX.X, ALU.min, negate=True), "g_col")
                made["g_T"] += 1
                dve.wait_ge(s["g_T"], made["g_T"])
                done(v.tensor_reduce(gred, bank(7)[:, 0:2 * P].rearrange("p (a n) -> p a n", a=2), AX.X, ALU.max))
                scale, ratio, top, inverse = (sc[:, at + k:at + k + 1] for k in range(4))
                done(v.tensor_scalar(gred, gred, 0.0, None, ALU.max))
                done(v.tensor_tensor(scale, gred[:, 0:1], gred[:, 1:2], ALU.add))
                done(v.tensor_scalar(scale, scale, 1.0 / 255.0 if kappa is None else kappa255, EPS, ALU.mult, ALU.max))
                if kappa is None:
                    done(v.reciprocal(ratio, scale))
                else:
                    done(v.reciprocal(inverse, scale))
                    done(v.tensor_scalar(ratio, inverse, kappa, None, ALU.mult))
                done(v.scalar_tensor_tensor(top, gred[:, 1:2], -1.0, ratio, ALU.mult, ALU.mult))
                done(v.tensor_scalar(top, top, MAGIC, 255.0 - MAGIC, ALU.add, ALU.add))

            quantiser(0, ymax, ymin)
            for t0, t1 in ((0, TQ), (TQ, T)):
                done(v.tensor_scalar(yint[:, t0:t1, :], y[:, t0:t1, :], sc[:, 1:2], sc[:, 2:3], ALU.mult, ALU.min), "yint_ok")
                v.tensor_copy(qk2.rearrange("p t k (j a d) -> p t (k j) a d", j=HQ, a=2)[:, t0:t1, :, 0, :],
                              yint[:, t0:t1, 0:2 * D].rearrange("p t (x d) -> p t x d", d=HD)).then_inc(s["copy_a"], 1)
            for t in range(T):
                R = rows(t)
                dve.wait_ge(s["qT_mm"], t + 1)
                v.tensor_tensor(qT[:, :, P * t:P * t + R],
                                bankb(t % 2)[:, 0:HG * P].rearrange("p (g n) -> p g n", g=HG)[:, :, 0:R],
                                parity[:, P * t:P * t + R].unsqueeze(1).to_broadcast([P, HG, R]), ALU.mult).then_inc(s["q_ok"], 1)
                if t == TQ - 1 or t == T - 1:
                    b0, b1 = (0, PB) if t == TQ - 1 else (PB, B - 1)
                    dve.wait_ge(s["k_ok"], t + 1)
                    v.tensor_tensor(kpair[:, :, b0 * N:b1 * N], kT[:, :, b0 * N:b1 * N], kT[:, :, (b0 + 1) * N:(b1 + 1) * N],
                                    ALU.add).then_inc(s["pair_ok"], 1)
            sy = sc[:, 0:1]
            done(v.tensor_scalar(sc[:, 8:9], sy, sy, 0.25, ALU.mult, ALU.mult))
            done(v.tensor_scalar(sc[:, 9:10], sc[:, 8:9], 1.0 / 255.0, None, ALU.mult))
            done(v.tensor_scalar(sc[:, 10:11], sy, 1.0 / 255.0, None, ALU.mult))
            for t in range(T):
                dve.wait_ge(s["s0_mm"], t + 1)
                view = scores_view(t, 4 * ((t + 1) % 2))
                full = view.rearrange("p a (g n) -> p a g n", g=HG) if t < T - 1 else view.rearrange("p (g n) -> p g n", g=HG)
                mx = rmax[:, H * t:H * t + units(t)]
                v.tensor_reduce(mx.rearrange("p (a g) -> p a g", a=4) if t < T - 1 else mx, full, AX.X, ALU.max)
                v.tensor_reduce(ymin[:, t:t + 1], view, AX.XY if t < T - 1 else AX.X, ALU.min).then_inc(s["s0_read"], 1)
            dve.wait_ge(s["s0_read"], T)
            quantiser(4, rmax, ymin, sc[:, 8:9], sc[:, 9:10])
            dve.wait_ge(s["v_zero"], 2)
            done(v.tensor_scalar(nm, rmax, sc[:, 5:6], MAGIC, ALU.mult, ALU.add))
            done(v.tensor_scalar(nm, nm, MAGIC, sc[:, 6:7], ALU.subtract, ALU.min))
            done(v.reciprocal(sc[:, 29:30], sc[:, 5:6]))
            done(v.tensor_scalar(nb, nm, sc[:, 29:30], -1.0, ALU.mult, ALU.mult))
            part = [nb_parts.rearrange("p t (j c) -> p t j c", j=HQ)[:, :, :, k:k + 7:3] for k in range(3)]
            def cube(x):
                return x.rearrange("p (t j g) -> p t j g", j=HQ, g=HG)

            done(v.tensor_copy(part[0], cube(nb)))
            done(v.tensor_tensor(cube(nb2), cube(nb), part[0], ALU.subtract))
            done(v.tensor_copy(part[1], cube(nb2)))
            done(v.tensor_tensor(cube(nb3), cube(nb2), part[1], ALU.subtract))
            done(v.tensor_copy(part[2], cube(nb3)), "nb_ok")
            rs = sc[:, 7:8]
            C0 = 0.35815147
            v.tensor_scalar(sc[:, 12:13], rs, -0.6931, None, ALU.mult)
            v.tensor_scalar(sc[:, 13:14], rs, 0.96963238 / C0, None, ALU.mult)
            done(v.tensor_scalar(sc[:, 14:15], rs, rs, 1.0 / C0, ALU.mult, ALU.mult))
            done(v.tensor_scalar(sc[:, 15:18], sc[:, 12:15], MAGIC, -MAGIC, ALU.add, ALU.add))
            done(v.tensor_tensor(sc[:, 30:33], sc[:, 15:18], sc[:, 12:15], ALU.is_gt))
            done(v.tensor_tensor(sc[:, 15:18], sc[:, 15:18], sc[:, 30:33], ALU.subtract))
            done(v.tensor_scalar(sc[:, 24:25], sc[:, 15:16], -30.0, 256.0, ALU.mult, ALU.min), "k_at")
            v.tensor_scalar(sc[:, 27:28], sc[:, 16:17], 0.5, None, ALU.mult).then_inc(s["dve_order"], 1)
            done(v.tensor_scalar(sc[:, 21:22], sc[:, 15:16], -1.0, None, ALU.mult))
            made["dve_order"] += 1
            dve.wait_ge(s["dve_order"], made["dve_order"])
            v.tensor_scalar(sc[:, 22:23], sc[:, 24:25], 0.5, None, ALU.add).then_inc(s["dve_order"], 1)
            made["dve_order"] += 1
            done(v.reciprocal(sc[:, 20:21], sc[:, 21:22]))
            done(v.tensor_scalar(sc[:, 23:24], sc[:, 22:23], sc[:, 20:21], -0.5, ALU.mult, ALU.add))
            v.tensor_scalar(sc[:, 19:20], sc[:, 20:21], -1.0, None, ALU.mult).then_inc(s["dve_order"], 1)
            made["dve_order"] += 1
            done(v.tensor_tensor(sc[:, 26:27], sc[:, 27:28], sc[:, 24:25], ALU.subtract), "half_b")
            done(v.tensor_scalar(sc[:, 28:29], sc[:, 27:28], sc[:, 27:28], -1.0, ALU.mult, ALU.mult))
            done(v.tensor_tensor(sc[:, 28:29], sc[:, 28:29], sc[:, 17:18], ALU.add))
            dve.wait_ge(s["nbT_mm"], 1)
            done(v.memset(obuf[:, T - 1, :], 0.0), "nb_free")

            def quotient(t):
                k, n = t % 2, units(t) * N
                dve.wait_ge(s["m_ok"], t + 1)
                if t >= 4:
                    dve.wait_ge(s["pT_mm"], t - 3)
                v.tensor_scalar(bufs["q", k][:, 0:n], bufs["m", k][:, 0:n], sc[:, 19:20], sc[:, 23:24],
                                ALU.mult, ALU.add).then_inc(s["q_done"], 1)

            def times(t):
                k, n = t % 2, units(t) * N
                q = bufs["q", k][:, 0:n]
                dve.wait_ge(s["q_done"], t + 1)
                if t >= 2:
                    dve.wait_ge(s["w_ok"], t - 1)
                v.tensor_scalar(bufs["r", k][:, 0:n], q, sc[:, 21:22], None, ALU.mult).then_inc(s["qx_done"], 1)
                v.tensor_scalar(bufs["pw", k][:, 0:n], q, -128.0, 127.0 * 128.0, ALU.mult, ALU.add).then_inc(s["pw_ok"], 1)

            def rest(t):
                k, n = t % 2, units(t) * N
                dve.wait_ge(s["qx_done"], t + 1)
                r = bufs["r", k][:, 0:n]
                v.tensor_tensor(r, r, bufs["m", k][:, 0:n], ALU.add).then_inc(s["r_ok"], 1)

            def exps(t, us):
                k = t % 2
                if us[0] == 0:
                    dve.wait_ge(s["w_ok"], t + 1)
                    dve.wait_ge(s["pw_ok"], t + 1)
                for u in us:
                    if u < units(t):
                        ks = slice(N * u, N * (u + 1))
                        last = v.scalar_tensor_tensor(bufs["e", k][:, ks], bufs["w", k][:, ks], sc[:, 28:29],
                                                      bufs["pw", k].bitcast(bf16)[:, ks], ALU.add, ALU.mult,
                                                      accum_out=S[:, k, u:u + 1])
                        if u == units(t) - 1:
                            last.then_inc(s["e_ok"], 1)

            def ratios(t):
                k, u = t % 2, units(t)
                dve.wait_ge(s["inv_ok"], t + 1)
                v.tensor_tensor(bufs["x", k][:, 0:u * N].rearrange("p (u n) -> p u n", n=N),
                                bufs["e", k][:, 0:u * N].rearrange("p (u n) -> p u n", n=N),
                                S[:, k, 0:u].unsqueeze(2).to_broadcast([P, u, N]), ALU.mult).then_inc(s["x_done"], 1)

            def powers(t):
                x = bufs["x", t % 2][:, 0:units(t) * N]
                dve.wait_ge(s["x_done"], t + 1)
                v.tensor_scalar(x.bitcast(bf16), x, RSCALE, None, ALU.mult).then_inc(s["pow_done"], 1)

            def probs(t):
                k, u = t % 2, units(t)
                dve.wait_ge(s["pow_done"], t + 1)
                xi = bufs["x", k][:, 0:u * N].bitcast(i16).rearrange("p (u n) -> p u n", n=N)
                p = bufs["q", k]
                for dst, ks in ((p[:, 0:P * u], slice(0, P)), (p[:, P * u:N * u], slice(P, N))):
                    v.tensor_scalar(dst.rearrange("p (u n) -> p u n", u=u), xi[:, :, ks], 0x7F80, 0x7F80,
                                    ALU.bitwise_xor, ALU.bitwise_and).then_inc(s["p_ok"], 1)

            def second_of_out(t):
                R = rows(t)
                dve.wait_ge(s["o_first"], t + 1)
                if batches(t) == 2:
                    v.scalar_tensor_tensor(obuf[0:R, t, :], bank(6 + t % 2)[0:R, D:2 * D], batch_sel[0:R, t, 1:2],
                                           obuf[0:R, t, :], ALU.mult, ALU.add).then_inc(s["o_ok"], 1)
                else:
                    v.engine_nop().then_inc(s["o_ok"], 1)

            def range_of(part, col, ok, n):
                dve.wait_ge(s[ok], n)
                v.tensor_reduce(ymax[:, col:col + 1], part, AX.XY, ALU.max).then_inc(s["dve_order"], 1)
                v.tensor_reduce(ymin[:, col:col + 1], part, AX.XY, ALU.min).then_inc(s["dve_order"], 1)
                made["dve_order"] += 2

            for i in range(T + 5):
                e = i - 1 if 1 <= i <= T else None
                x = i - 2 if 2 <= i <= T + 1 else None
                if i < T:
                    quotient(i)
                if e is not None:
                    exps(e, range(0, 4))
                if i < T:
                    times(i)
                if e is not None:
                    exps(e, range(4, 8))
                if i < T:
                    rest(i)
                if x is not None:
                    ratios(x)
                if e is not None:
                    exps(e, range(8, 12))
                if x is not None:
                    powers(x)
                if i >= 5:
                    second_of_out(i - 5)
                if i == T + 2:
                    range_of(obuf[:, 0:T - 2, :], 0, "o_ok", T - 2)
                if i == T + 4:
                    range_of(obuf[:, T - 2:, :], 1, "o_ok", T)
                if x is not None:
                    probs(x)
            quantiser(36, ymax[:, 0:2], ymin[:, 0:2], sy, sc[:, 10:11])
            done(v.tensor_scalar(oint, obuf, sc[:, 37:38], sc[:, 38:39], ALU.mult, ALU.min))
            done(v.tensor_copy(obf, oint), "obf_ok")
            done(v.tensor_scalar(proj_scale[:, :], proj_scale[:, :], sc[:, 36:37], None, ALU.mult))
            for t in range(T):
                R = rows(t)
                dve.wait_ge(s["pr_mm"], t + 1)
                v.tensor_tensor(obuf[0:R, t, :], bank(2 + t % 4)[0:R, 0:D], proj_scale[0:R, :], ALU.mult).then_inc(s["y2_ok"], 1)
                if t in Y2T:
                    n = Y2T.index(t)
                    range_of(obuf[:, YT[n]:YT[n + 1], :], n, "y2_sum", YT[n + 1])
            range_of(obuf[:, YT[-1]:, :], len(Y2T), "y2_sum", T)
            quantiser(44, ymax[:, 0:len(YT)], ymin[:, 0:len(YT)])
            dve.wait_ge(s["oT_mm"], T)
            done(v.tensor_scalar(y2int, obuf, sc[:, 45:46], sc[:, 46:47], ALU.mult, ALU.min))
            for t0, t1 in LNT:
                done(v.scalar_tensor_tensor(h[:, t0:t1, :], y2int[:, t0:t1, :], sc[:, 44:45], h[:, t0:t1, :], ALU.mult, ALU.add))
                layer_norm(xf, "xf_ok", t0, t1)
            v.tensor_copy(xs[:, :, 2 * D], token_no).then_inc(s["xf_ok"], 1)
            dve.wait_ge(s["lg_mm"], 1)
            L = [lg[:, k, :, :] for k in range(6)]

            def wide(col):
                return rt[:, col, :].unsqueeze(2).to_broadcast([P, T, EXP])

            for t0, t1, R in ((0, T - 1, P), (T - 1, T, LAST)):
                done(v.tensor_tensor(L[0][0:R, t0:t1], bank(2)[0:R, EXP * t0:EXP * t1].rearrange("p (t e) -> p t e", e=EXP),
                                     swb_b[0:R, :].unsqueeze(1).to_broadcast([R, t1 - t0, EXP]), ALU.add))
            done(v.tensor_reduce(rt[:, 0, :], L[0], AX.X, ALU.max))
            done(v.tensor_tensor(L[2], L[0], wide(0), ALU.subtract), "lg_ok")
            done(v.tensor_tensor(L[1], L[0], wide(0), ALU.is_equal))
            done(v.scalar_tensor_tensor(L[4], L[1], -float(EXP), expert_no, ALU.mult, ALU.add))
            done(v.tensor_reduce(rt[:, 3, :], L[4], AX.X, ALU.min))
            for t0, t1, R in ((0, T - 1, P), (T - 1, T, LAST)):
                done(v.tensor_tensor(onehot[0:R, t0:t1, :], L[4][0:R, t0:t1],
                                     rt[0:R, 3, t0:t1].unsqueeze(2).to_broadcast([R, t1 - t0, EXP]), ALU.is_equal))
            dve.wait_ge(s["ex_ok"], 1)
            done(v.tensor_reduce(rt[:, 1, :], L[3], AX.X, ALU.add))
            done(v.reciprocal(rt[:, 2, :], rt[:, 1, :]), "p_col")
            v.tensor_copy(xs[:, :, 2 * D + 1], rt[:, 2, :]).then_inc(s["xf_ok"], 1)
            dve.wait_ge(s["prow_ok"], 1)
            for t in range(T):
                R, lo, hi = rows(t), P * t, P * t + rows(t)
                v.scalar_tensor_tensor(tie[0:R, lo:hi], prow[0:R, lo:hi], rt[0:R, 2, t:t + 1], lower[0:R, 0:R],
                                       ALU.is_equal, ALU.mult).then_inc(s["tie_ok"], 1)

            def slots_of(t0, t1):
                for a, b, R in ((t0, min(t1, T - 1), P), (T - 1, T, LAST)):
                    if a < b <= t1:
                        done(v.tensor_tensor(L[5][0:R, a:b], bank(6 + (t0 > 0))[0:R, EXP * a:EXP * b].rearrange("p (t e) -> p t e", e=EXP),
                                             onehot[0:R, a:b, :], ALU.mult))
                r = rt[:, :, t0:t1]
                done(v.tensor_reduce(r[:, 4, :], L[5][:, t0:t1], AX.X, ALU.add))
                done(v.tensor_scalar(r[:, 5, :], r[:, 4, :], float(CAP), 1e6, ALU.is_ge, ALU.mult))
                done(v.tensor_tensor(r[:, 5, :], r[:, 5, :], r[:, 4, :], ALU.add))
                done(v.tensor_tensor(slot[:, t0:t1], r[:, 5, :], r[:, 6, :], ALU.add), "slot_ok")

            done(v.tensor_scalar(rt[:, 6, :], rt[:, 3, :], float(EXP), float(SLOTS), ALU.add, ALU.mult))
            n = 0
            for half in range(2):
                below = {}
                for kind, t, lo, hi in compares(half):
                    R, n = rows(t), n + 1
                    if kind == "tie":
                        dve.wait_ge(s["tie_ok"], t + 1)
                        dve.wait_ge(s["cmp_ok"], below[t])
                        ins = v.tensor_tensor(G[0:R, t, lo:hi], G[0:R, t, lo:hi], tie[0:R, lo:hi], ALU.add)
                    else:
                        if kind == "lt":
                            below[t] = n
                        ins = v.tensor_scalar(G[0:R, t, lo:hi], prow[0:R, lo:hi], rt[0:R, 2, t:t + 1], None,
                                              ALU.is_lt if kind == "lt" else ALU.is_le)
                    ins.then_inc(s["cmp_ok"], 1)
                dve.wait_ge(s["cnt_mm"], half + 1)
                slots_of((0, TH)[half], (TH, T)[half])
            done(v.tensor_scalar(rt[:, 7, :], rt[:, 4, :], float(CAP), None, ALU.is_ge))
            done(v.tensor_tensor(rt[:, 7, :], rt[:, 7, :], rt[:, 2, :], ALU.mult))
            for t in range(T):
                R = rows(t)
                v.scalar_tensor_tensor(obuf[0:R, t, :], xf[0:R, t, :], rt[0:R, 7, t:t + 1], h[0:R, t, :],
                                       ALU.mult, ALU.add).then_inc(s["out_ok"], 1)

            def keep_expert(e):
                dve.wait_ge(s["xeT_mm"], e + 1)
                if e >= 2:
                    dve.wait_ge(s["h_mm"], 3 * (e - 1))
                v.tensor_copy(xeT[0:DC, e % 2], bank(0)[0:DC, 0:2 * SLOTS].rearrange("p (c n) -> p c n", c=2)
                              ).then_inc(s["xeT_ok"], 1)

            keep_expert(0)
            dve.wait_ge(s["xe_in"], 16 * (EXP - 1))
            v.tensor_copy(whose, xe[0:HALF, :, :, 2 * D]).then_inc(s["whose_ok"], 1)
            keep_expert(1)
            dve.wait_ge(s["ffn_in2"], 48)
            for e in range(EXP):
                if e + 2 < EXP:
                    keep_expert(e + 2)
                dve.wait_ge(s["oe_mm"], e + 1)
                if e >= 2:
                    dve.wait_ge(s[("oe_out0", "oe_out1")[e % 2]], 32 * (e // 2))
                o = oe[0:HALF, e % 2]
                done(v.tensor_tensor(o, bank(1)[0:HALF, 0:2 * D].rearrange("p (a d) -> p a d", a=2),
                                     b2_s[0:HALF, e, :].unsqueeze(1).to_broadcast([HALF, 2, D]), ALU.add), "oe_read")
                for a in range(2):
                    v.scalar_tensor_tensor(o[:, a, :], o[:, a, :], xe[0:HALF, e, a, 2 * D + 1:2 * D + 2], xe[0:HALF, e, a, D:2 * D],
                                           ALU.mult, ALU.add).then_inc(s["oe_ok"], 1)


def constants():
    import numpy as np
    c = np.zeros((P, C_END), np.float32)
    p = np.arange(P)
    c[p, C_ID + p] = 1.0
    tok = np.arange(TOK)
    c[:, C_PAR:C_PAR + TOK] = ((p[:, None] // HD) % 2 == (tok[None, :] // N) % 2)
    for j in range(HQ):
        for g in range(HG):
            for k in range(3):
                c[32 * j + 3 * g + k, C_SEL + N * g:C_SEL + N * (g + 1)] = 1.0
    c[:, C_LOW:C_LOW + P] = p[:, None] < p[None, :]
    for t in range(T):
        b = np.minimum((P * t + p) // N, B - 1)
        c[:, C_BSEL + 2 * t] = (b == first_batch(t)) * PSCALE
        c[:, C_BSEL + 2 * t + 1] = (b != first_batch(t)) * PSCALE
    c[:, C_EXP:C_TOK] = np.tile(np.arange(EXP), T)[None, :]
    c[:, C_TOK:] = P * np.arange(T)[None, :] + p[:, None]
    return c


def kernel(x, txt, L0_tok_W_lin, L0_tok_b_lin, L0_attn_w_qkv, L0_attn_b_qkv, L0_attn_w_proj, L0_attn_b_proj,
           L0_ffn_switch_w, L0_ffn_switch_b, L0_ffn_w1, L0_ffn_b1, L0_ffn_w2, L0_ffn_b2):
    import numpy as np
    import concourse.bacc as bacc
    from concourse.bass_utils import run_bass_kernel_spmd

    hp = IMG // PATCH
    a = {}
    xs = np.asarray(x).reshape(B, CH, hp, PATCH, hp, PATCH).transpose(3, 5, 1, 0, 2, 4)
    a["x"] = xs.reshape(KC, P, B * NIMG).transpose(1, 0, 2)
    a["wlin"] = np.asarray(L0_tok_W_lin).T.reshape(KC, P, D).transpose(1, 0, 2)
    a["blin"] = np.asarray(L0_tok_b_lin)
    a["txt"] = np.asarray(txt)
    order = np.arange(D).reshape(HG, HQ, HD).transpose(1, 0, 2).reshape(-1)
    wq = np.asarray(L0_attn_w_qkv)
    bq = np.asarray(L0_attn_b_qkv)
    rows_ = np.concatenate([np.arange(2 * D), 2 * D + order])
    wq = np.concatenate([wq[rows_], np.asarray(L0_attn_w_proj)[:, order]], 0)
    a["wqkv"] = wq.reshape(8, DC, D).transpose(1, 0, 2)
    a["bqkv"] = bq[rows_]
    a["bproj"] = np.asarray(L0_attn_b_proj)
    a["sww"] = np.asarray(L0_ffn_switch_w).reshape(2, DC, EXP).transpose(1, 0, 2)
    a["swb"] = np.asarray(L0_ffn_switch_b)
    a["w1"] = np.asarray(L0_ffn_w1).reshape(EXP, 2, DC, F).transpose(2, 0, 1, 3)
    a["b1"] = np.asarray(L0_ffn_b1).reshape(EXP, FC, P).transpose(2, 0, 1)
    a["w2"] = np.asarray(L0_ffn_w2).reshape(EXP, FC, P, D).transpose(2, 0, 1, 3)
    a["b2"] = np.asarray(L0_ffn_b2)
    a["consts"] = constants()
    a = {k: np.ascontiguousarray(v) for k, v in a.items()}
    nc = bacc.Bacc("TRN2", target_bir_lowering=False, num_devices=1)
    ins = {k: nc.dram_tensor(k + "_dram", v.shape, mybir.dt.from_np(v.dtype), kind="ExternalInput").ap() for k, v in a.items()}
    out = nc.dram_tensor("out_dram", (TOK, D), mybir.dt.float32, kind="ExternalOutput").ap()
    fusion_kernel(nc, out=out, **ins)
    r = run_bass_kernel_spmd(nc, [{k + "_dram": v for k, v in a.items()}], core_ids=[0])
    return r.results[0]["out_dram"].reshape(B, N, D)
```

```python
import concourse.bass as bass
from concourse import mybir
from contextlib import ExitStack

B, CH, IMG, PATCH = 8, 3, 96, 16
D = 192
NIMG = (IMG // PATCH) ** 2
NTXT = 128
N = NIMG + NTXT
TOK = B * N
P = 128
T = -(-TOK // P)
LAST = TOK - (T - 1) * P
PD = CH * PATCH * PATCH
KC = PD // P
H, HD = 12, 16
HG, HQ = 3, 4
DC = D // 2
QKV = 3 * D
EXP, F = 8, 768
CAP = int(1.25 * TOK / EXP)
SLOTS = CAP + CAP % 2
SD = 2 * D + 2
NOBODY = 1e6
HALF = SLOTS // 2
FC = F // P
KR = N - P
EB = 3
ET = -(-B // EB)
EPS = 1.1920928955078125e-07
LNEPS = 1e-5
MAGIC = 1.5 * 2.0 ** 23
PSCALE = 2.0 ** 111
RSCALE = (4.0 / 3.0) * (1.0 - 2.0 ** -9 * (1.0 - 2.0 ** -9)) * 2.0 ** 112


LNT = ((0, EB * N // P), (EB * N // P, 2 * EB * N // P), (2 * EB * N // P, T))
assert ET == 3
LNT2 = ((0, 4), (4, 8), (8, T))
FEW = 2
OT = (0, 1, 6)
NB = -(-TOK // 512)
UA = HG
WARM = (20, 24, 36)
TH = T // 2 + 2
TQ = T // 2 + 1
YT = (0, 2, 4, 6, 8)
Y2T = tuple(t + 1 for t in YT[1:])


def rows(t):
    return P if t < T - 1 else LAST


def first_batch(t):
    return P * t // N


def batches(t):
    return (P * t + rows(t) - 1) // N - first_batch(t) + 1


def pieces(b, lo, hi):
    out, n = [], lo
    while n < hi:
        at = N * b + n
        k = min(hi - n, P - at % P)
        out.append((at // P, at % P, n, k))
        n += k
    return out


C_ID, C_PAR, C_SEL, C_LOW, C_BSEL, C_EXP = 0, P, P + TOK, P + TOK + HG * N, 2 * P + TOK + HG * N, 2 * P + TOK + HG * N + 2 * T
C_TOK = C_EXP + T * EXP
C_END = C_TOK + T


def fusion_kernel(nc, x, wlin, blin, txt, wqkv, bqkv, bproj, sww, swb, w1, b1, w2, b2, consts, out):
    f32, bf16, i16, u16, u32 = (mybir.dt.float32, mybir.dt.bfloat16, mybir.dt.int16, mybir.dt.uint16,
                                mybir.dt.uint32)
    ALU = mybir.AluOpType
    ACT = mybir.ActivationFunctionType
    AX = mybir.AxisListType

    ctx = ExitStack()
    with ctx:
        def sb(name, shape, dt=f32):
            return ctx.enter_context(nc.sbuf_tensor(name, shape, dt))[:]

        def sem(name):
            return ctx.enter_context(nc.semaphore(name))

        def dram(name, shape, dt):
            return nc.dram_tensor(name, shape, dt, kind="Internal").ap()

        v_dram = dram("v_dram", (TOK, D), bf16)
        slots = dram("slots", (EXP * SLOTS, SD), f32)

        UW = H * N
        HE = 2
        cst = sb("cst", [P, C_END])
        ident = cst[:, C_ID:C_ID + P]
        parity = cst[:, C_PAR:C_PAR + TOK]
        lower = cst[:, C_LOW:C_LOW + P]
        batch_sel = cst[:, C_BSEL:C_BSEL + 2 * T].rearrange("p (t b) -> p t b", b=2)
        expert_no = cst[:, C_EXP:C_EXP + T * EXP].rearrange("p (t e) -> p t e", e=EXP)
        token_no = cst[:, C_TOK:C_END]
        ident_b = sb("ident_b", [P, P], bf16)
        sel_b = sb("sel_b", [P, HG * N], bf16)
        xs = sb("xs", [P, T, SD])
        xf, h = xs[:, :, 0:D], xs[:, :, D:2 * D]
        xT = sb("xT", [DC, 2, TOK])
        wprojT = sb("wprojT", [DC, 2, D], bf16)
        proj_scale = sb("proj_scale", [P, D])
        bproj_b = sb("bproj_b", [P, D])
        swb_b = sb("swb_b", [P, EXP])
        sww_s = sb("sww_s", [DC, 2, EXP])
        probsT = sb("probsT", [P, 16, P], bf16)
        b1_s = sb("b1_s", [P, EXP, FC])
        stat = sb("stat", [P, T, 6])
        mv = sb("mv", [P, T, 2])
        var = sb("var", [P, T])
        std = sb("std", [P, T])
        rstd = sb("rstd", [P, T])
        ymax = sb("ymax", [P, T])
        ymin = sb("ymin", [P, T])
        rmax = sb("rmax", [P, T * H])
        gcol = sb("gcol", [P, 2])
        gred = sb("gred", [P, 2])
        sc = sb("sc", [P, 64])
        S = sb("S", [P, 2, H])
        lnS = sb("lnS", [P, 2, UA])
        lg = sb("lg", [P, 6, T, EXP])
        onehot = sb("onehot", [P, T, EXP], bf16)
        rt = sb("rt", [P, 8, T])
        slot = sb("slot", [P, T], u32)
        whose = sb("whose", [HALF, EXP, 2], u32)
        empty = sb("empty", [HALF, SD])
        ones = sb("ones", [1, P])
        zeros = sb("zeros", [P, P], bf16)
        w1_a = sb("w1_a", [DC, HE, 2, F])
        w2_a = sb("w2_a", [P, HE, FC, D])

        def cutter(name, words):
            whole, at = sb(name, [P, words]), [0]

            def cut(n, dt=f32):
                if n is None:
                    at[0] = 0
                    return None
                assert at[0] + n <= words, (name, at, n)
                v = whole[:, at[0]:at[0] + n]
                at[0] += n
                return v if dt == f32 else v.bitcast(dt)
            return cut

        cut = cutter("attn", 3 * HG * TOK // 2 + 2 * B * D // 2 + T * P // 2)
        qT = cut(HG * TOK // 2, bf16).rearrange("p (g n) -> p g n", g=HG)
        kT = cut(HG * TOK // 2, bf16).rearrange("p (g n) -> p g n", g=HG)
        vmain = cut(B * D // 2, bf16).rearrange("p (b u d) -> p b u d", b=B, u=H)
        vrest = cut(B * D // 2, bf16).rearrange("p (b j c) -> p b j c", b=B, j=HQ)
        nbT = cut(T * P // 2, bf16)
        cut(None)
        G = cut(T * TOK // 2, bf16).rearrange("p (t n) -> p t n", n=TOK)
        cut(None)
        xeT = cut(2 * 2 * SLOTS).rearrange("p (k c n) -> p k c n", k=2, c=2)
        hT = cut(2 * FC * SLOTS).rearrange("p (k f n) -> p k f n", k=2, f=FC)
        oe = cut(2 * 2 * D).rearrange("p (k a d) -> p k a d", k=2, a=2)

        NB2 = EXP - HE
        cut = cutter("region", 18432)
        xn = cut(T * D).rearrange("p (t d) -> p t d", d=D)
        y = cut(T * QKV).rearrange("p (t c) -> p t c", c=QKV)
        yint = cut(T * QKV // 2, i16).rearrange("p (t c) -> p t c", c=QKV)
        emb_w = cut(KC * D).rearrange("p (c e) -> p c e", e=D)
        blin_b = cut(D)
        emb = cut(ET * D).rearrange("p (t e) -> p t e", e=D)
        wall = cut(8 * D).rearrange("p (g i) -> p g i", g=8)[0:DC]
        wdeq = cut(8 * D).rearrange("p (g i) -> p g i", g=8)[0:DC]
        bqkv_b = cut(QKV)
        wqkvT = cut(2 * QKV).rearrange("p (c o) -> p c o", c=2)[0:DC]
        qk2 = y.rearrange("p t c -> p (t c)")[:, 0:T * 2 * D].bitcast(bf16).rearrange("p (t k c) -> p t k c", t=T, k=2 * HG)
        cut(None)
        bufs = {}
        for k in range(2):
            for n, words, dt in (("m", UW // 2, i16), ("q", UW // 2, i16), ("r", UW // 2, i16), ("pw", UW // 2, i16),
                                 ("x", UW // 2, u16), ("w", UW, f32), ("e", UW, f32)):
                bufs[n, k] = cut(words, dt)
        cut(None)
        w1_b = cut(NB2 * 2 * F).rearrange("p (e c f) -> p e c f", e=NB2, c=2)
        b2_s = cut(EXP * D).rearrange("p (e d) -> p e d", e=EXP)
        w2_b = cut(NB2 * FC * D).rearrange("p (e c d) -> p e c d", e=NB2, c=FC)
        cut = cutter("share", EXP * 2 * SD)
        patches = cut(KC * B * NIMG).rearrange("p (c n) -> p c n", c=KC)
        cut(None)
        oT = cut(TOK, bf16).rearrange("p (c n) -> p c n", c=2)[0:DC]
        y2int, oint = (cut(T * D // 2, i16).rearrange("p (t d) -> p t d", d=D) for _ in range(2))
        obf = cut(T * D // 2, bf16).rearrange("p (t d) -> p t d", d=D)
        cut(None)
        prow = cut(TOK)
        cut(T * D // 2)
        lgT = cut(TOK)[0:EXP]
        cut(None)
        xe = cut(EXP * 2 * SD).rearrange("p (e a d) -> p e a d", e=EXP, a=2)
        cut = cutter("obuf", T * D)
        obuf_w = cut(T * D)
        obuf = obuf_w.rearrange("p (t d) -> p t d", d=D)
        cut(None)
        nm = cut(T * H)
        nb = cut(T * H)
        nb2 = cut(T * H)
        nb3 = cut(T * H)
        parts = [cut(T * H // 2, bf16) for _ in range(3)]
        nb_parts = cut(T * P // 2, bf16).rearrange("p (t c) -> p t c", c=P)
        tie = probsT.rearrange("p u n -> p (u n)")[:, 0:TOK]
        wst = sb("wst", [DC, 8, 8])
        wproj_n = probsT.rearrange("p u n -> p (u n)")[0:DC, 0:2 * D].rearrange("p (a d) -> p a d", a=2)
        ps = ctx.enter_context(nc.psum_tensor("ps", [P, 8 * 512], f32))

        def bank(k, n=1):
            return ps[:, 512 * k:512 * (k + n)]

        def bankb(k, n=1):
            return ps[:, 512 * k:512 * (k + n)].bitcast(bf16)

        def w1_of(e):
            return w1_a[:, e] if e < HE else w1_b[0:DC, e - HE]

        def w2_of(e):
            return w2_a[:, e] if e < HE else w2_b[:, e - HE]

        names = ("wint_ok lgT_mm lgT_ok m0_read yint_ok v_int h_in0 h_in1 h_in2 xe_first oe_read cst_in emb_in "
                 "w_in bias_in txt_in ffn_in ffn_in2 zeroed v_out v_in v_zero xe_in oe_out0 oe_out1 scat "
                 "stored pool_zero emb_mm emb_sb var_ok std_ok xn_ok xnT_mm xT_ok wdeq_ok wproj_ok wT_mm wT_ok "
                 "qkv_mm y_ok g_col g_T copy_a copy_b qT_mm kT_mm q_ok k_ok s0_mm s0_read nb_ok nbT_mm nbT_ok "
                 "s_mm m_ok r_ok w_ok e_ok inv_ok p_ok pT_mm pT_ok o_mm o_ok obf_ok oT_mm oT_ok pr_mm y2_ok "
                 "xf_ok lg_mm lg_ok ex_ok p_col prow_mm prow_ok cmp_ok cnt_mm slot_ok xeT_mm xeT_ok h_mm h_ok "
                 "oe_mm oe_ok out_ok dve_order act_order cst_b pool_made q_done pw_ok y2_sum o_first nb_free "
                 "half_b k_at qx_done x_done pow_done tie_ok whose_ok").split()
        s = {n: sem(n) for n in names}

        block = ctx.enter_context(nc.Block())
        text = [(b, pc) for b in range(B) for pc in pieces(b, NIMG, N)]
        image = [(b // EB, NIMG * (b % EB) + pc[2], pc) for b in range(B) for pc in pieces(b, 0, NIMG)]

        def units(t):
            return H if t < T - 1 else HG

        @block.sync
        def _(sp):
            def load(dst, src, what):
                sp.dma_start(dst, src).then_inc(s[what], 16)

            load(patches, x, "emb_in")
            load(emb_w, wlin, "emb_in")
            load(blin_b[0:1], blin.partition_broadcast(1), "emb_in")
            load(cst[:, :], consts, "cst_in")
            load(bqkv_b, bqkv.partition_broadcast(P), "bias_in")
            load(bproj_b[:, :], bproj.partition_broadcast(P), "bias_in")
            load(swb_b[:, :], swb.partition_broadcast(P), "bias_in")
            load(sww_s[:, :, :], sww, "bias_in")
            sp.wait_ge(s["pool_zero"], 1)
            for b, (t, r, n, k) in text:
                load(h[r:r + k, t, :], txt[b, n - NIMG:n - NIMG + k, :], "txt_in")
            for j, n, (t, r, m, k) in image:
                sp.wait_ge(s["emb_sb"], j + 1)
                load(h[r:r + k, t, :], emb[n:n + k, j, :], ("h_in0", "h_in1", "h_in2")[j])
            sp.wait_ge(s["pool_zero"], 9)
            load(slots.rearrange("(p a) d -> p a d", p=HALF), empty.unsqueeze(1).to_broadcast([HALF, EXP * SLOTS // HALF, SD]), "zeroed")
            load(w1_a[:, :, :, :], w1[:, 0:HE], "ffn_in")
            load(w2_a[:, :, :, :], w2[:, 0:HE], "ffn_in")
            load(b1_s[:, :, :], b1, "ffn_in")
            sp.wait_ge(s["v_int"], 1)
            vint = yint.bitcast(bf16)
            load(v_dram[0:(T - 1) * P, :].rearrange("(t p) c -> p t c", p=P), vint[:, 0:T - 1, 2 * D:], "v_out")
            load(v_dram[(T - 1) * P:, :], vint[0:LAST, T - 1, 2 * D:], "v_out")
            sp.wait_ge(s["v_out"], 32)
            vb = v_dram.rearrange("(b n) c -> n b c", n=N)
            load(vmain.rearrange("p b u d -> p b (u d)"), vb[0:P], "v_in")
            sp.wait_ge(s["v_zero"], 2)
            for b in range(B):
                for g in range(HG):
                    load(vrest[KR * g:KR * (g + 1), b, :, HD * g:HD * (g + 1)],
                         vb[P:N, b, :].rearrange("n (j g d) -> n j g d", j=HQ, g=HG)[:, :, g, :], "v_in")
            sp.wait_ge(s["p_ok"], 2 * T)
            sp.wait_ge(s["inv_ok"], T)
            sp.wait_ge(s["pT_mm"], T)
            load(w1_b[0:DC], w1[:, HE:], "ffn_in2")
            load(w2_b, w2[:, HE:], "ffn_in2")
            load(b2_s, b2.partition_broadcast(P), "ffn_in2")
            for t in range(T):
                sp.wait_ge(s["out_ok"], t + 1)
                load(out[P * t:P * t + rows(t), :], obuf[0:rows(t), t, :], "stored")
            sp.wait_ge(s["scat"], 16 * T)
            for e in range(EXP):
                load(xe[0:HALF, e], slots[e * SLOTS:(e + 1) * SLOTS, :].rearrange("(a p) d -> p a d", a=2),
                     "xe_first" if e == 0 else "xe_in")

        @block.gpsimd
        def _(pool):
            pool.memset(h[:, T - 1, :], 0.0).then_inc(s["pool_zero"], 1)
            pool.memset(zeros, 0.0).then_inc(s["pool_zero"], 1)
            pool.memset(ones, 1.0).then_inc(s["pool_zero"], 1)
            pool.memset(y[:, T - 1, :], 0.0).then_inc(s["pool_zero"], 1)
            pool.memset(lg, 0.0).then_inc(s["pool_zero"], 1)
            pool.memset(onehot, 0.0).then_inc(s["pool_zero"], 1)
            pool.memset(rmax, 0.0).then_inc(s["pool_zero"], 1)
            pool.memset(ymax, 0.0).then_inc(s["pool_zero"], 1)
            pool.memset(empty, 0.0).then_inc(s["pool_made"], 1)
            pool.wait_ge(s["pool_made"], 1)
            pool.memset(empty[:, 2 * D:2 * D + 1], NOBODY).then_inc(s["pool_zero"], 1)
            pool.memset(vrest, 0.0).then_inc(s["v_zero"], 1)
            pool.memset(obuf_w, 0.0).then_inc(s["v_zero"], 1)
            for t in range(T):
                R = rows(t)
                pool.wait_ge(s["y2_ok"], t + 1)
                pool.tensor_tensor(obuf[0:R, t, :], obuf[0:R, t, :], bproj_b[0:R, :], ALU.add).then_inc(s["y2_sum"], 1)
            pool.wait_ge(s["zeroed"], 16)
            pool.wait_ge(s["xf_ok"], T + 2)
            for t in range(T):
                if t == 0 or t == TH:
                    pool.wait_ge(s["slot_ok"], 1 if t == 0 else 2)
                pool.indirect_dma_start(out=slots, out_offset=bass.IndirectOffsetOnAxis(ap=slot[0:rows(t), t:t + 1], axis=0),
                                        in_=xs[0:rows(t), t, :], in_offset=None, bounds_check=EXP * SLOTS - 1,
                                        oob_is_err=False).then_inc(s["scat"], 16)
            pool.wait_ge(s["stored"], 16 * T)
            pool.wait_ge(s["whose_ok"], 1)
            for e in range(EXP):
                pool.wait_ge(s["oe_ok"], 2 * (e + 1))
                for a in range(2):
                    pool.indirect_dma_start(out=out, out_offset=bass.IndirectOffsetOnAxis(ap=whose[0:HALF, e, a:a + 1], axis=0),
                                            in_=oe[0:HALF, e % 2, a, :], in_offset=None, bounds_check=TOK - 1,
                                            oob_is_err=False).then_inc(s[("oe_out0", "oe_out1")[e % 2]], 16)
            pool.wait_ge(s["oe_out0"], 16 * EXP)
            pool.wait_ge(s["oe_out1"], 16 * EXP)

        def compares(half):
            a, b = ((0, P * TH), (P * TH, TOK))[half]
            for t in range(T):
                end = P * t + rows(t)
                if end > a:
                    yield "lt", t, a, min(b, end)
                if end < b:
                    yield "le", t, max(a, end), b
                if t >= 1 and a <= P * (t - 1) < b:
                    yield "tie", t - 1, P * (t - 1), end - rows(t)
            if a <= P * (T - 1) < b:
                yield "tie", T - 1, P * (T - 1), TOK

        def scores_of(t):
            b, R = first_batch(t), rows(t)
            for j in range(HQ):
                for g in range(HG):
                    rws = slice(32 * j, 32 * j + 32)
                    keys = [kT[rws, g, N * c:N * (c + 1)] for c in range(b, b + batches(t))]
                    qs = qT[rws, g, P * t:P * t + R]
                    if t < T - 1:
                        yield j, g, slice(0, P), slice(N * g, N * (g + 1)), qs, keys
                    else:
                        yield 0, g, rws, slice(N * g, N * (g + 1)), qs, keys

        def scores_view(t, k):
            if t < T - 1:
                return bank(k, 4).rearrange("p (a c) -> p a c", a=4)[:, :, 0:HG * N]
            return bank(k)[:, 0:HG * N]

        @block.tensor
        def _(pe):
            mm = nc.tensor.matmul
            tr = nc.tensor.transpose

            def warm(n):
                for _ in range(n):
                    mm(bank(5), zeros, zeros.unsqueeze(1).to_broadcast([P, 4, P]), start=True, stop=True)

            pe.wait_ge(s["pool_zero"], 2)
            warm(WARM[0])
            pe.wait_ge(s["emb_in"], 48)
            for j in range(ET):
                n = min(EB, B - EB * j) * NIMG
                if j == 0:
                    pe.wait_ge(s["pool_zero"], 3)
                mm(bank(j)[0:n, 0:D], ones[:, 0:n], blin_b[0:1, :], start=True, stop=False)
                for c in range(KC):
                    last = mm(bank(j)[0:n, 0:D], patches[:, c, EB * NIMG * j:EB * NIMG * j + n], emb_w[:, c, :],
                              start=False, stop=(c == KC - 1))
                last.then_inc(s["emb_mm"], 1)
            pe.wait_ge(s["wdeq_ok"], 6)
            pe.wait_ge(s["cst_in"], 16)
            for c in range(2):
                for o in range(6):
                    last = tr(bank(3 + 2 * c + o // 3)[0:DC, DC * (o % 3):DC * (o % 3 + 1)],
                              wdeq[:, o, DC * c:DC * (c + 1)], ident[0:DC, 0:DC])
            last.then_inc(s["wT_mm"], 1)
            pe.wait_ge(s["wproj_ok"], 1)
            pe.wait_ge(s["cst_b"], 2)
            for c in range(2):
                for o in range(2):
                    tr(bankb(7)[0:DC, D * c + DC * o:D * c + DC * (o + 1)], wproj_n[:, o, DC * c:DC * (c + 1)],
                       ident_b[0:DC, 0:DC])
            for o in range(2):
                last = tr(bank(7)[:, 256 + DC * o:256 + DC * (o + 1)], wst[:, 6 + o, 2:3].to_broadcast([DC, P]),
                          ident[0:DC, 0:DC])
            last.then_inc(s["wT_mm"], 1)
            def turn(t, src, ready, banks=(0, 1)):
                R = rows(t)
                pe.wait_ge(s[ready[0]], ready[1])
                for c in range(2):
                    last = tr(bank(banks[t % len(banks)])[0:DC, P * c:P * c + R], src[0:R, t, DC * c:DC * (c + 1)], ident[0:R, 0:R])
                last.then_inc(s["xnT_mm"], 1)

            def qkv(t):
                R = rows(t)
                pe.wait_ge(s["xT_ok"], t + 1)
                if t >= 3:
                    pe.wait_ge(s["y_ok"], t - 2)
                for a in range(2):
                    for c in range(2):
                        last = mm(bank(2 + 2 * (t % 3) + a)[0:R, 0:QKV // 2], xT[:, c, P * t:P * t + R],
                                  wqkvT[:, c, QKV // 2 * a:QKV // 2 * (a + 1)], start=(c == 0), stop=(c == 1))
                last.then_inc(s["qkv_mm"], 1)

            for t in range(T + 1):
                if t < T:
                    if t >= 2:
                        pe.wait_ge(s["xT_ok"], t - 1)
                    else:
                        pe.wait_ge(s["emb_sb"], t + 1)
                    turn(t, xn, ("xn_ok", t + 1))
                if t == 1:
                    pe.wait_ge(s["wT_ok"], 2)
                if t == 3:
                    pe.wait_ge(s["wT_ok"], 4)
                if t >= 1:
                    qkv(t - 1)

            def global_stat(n):
                pe.wait_ge(s["g_col"], n)
                for a in range(2):
                    last = tr(bank(7)[:, P * a:P * (a + 1)], gcol[:, a:a + 1].to_broadcast([P, P]), ident)
                last.then_inc(s["g_T"], 1)

            global_stat(1)
            for t in range(T):
                R = rows(t)
                pe.wait_ge(s["copy_a"], 1 if t < TQ else 2)
                pe.wait_ge(s["copy_b"], 1 if t < TQ else 2)
                for k, name, ok in ((0, "qT_mm", "q_ok"), (1, "kT_mm", "k_ok")):
                    if t >= 2:
                        pe.wait_ge(s[ok], t - 1)
                    for g in range(HG):
                        last = tr(bankb(2 * k + t % 2)[:, P * g:P * g + R], qk2[0:R, t, HG * k + g, :], ident_b[0:R, 0:R])
                    last.then_inc(s[name], 1)
            def banks_of(t):
                return range(HQ) if t < T - 1 else range(1)

            def row_maxima(t, j, start):
                return mm(bank(j)[:, 0:HG * N], nbT[32 * j:32 * j + 3 * HG, P * t:P * (t + 1)], sel_b[32 * j:32 * j + 3 * HG, :],
                          start=start, stop=True, skip_group_check=not start)

            def add_scores(t, jj):
                for j, g, prt, col, qs, keys in scores_of(t):
                    if j == jj or t == T - 1:
                        for k in keys:
                            last = mm(bank(0 if t == T - 1 else j)[prt, col], qs, k, start=False, stop=True, skip_group_check=True)
                return last

            for t in range(T):
                R = rows(t)
                need = min(T, (N * (first_batch(t) + batches(t)) - 1) // P + 1) if t == 0 else T
                pe.wait_ge(s["q_ok"], need)
                pe.wait_ge(s["k_ok"], need)
                if t >= 2:
                    pe.wait_ge(s["s0_read"], t - 1)
                for j, g, prt, col, qs, keys in scores_of(t):
                    for k in keys:
                        last = mm(bank(4 * ((t + 1) % 2) + j)[prt, col], qs, k, start=(k is keys[0]), stop=(k is keys[-1]))
                last.then_inc(s["s0_mm"], 1)
            pe.wait_ge(s["s0_read"], T - 1)
            for j in range(HQ):
                mm(bank(j)[:, 0:HG * N], zeros, sel_b, start=True, stop=True)
                add_scores(0, j)
            global_stat(2)
            pe.wait_ge(s["nb_ok"], 1)
            for t in range(T):
                last = tr(bankb(6)[:, 0:P] if t == 0 else bankb(4, 2)[:, P * t:P * (t + 1)], nb_parts[:, t, :], ident_b)
                if t == 0 or t == T - 1:
                    last.then_inc(s["nbT_mm"], 1)
            pe.wait_ge(s["nbT_ok"], 1)

            def scores(t):
                if t > FEW:
                    pe.wait_ge(s["m_ok"], t - FEW)
                for j in banks_of(t):
                    if t <= FEW:
                        pe.wait_ge(s["m0_read"], HQ * (t - 1) + j + 1)
                    row_maxima(t, j, True)
                    last = add_scores(t, j)
                    if t < FEW:
                        last.then_inc(s["s_mm"], 1)
                if t >= FEW:
                    last.then_inc(s["s_mm"], 1)

            def turn_probs(t):
                pe.wait_ge(s["p_ok"], 2 * (t + 1))
                if t >= 1:
                    pe.wait_ge(s["pT_ok"], t)
                pr, n0 = bufs["q", t % 2].bitcast(bf16), P * units(t)
                for u in range(units(t)):
                    tr(bankb(4, 2)[:, P * u:P * (u + 1)], pr[:, P * u:P * (u + 1)], ident_b)
                for j in range(units(t) // HG):
                    last = tr(bankb(4, 2)[0:HG * KR, P * (H + j):P * (H + j + 1)], pr[:, n0 + HG * KR * j:n0 + HG * KR * (j + 1)],
                              ident_b)
                last.then_inc(s["pT_mm"], 1)

            def attend(t):
                b, nb_, R = first_batch(t), batches(t), rows(t)
                pe.wait_ge(s["pT_ok"], t + 1)
                if t == 0:
                    pe.wait_ge(s["v_in"], 16 * (1 + HG * B))
                if t >= 2:
                    pe.wait_ge(s["o_ok"], t - 1)
                o = bank(6 + t % 2)[0:R, 0:nb_ * D].rearrange("p (b c) -> p b c", b=nb_)
                for j in range(HQ):
                    if t < T - 1:
                        rest, main = probsT[0:HG * KR, H + j, :], [probsT[:, HG * j + g, :] for g in range(HG)]
                    else:
                        qs = slice(LAST * j, LAST * (j + 1))
                        rest, main = probsT[0:HG * KR, H, qs], [probsT[:, g, qs] for g in range(HG)]
                    mm(o[:, :, HG * HD * j:HG * HD * (j + 1)], rest, vrest[0:HG * KR, b:b + nb_, j, :],
                       start=True, stop=True)
                    for g in range(HG):
                        u = HG * j + g
                        last = mm(o[:, :, HD * u:HD * (u + 1)], main[g], vmain[:, b:b + nb_, u, :],
                                  start=False, stop=True, skip_group_check=True)
                last.then_inc(s["o_mm"], 1)

            for j in range(HQ):
                row_maxima(0, j, False).then_inc(s["s_mm"], 1)
            pe.wait_ge(s["nbT_ok"], 2)
            for i in range(T + 4):
                if i + 1 < T:
                    scores(i + 1)
                if i >= 4:
                    attend(i - 4)
                if 3 <= i < T + 3:
                    turn_probs(i - 3)
            global_stat(3)
            for t in range(T + 2):
                if t < T:
                    R = rows(t)
                    pe.wait_ge(s["obf_ok"], 1 if t < 3 else 2)
                    if t >= 3:
                        pe.wait_ge(s["oT_ok"], t - 2)
                    for c in range(2):
                        last = tr(bankb(OT[t % 3])[0:DC, P * c:P * c + R], obf[0:R, t, DC * c:DC * (c + 1)], ident_b[0:R, 0:R])
                    last.then_inc(s["oT_mm"], 1)
                if t >= 2:
                    u, R = t - 2, rows(t - 2)
                    pe.wait_ge(s["oT_ok"], u + 1)
                    if u >= 4:
                        pe.wait_ge(s["y2_ok"], u - 3)
                    for c in range(2):
                        last = mm(bank(2 + u % 4)[0:R, 0:D], oT[:, c, P * u:P * u + R], wprojT[:, c, :],
                                  start=(c == 0), stop=(c == 1))
                    last.then_inc(s["pr_mm"], 1)
            global_stat(4)
            warm(WARM[1])
            def turn_logits(c):
                pe.wait_ge(s["lgT_ok"], c + 1)
                for t in range(4 * c, min(4 * c + 4, T)):
                    last = tr(bank(2)[0:rows(t), EXP * t:EXP * (t + 1)], lgT[:, P * t:P * t + rows(t)], ident[0:EXP, 0:EXP])
                return last

            for c in range(NB):
                for t in range(4 * c, min(4 * c + 4, T)):
                    pe.wait_ge(s["xT_ok"], T + max(t - 3, 0))
                    turn(t, xf, ("xf_ok", t + 1), (0, 1, 3, 4))
                if c >= 1:
                    turn_logits(c - 1)
                pe.wait_ge(s["xT_ok"], T + min(4 * c + 4, T))
                lo, hi = 512 * c, min(512 * (c + 1), TOK)
                for k in range(2):
                    last = mm(bank(5 + c)[0:EXP, 0:hi - lo], sww_s[:, k, :], xT[:, k, lo:hi], start=(k == 0), stop=(k == 1))
                last.then_inc(s["lgT_mm"], 1)
            turn_logits(NB - 1).then_inc(s["lg_mm"], 1)
            pe.wait_ge(s["p_col"], 1)
            for t in range(T):
                R = rows(t)
                last = tr(bank(3, 3)[:, P * t:P * t + R], rt[0:R, 2, t:t + 1].to_broadcast([R, P]), ident[0:R, 0:R])
                if P * (t + 1) % 512 == 0 or t == T - 1:
                    last.then_inc(s["prow_mm"], 1)
            for half in range(2):
                mm(bank(6 + half)[:, 0:T * EXP], ident_b, zeros[:, 0:T * EXP], start=True, stop=True)
            n = 0
            for half in range(2):
                todo = [t for _, t, _, _ in compares(half)]
                for t in range(T):
                    R = rows(t)
                    pe.wait_ge(s["cmp_ok"], n + len(todo) - todo[::-1].index(t))
                    for i in range((0, TH)[half], (TH, T)[half]):
                        last = mm(bank(6 + half)[0:rows(i), EXP * i:EXP * (i + 1)], G[0:R, t, P * i:P * i + rows(i)],
                                  onehot[0:R, t, :], start=False, stop=True, skip_group_check=True)
                last.then_inc(s["cnt_mm"], 1)
                n += len(todo)

            def expert_turn(e):
                if e <= 1:
                    pe.wait_ge(s["xe_first" if e == 0 else "xe_in"], 16 if e == 0 else 16 * (EXP - 1))
                if e >= 1:
                    pe.wait_ge(s["xeT_ok"], e)
                for c in range(2):
                    for a in range(2):
                        last = tr(bank(0)[0:DC, SLOTS * c + HALF * a:SLOTS * c + HALF * (a + 1)],
                                  xe[0:HALF, e, a, DC * c:DC * (c + 1)], ident[0:HALF, 0:HALF])
                last.then_inc(s["xeT_mm"], 1)

            def expert_in(e):
                pe.wait_ge(s["xeT_ok"], e + 1)
                if e == 0:
                    pe.wait_ge(s["ffn_in"], 48)
                if e == HE:
                    pe.wait_ge(s["ffn_in2"], 48)
                for f in range(FC):
                    if e >= 2 and f % 2 == 0:
                        pe.wait_ge(s["h_ok"], 3 * (e - 2) + f // 2 + 1)
                    for c in range(2):
                        last = mm(bank(2 + 3 * (e % 2) + f // 2)[:, SLOTS * (f % 2):SLOTS * (f % 2 + 1)],
                                  w1_of(e)[:, c, P * f:P * (f + 1)], xeT[0:DC, e % 2, c, :], start=(c == 0), stop=(c == 1))
                    if f % 2:
                        last.then_inc(s["h_mm"], 1)

            def expert_out(e):
                pe.wait_ge(s["h_ok"], 3 * (e + 1))
                if e >= 1:
                    pe.wait_ge(s["oe_read"], e)
                for a in range(2):
                    o = bank(1)[0:HALF, D * a:D * (a + 1)]
                    for f in range(FC):
                        last = mm(o, hT[:, e % 2, f, HALF * a:HALF * (a + 1)], w2_of(e)[:, f, :],
                                  start=(f == 0), stop=(f == FC - 1))
                last.then_inc(s["oe_mm"], 1)

            pe.wait_ge(s["slot_ok"], 2)
            warm(WARM[2])
            expert_turn(0)
            expert_in(0)
            expert_turn(1)
            for e in range(EXP):
                if e + 1 < EXP:
                    expert_in(e + 1)
                if e + 2 < EXP:
                    expert_turn(e + 2)
                expert_out(e)

        @block.scalar
        def _(act):
            A = nc.scalar.activation
            act.dma_start(wall, wqkv).then_inc(s["w_in"], 16)
            act.preload_act_table_set("sqrt_and_others")
            for j in range(ET):
                n = min(EB, B - EB * j) * NIMG
                if j == 2:
                    for o in range(6):
                        act.wait_ge(s["wint_ok"], o + 1)
                        A(wdeq[:, o, :], wdeq[:, o, :], ACT.Copy, scale=wst[:, o, 2:3]).then_inc(s["wdeq_ok"], 1)
                act.wait_ge(s["emb_mm"], j + 1)
                A(emb[0:n, j, :], bank(j)[0:n, 0:D], ACT.Copy).then_inc(s["emb_sb"], 1)

            def deviation(c, n, chunks=LNT):
                t0, t1 = chunks[c]
                act.wait_ge(s["var_ok"], n + 1)
                A(std[:, t0:t1], var[:, t0:t1], ACT.Sqrt).then_inc(s["std_ok"], 1)

            deviation(0, 0)
            act.wait_ge(s["wT_mm"], 1)
            for c in range(2):
                A(wqkvT[:, c, :].rearrange("p (a o) -> p a o", a=2),
                  bank(3 + 2 * c, 2).rearrange("p (a o) -> p a o", a=2)[0:DC, :, 0:QKV // 2], ACT.Copy).then_inc(s["wT_ok"], 1)

            def keep_turned(t, n, banks=(0, 1)):
                R = rows(t)
                act.wait_ge(s["xnT_mm"], n + 1)
                A(xT[:, :, P * t:P * t + R], bank(banks[t % len(banks)])[0:DC, 0:2 * P].rearrange("p (c n) -> p c n", c=2)[:, :, 0:R],
                  ACT.Copy).then_inc(s["xT_ok"], 1)

            for t in range(T):
                if t == 2:
                    act.wait_ge(s["wT_mm"], 2)
                    A(wprojT[:, :, :].rearrange("p c o -> p (c o)"), bankb(7)[0:DC, 0:2 * D], ACT.Copy).then_inc(s["wT_ok"], 1)
                    A(proj_scale[:, :], bank(7)[:, 256:256 + D], ACT.Copy).then_inc(s["wT_ok"], 1)
                    deviation(1, 1)
                if t == 4:
                    deviation(2, 2)
                keep_turned(t, t)
            for n, (t0, t1) in enumerate(((0, TQ), (TQ, T))):
                act.wait_ge(s["yint_ok"], n + 1)
                A(qk2.rearrange("p t k (j a d) -> p t (k j) a d", j=HQ, a=2)[:, t0:t1, :, 1, :],
                  yint[:, t0:t1, 0:2 * D].rearrange("p t (x d) -> p t x d", d=HD), ACT.Copy).then_inc(s["copy_b"], 1)
            act.wait_ge(s["cst_in"], 16)
            for t in range(T):
                act.wait_ge(s["kT_mm"], t + 1)
                lo = P * t
                for b in range(first_batch(t), first_batch(t) + batches(t)):
                    hi = min(N * (b + 1), P * t + rows(t))
                    last = A(kT[:, :, lo:hi],
                             bankb(2 + t % 2)[:, 0:HG * P].rearrange("p (g n) -> p g n", g=HG)[:, :, lo - P * t:hi - P * t],
                             ACT.Copy, scale=parity[:, N * b:N * b + 1])
                    lo = hi
                last.then_inc(s["k_ok"], 1)
            A(yint.bitcast(bf16)[:, :, 2 * D:], yint[:, :, 2 * D:], ACT.Copy).then_inc(s["v_int"], 1)
            act.preload_act_table_set("natural_log_exp_and_others")
            act.wait_ge(s["nbT_mm"], 1)
            A(nbT[:, 0:P], bankb(6)[:, 0:P], ACT.Copy).then_inc(s["nbT_ok"], 1)
            act.wait_ge(s["nbT_mm"], 2)
            A(nbT[:, P:], bankb(4, 2)[:, P:T * P], ACT.Copy).then_inc(s["nbT_ok"], 1)

            def distance(t):
                if t == 0:
                    act.wait_ge(s["k_at"], 1)
                    act.wait_ge(s["v_out"], 32)
                if t >= 2:
                    act.wait_ge(s["r_ok"], t - 1)
                m = bufs["m", t % 2][:, 0:units(t) * N]
                if t < T - 1:
                    m = m.rearrange("p (a c) -> p a c", a=4)
                if t < FEW:
                    for j in range(HQ):
                        act.wait_ge(s["s_mm"], HQ * t + j + 1)
                        A(m[:, j], bank(j)[:, 0:HG * N], ACT.Relu, scale=sc[:, 5:6], bias=sc[:, 24:25]).then_inc(s["m0_read"], 1)
                    return
                act.wait_ge(s["s_mm"], HQ * FEW + t - FEW + 1)
                A(m, scores_view(t, 0), ACT.Relu, scale=sc[:, 5:6], bias=sc[:, 24:25]).then_inc(s["m_ok"], 1)

            def square(t):
                act.wait_ge(s["r_ok"], t + 1)
                if t == 0:
                    act.wait_ge(s["half_b"], 1)
                if t >= 2:
                    act.wait_ge(s["e_ok"], t - 1)
                n = units(t) * N
                A(bufs["w", t % 2][:, 0:n], bufs["r", t % 2][:, 0:n], ACT.Square, bias=sc[:, 26:27]).then_inc(s["w_ok"], 1)

            def invert(t):
                k = t % 2
                e = bufs["e", k][:, 0:units(t) * N]
                act.wait_ge(s["e_ok"], t + 1)
                A(e, e, ACT.Ln).then_inc(s["act_order"], 1)
                A(lnS[:, k], S[:, k, 0:UA], ACT.Ln).then_inc(s["act_order"], 1)
                act.wait_ge(s["act_order"], 2 * (t + 1))
                if units(t) > UA:
                    A(e[:, UA * N:], e[:, UA * N:], ACT.Exp, scale=-1.0)
                if t >= 2:
                    act.wait_ge(s["p_ok"], 2 * (t - 1))
                for u in range(UA):
                    last = A(bufs["x", k][:, u * N:(u + 1) * N], e[:, u * N:(u + 1) * N], ACT.Exp, scale=-1.0, bias=lnS[:, k, u:u + 1])
                last.then_inc(s["inv_ok"], 1)

            def keep_probs(t):
                act.wait_ge(s["pT_mm"], t + 1)
                if t >= 1:
                    act.wait_ge(s["o_mm"], t)
                n, k = units(t), units(t) // HG
                A(probsT[:, 0:n, :].rearrange("p u n -> p (u n)"), bankb(4, 2)[:, 0:P * n], ACT.Copy)
                A(probsT[0:HG * KR, H:H + k, :].rearrange("p u n -> p (u n)"),
                  bankb(4, 2)[0:HG * KR, P * H:P * (H + k)], ACT.Copy).then_inc(s["pT_ok"], 1)

            def first_of_out(t):
                R = rows(t)
                act.wait_ge(s["o_mm"], t + 1)
                A(obuf[0:R, t, :], bank(6 + t % 2)[0:R, 0:D], ACT.Copy, scale=batch_sel[0:R, t, 0:1]).then_inc(s["o_first"], 1)

            act.wait_ge(s["nb_free"], 1)
            distance(0)
            for i in range(T + 4):
                if i + 1 < T:
                    distance(i + 1)
                if i >= 4:
                    first_of_out(i - 4)
                if 3 <= i < T + 3:
                    keep_probs(i - 3)
                if i < T:
                    square(i)
                if 1 <= i <= T:
                    invert(i - 1)
            act.preload_act_table_set("sqrt_and_others")
            for t in range(T):
                R = rows(t)
                act.wait_ge(s["oT_mm"], t + 1)
                A(oT[:, :, P * t:P * t + R], bankb(OT[t % 3])[0:DC, 0:2 * P].rearrange("p (c n) -> p c n", c=2)[:, :, 0:R],
                  ACT.Copy).then_inc(s["oT_ok"], 1)
            deviation(0, 3, LNT2)
            for t in range(T):
                if t in (LNT2[1][0], LNT2[2][0]):
                    deviation(t // 4, 3 + t // 4, LNT2)
                keep_turned(t, T + t, (0, 1, 3, 4))
                if t in (4, 8, T - 1):
                    c = t // 4 - (t < T - 1)
                    lo, hi = 512 * c, min(512 * (c + 1), TOK)
                    act.wait_ge(s["lgT_mm"], c + 1)
                    A(lgT[:, lo:hi], bank(5 + c)[0:EXP, 0:hi - lo], ACT.Copy).then_inc(s["lgT_ok"], 1)
            act.preload_act_table_set("natural_log_exp_and_others")
            act.wait_ge(s["lg_ok"], 1)
            A(lg[:, 3, :, :], lg[:, 2, :, :], ACT.Exp).then_inc(s["ex_ok"], 1)
            for c in range(NB):
                act.wait_ge(s["prow_mm"], c + 1)
                lo, hi = 512 * c, min(512 * (c + 1), TOK)
                A(prow[:, lo:hi], bank(3 + c)[:, 0:hi - lo], ACT.Copy).then_inc(s["prow_ok"], 1)
            act.preload_act_table_set("gelu_and_others")
            for e in range(EXP):
                for f in range(FC):
                    if f % 2 == 0:
                        act.wait_ge(s["h_mm"], 3 * e + f // 2 + 1)
                        if e >= 2:
                            act.wait_ge(s["oe_mm"], e - 1)
                    last = A(hT[:, e % 2, f, :], bank(2 + 3 * (e % 2) + f // 2)[:, SLOTS * (f % 2):SLOTS * (f % 2 + 1)],
                             ACT.Gelu, bias=b1_s[:, e, f:f + 1])
                    if f % 2:
                        last.then_inc(s["h_ok"], 1)

        @block.vector
        def _(dve):
            v = nc.vector
            made = {n: 0 for n in names}

            def done(ins, what="dve_order"):
                made[what] += 1
                ins.then_inc(s[what], 1)
                dve.wait_ge(s[what], made[what])

            dve.wait_ge(s["w_in"], 16)
            W = [wst[:, :, k] for k in range(5)]
            done(v.tensor_reduce(W[0], wall, AX.X, ALU.max))
            done(v.tensor_reduce(W[1], wall, AX.X, ALU.min, negate=True))
            done(v.tensor_scalar(wst[:, :, 0:2], wst[:, :, 0:2], 0.0, None, ALU.max))
            done(v.tensor_tensor(W[2], W[0], W[1], ALU.add))
            done(v.tensor_scalar(W[2], W[2], 1.0 / 255.0, EPS, ALU.mult, ALU.max))
            done(v.reciprocal(W[3], W[2]))
            done(v.tensor_tensor(W[4], W[1], W[3], ALU.mult))
            done(v.tensor_scalar(W[4], W[4], -1.0, MAGIC, ALU.mult, ALU.add))
            done(v.tensor_scalar(W[4], W[4], 255.0 - MAGIC, None, ALU.add))
            for o in range(8):
                v.tensor_scalar(wdeq[:, o, :], wall[:, o, :], wst[:, o, 3:4], MAGIC, ALU.mult, ALU.add).then_inc(s["dve_order"], 1)
                made["dve_order"] += 1
            dve.wait_ge(s["dve_order"], made["dve_order"])
            for o in range(6):
                v.tensor_scalar(wdeq[:, o, :], wdeq[:, o, :], MAGIC, wst[:, o, 4:5], ALU.subtract, ALU.min).then_inc(s["wint_ok"], 1)
            for o in range(2):
                last = v.tensor_scalar(wproj_n[:, o, :], wdeq[:, 6 + o, :], MAGIC, wst[:, 6 + o, 4:5], ALU.subtract, ALU.min)
            last.then_inc(s["wproj_ok"], 1)
            dve.wait_ge(s["cst_in"], 16)
            v.tensor_copy(ident_b[:, :], ident).then_inc(s["cst_b"], 1)
            v.tensor_copy(sel_b[:, :], cst[:, C_SEL:C_SEL + HG * N]).then_inc(s["cst_b"], 1)

            def layer_norm(dst, ok, t0, t1):
                for t in range(t0, t1):
                    v.bn_stats(stat[:, t, :], h[:, t, :]).then_inc(s["dve_order"], 1)
                made["dve_order"] += t1 - t0
                dve.wait_ge(s["dve_order"], made["dve_order"])
                for t in range(t0, t1):
                    v.bn_aggr(mv[:, t, :], stat[:, t, :]).then_inc(s["dve_order"], 1)
                made["dve_order"] += t1 - t0
                dve.wait_ge(s["dve_order"], made["dve_order"])
                v.tensor_scalar(var[:, t0:t1], mv[:, t0:t1, 1], LNEPS, None, ALU.add).then_inc(s["var_ok"], 1)
                made["std_ok"] += 1
                dve.wait_ge(s["std_ok"], made["std_ok"])
                done(v.reciprocal(rstd[:, t0:t1], std[:, t0:t1]))
                for t in range(t0, t1):
                    v.tensor_scalar(dst[:, t, :], h[:, t, :], mv[:, t, 0:1], rstd[:, t:t + 1],
                                    ALU.subtract, ALU.mult).then_inc(s[ok], 1)

            def qkv_out(t):
                R = rows(t)
                dve.wait_ge(s["qkv_mm"], t + 1)
                done(v.tensor_tensor_reduce(y[0:R, t, :].rearrange("p (a c) -> p a c", a=2),
                                            bank(2 + 2 * (t % 3), 2).rearrange("p (a c) -> p a c", a=2)[0:R, :, 0:QKV // 2],
                                            bqkv_b[0:R].rearrange("p (a c) -> p a c", a=2), 1.0, 0.0, ALU.add, ALU.max,
                                            ymax[0:R, t:t + 1]), "y_ok")
                v.tensor_reduce(ymin[:, t:t + 1], y[:, t, :], AX.X, ALU.min).then_inc(s["dve_order"], 1)
                made["dve_order"] += 1

            dve.wait_ge(s["txt_in"], 16 * len(text))
            dve.wait_ge(s["pool_zero"], 8)
            dve.wait_ge(s["bias_in"], 64)
            dve.wait_ge(s["h_in0"], 16 * sum(im[0] == 0 for im in image))
            layer_norm(xn, "xn_ok", *LNT[0])
            dve.wait_ge(s["h_in1"], 16 * sum(im[0] == 1 for im in image))
            layer_norm(xn, "xn_ok", *LNT[1])
            for t in range(T):
                if t == 2:
                    dve.wait_ge(s["h_in2"], 16 * sum(im[0] == 2 for im in image))
                    layer_norm(xn, "xn_ok", *LNT[2])
                qkv_out(t)
            dve.wait_ge(s["dve_order"], made["dve_order"])

            def quantiser(at, mx, mn, kappa=None, kappa255=None):
                dve.wait_ge(s["dve_order"], made["dve_order"])
                done(v.tensor_reduce(gcol[:, 0:1], mx, AX.X, ALU.max))
                done(v.tensor_reduce(gcol[:, 1:2], mn, AX.X, ALU.min, negate=True), "g_col")
                made["g_T"] += 1
                dve.wait_ge(s["g_T"], made["g_T"])
                done(v.tensor_reduce(gred, bank(7)[:, 0:2 * P].rearrange("p (a n) -> p a n", a=2), AX.X, ALU.max))
                scale, ratio, top, inverse = (sc[:, at + k:at + k + 1] for k in range(4))
                done(v.tensor_scalar(gred, gred, 0.0, None, ALU.max))
                done(v.tensor_tensor(scale, gred[:, 0:1], gred[:, 1:2], ALU.add))
                done(v.tensor_scalar(scale, scale, 1.0 / 255.0 if kappa is None else kappa255, EPS, ALU.mult, ALU.max))
                if kappa is None:
                    done(v.reciprocal(ratio, scale))
                else:
                    done(v.reciprocal(inverse, scale))
                    done(v.tensor_scalar(ratio, inverse, kappa, None, ALU.mult))
                done(v.scalar_tensor_tensor(top, gred[:, 1:2], -1.0, ratio, ALU.mult, ALU.mult))
                done(v.tensor_scalar(top, top, MAGIC, 255.0 - MAGIC, ALU.add, ALU.add))

            quantiser(0, ymax, ymin)
            for t0, t1 in ((0, TQ), (TQ, T)):
                done(v.tensor_scalar(yint[:, t0:t1, :], y[:, t0:t1, :], sc[:, 1:2], sc[:, 2:3], ALU.mult, ALU.min), "yint_ok")
                v.tensor_copy(qk2.rearrange("p t k (j a d) -> p t (k j) a d", j=HQ, a=2)[:, t0:t1, :, 0, :],
                              yint[:, t0:t1, 0:2 * D].rearrange("p t (x d) -> p t x d", d=HD)).then_inc(s["copy_a"], 1)
            for t in range(T):
                R = rows(t)
                dve.wait_ge(s["qT_mm"], t + 1)
                v.tensor_tensor(qT[:, :, P * t:P * t + R],
                                bankb(t % 2)[:, 0:HG * P].rearrange("p (g n) -> p g n", g=HG)[:, :, 0:R],
                                parity[:, P * t:P * t + R].unsqueeze(1).to_broadcast([P, HG, R]), ALU.mult).then_inc(s["q_ok"], 1)
            sy = sc[:, 0:1]
            done(v.tensor_scalar(sc[:, 8:9], sy, sy, 0.25, ALU.mult, ALU.mult))
            done(v.tensor_scalar(sc[:, 9:10], sc[:, 8:9], 1.0 / 255.0, None, ALU.mult))
            done(v.tensor_scalar(sc[:, 10:11], sy, 1.0 / 255.0, None, ALU.mult))
            for t in range(T):
                dve.wait_ge(s["s0_mm"], t + 1)
                view = scores_view(t, 4 * ((t + 1) % 2))
                full = view.rearrange("p a (g n) -> p a g n", g=HG) if t < T - 1 else view.rearrange("p (g n) -> p g n", g=HG)
                mx = rmax[:, H * t:H * t + units(t)]
                v.tensor_reduce(mx.rearrange("p (a g) -> p a g", a=4) if t < T - 1 else mx, full, AX.X, ALU.max)
                v.tensor_reduce(ymin[:, t:t + 1], view, AX.XY if t < T - 1 else AX.X, ALU.min).then_inc(s["s0_read"], 1)
            dve.wait_ge(s["s0_read"], T)
            quantiser(4, rmax, ymin, sc[:, 8:9], sc[:, 9:10])
            dve.wait_ge(s["v_zero"], 2)
            done(v.tensor_scalar(nm, rmax, sc[:, 5:6], MAGIC, ALU.mult, ALU.add))
            done(v.tensor_scalar(nm, nm, MAGIC, sc[:, 6:7], ALU.subtract, ALU.min))
            done(v.reciprocal(sc[:, 29:30], sc[:, 5:6]))
            done(v.tensor_scalar(nb, nm, sc[:, 29:30], -1.0, ALU.mult, ALU.mult))
            part = [nb_parts.rearrange("p t (j c) -> p t j c", j=HQ)[:, :, :, k:k + 7:3] for k in range(3)]
            def cube(x):
                return x.rearrange("p (t j g) -> p t j g", j=HQ, g=HG)

            done(v.tensor_copy(part[0], cube(nb)))
            done(v.tensor_tensor(cube(nb2), cube(nb), part[0], ALU.subtract))
            done(v.tensor_copy(part[1], cube(nb2)))
            done(v.tensor_tensor(cube(nb3), cube(nb2), part[1], ALU.subtract))
            done(v.tensor_copy(part[2], cube(nb3)), "nb_ok")
            rs = sc[:, 7:8]
            C0 = 0.35815147
            v.tensor_scalar(sc[:, 12:13], rs, -0.6931, None, ALU.mult)
            v.tensor_scalar(sc[:, 13:14], rs, 0.96963238 / C0, None, ALU.mult)
            done(v.tensor_scalar(sc[:, 14:15], rs, rs, 1.0 / C0, ALU.mult, ALU.mult))
            done(v.tensor_scalar(sc[:, 15:18], sc[:, 12:15], MAGIC, -MAGIC, ALU.add, ALU.add))
            done(v.tensor_tensor(sc[:, 30:33], sc[:, 15:18], sc[:, 12:15], ALU.is_gt))
            done(v.tensor_tensor(sc[:, 15:18], sc[:, 15:18], sc[:, 30:33], ALU.subtract))
            done(v.tensor_scalar(sc[:, 24:25], sc[:, 15:16], -30.0, 256.0, ALU.mult, ALU.min), "k_at")
            v.tensor_scalar(sc[:, 27:28], sc[:, 16:17], 0.5, None, ALU.mult).then_inc(s["dve_order"], 1)
            done(v.tensor_scalar(sc[:, 21:22], sc[:, 15:16], -1.0, None, ALU.mult))
            made["dve_order"] += 1
            dve.wait_ge(s["dve_order"], made["dve_order"])
            v.tensor_scalar(sc[:, 22:23], sc[:, 24:25], 0.5, None, ALU.add).then_inc(s["dve_order"], 1)
            made["dve_order"] += 1
            done(v.reciprocal(sc[:, 20:21], sc[:, 21:22]))
            done(v.tensor_scalar(sc[:, 23:24], sc[:, 22:23], sc[:, 20:21], -0.5, ALU.mult, ALU.add))
            v.tensor_scalar(sc[:, 19:20], sc[:, 20:21], -1.0, None, ALU.mult).then_inc(s["dve_order"], 1)
            made["dve_order"] += 1
            done(v.tensor_tensor(sc[:, 26:27], sc[:, 27:28], sc[:, 24:25], ALU.subtract), "half_b")
            done(v.tensor_scalar(sc[:, 28:29], sc[:, 27:28], sc[:, 27:28], -1.0, ALU.mult, ALU.mult))
            done(v.tensor_tensor(sc[:, 28:29], sc[:, 28:29], sc[:, 17:18], ALU.add))
            dve.wait_ge(s["nbT_mm"], 2)
            done(v.memset(obuf[:, T - 1, :], 0.0), "nb_free")

            def quotient(t):
                k, n = t % 2, units(t) * N
                if t < FEW:
                    dve.wait_ge(s["m0_read"], HQ * (t + 1))
                else:
                    dve.wait_ge(s["m_ok"], t - FEW + 1)
                if t >= 4:
                    dve.wait_ge(s["pT_mm"], t - 3)
                v.tensor_scalar(bufs["q", k][:, 0:n], bufs["m", k][:, 0:n], sc[:, 19:20], sc[:, 23:24],
                                ALU.mult, ALU.add).then_inc(s["q_done"], 1)

            def times(t):
                k, n = t % 2, units(t) * N
                q = bufs["q", k][:, 0:n]
                dve.wait_ge(s["q_done"], t + 1)
                if t >= 2:
                    dve.wait_ge(s["w_ok"], t - 1)
                v.tensor_scalar(bufs["r", k][:, 0:n], q, sc[:, 21:22], None, ALU.mult).then_inc(s["qx_done"], 1)
                v.tensor_scalar(bufs["pw", k][:, 0:n], q, -128.0, 127.0 * 128.0, ALU.mult, ALU.add).then_inc(s["pw_ok"], 1)

            def rest(t):
                k, n = t % 2, units(t) * N
                dve.wait_ge(s["qx_done"], t + 1)
                r = bufs["r", k][:, 0:n]
                v.tensor_tensor(r, r, bufs["m", k][:, 0:n], ALU.add).then_inc(s["r_ok"], 1)

            def exps(t, us):
                k = t % 2
                if us[0] == 0:
                    dve.wait_ge(s["w_ok"], t + 1)
                    dve.wait_ge(s["pw_ok"], t + 1)
                for u in us:
                    if u < units(t):
                        ks = slice(N * u, N * (u + 1))
                        last = v.scalar_tensor_tensor(bufs["e", k][:, ks], bufs["w", k][:, ks], sc[:, 28:29],
                                                      bufs["pw", k].bitcast(bf16)[:, ks], ALU.add, ALU.mult,
                                                      accum_out=S[:, k, u:u + 1])
                        if u == units(t) - 1:
                            last.then_inc(s["e_ok"], 1)

            def ratios(t):
                k, u = t % 2, units(t)
                dve.wait_ge(s["inv_ok"], t + 1)
                if u > UA:
                    v.tensor_tensor(bufs["x", k][:, UA * N:u * N].rearrange("p (u n) -> p u n", n=N),
                                    bufs["e", k][:, UA * N:u * N].rearrange("p (u n) -> p u n", n=N),
                                    S[:, k, UA:u].unsqueeze(2).to_broadcast([P, u - UA, N]), ALU.mult).then_inc(s["x_done"], 1)

            def powers(t):
                x = bufs["x", t % 2][:, 0:units(t) * N]
                dve.wait_ge(s["x_done"], min(t + 1, T - 1))
                v.tensor_scalar(x.bitcast(bf16), x, RSCALE, None, ALU.mult).then_inc(s["pow_done"], 1)

            def probs(t):
                k, u = t % 2, units(t)
                dve.wait_ge(s["pow_done"], t + 1)
                xi = bufs["x", k][:, 0:u * N].bitcast(i16).rearrange("p (u n) -> p u n", n=N)
                p = bufs["q", k]
                for dst, ks in ((p[:, 0:P * u], slice(0, P)), (p[:, P * u:N * u], slice(P, N))):
                    v.tensor_scalar(dst.rearrange("p (u n) -> p u n", u=u), xi[:, :, ks], 0x7F80, 0x7F80,
                                    ALU.bitwise_xor, ALU.bitwise_and).then_inc(s["p_ok"], 1)

            def second_of_out(t):
                R = rows(t)
                dve.wait_ge(s["o_first"], t + 1)
                if batches(t) == 2:
                    v.scalar_tensor_tensor(obuf[0:R, t, :], bank(6 + t % 2)[0:R, D:2 * D], batch_sel[0:R, t, 1:2],
                                           obuf[0:R, t, :], ALU.mult, ALU.add).then_inc(s["o_ok"], 1)
                else:
                    v.engine_nop().then_inc(s["o_ok"], 1)

            def range_of(part, col, ok, n):
                dve.wait_ge(s[ok], n)
                v.tensor_reduce(ymax[:, col:col + 1], part, AX.XY, ALU.max).then_inc(s["dve_order"], 1)
                v.tensor_reduce(ymin[:, col:col + 1], part, AX.XY, ALU.min).then_inc(s["dve_order"], 1)
                made["dve_order"] += 2

            for i in range(T + 5):
                e = i - 1 if 1 <= i <= T else None
                x = i - 2 if 2 <= i <= T + 1 else None
                if i < T:
                    quotient(i)
                if e is not None:
                    exps(e, range(0, 4))
                if i < T:
                    times(i)
                if e is not None:
                    exps(e, range(4, 8))
                if i < T:
                    rest(i)
                if x is not None:
                    ratios(x)
                if e is not None:
                    exps(e, range(8, 12))
                if x is not None:
                    powers(x)
                if i >= 5:
                    second_of_out(i - 5)
                if i == T + 2:
                    range_of(obuf[:, 0:T - 2, :], 0, "o_ok", T - 2)
                if i == T + 4:
                    range_of(obuf[:, T - 2:, :], 1, "o_ok", T)
                if x is not None:
                    probs(x)
            quantiser(36, ymax[:, 0:2], ymin[:, 0:2], sy, sc[:, 10:11])
            for t0, t1 in ((0, 3), (3, T)):
                done(v.tensor_scalar(oint[:, t0:t1], obuf[:, t0:t1], sc[:, 37:38], sc[:, 38:39], ALU.mult, ALU.min))
                done(v.tensor_copy(obf[:, t0:t1], oint[:, t0:t1]), "obf_ok")
            done(v.tensor_scalar(proj_scale[:, :], proj_scale[:, :], sc[:, 36:37], None, ALU.mult))
            for t in range(T):
                R = rows(t)
                dve.wait_ge(s["pr_mm"], t + 1)
                v.tensor_tensor(obuf[0:R, t, :], bank(2 + t % 4)[0:R, 0:D], proj_scale[0:R, :], ALU.mult).then_inc(s["y2_ok"], 1)
                if t in Y2T:
                    n = Y2T.index(t)
                    range_of(obuf[:, YT[n]:YT[n + 1], :], n, "y2_sum", YT[n + 1])
            range_of(obuf[:, YT[-1]:, :], len(Y2T), "y2_sum", T)
            quantiser(44, ymax[:, 0:len(YT)], ymin[:, 0:len(YT)])
            dve.wait_ge(s["oT_mm"], T)
            done(v.tensor_scalar(y2int, obuf, sc[:, 45:46], sc[:, 46:47], ALU.mult, ALU.min))
            for t0, t1 in LNT2:
                done(v.scalar_tensor_tensor(h[:, t0:t1, :], y2int[:, t0:t1, :], sc[:, 44:45], h[:, t0:t1, :], ALU.mult, ALU.add))
                layer_norm(xf, "xf_ok", t0, t1)
            v.tensor_copy(xs[:, :, 2 * D], token_no).then_inc(s["xf_ok"], 1)
            dve.wait_ge(s["lg_mm"], 1)
            L = [lg[:, k, :, :] for k in range(6)]

            def wide(col):
                return rt[:, col, :].unsqueeze(2).to_broadcast([P, T, EXP])

            for t0, t1, R in ((0, T - 1, P), (T - 1, T, LAST)):
                done(v.tensor_tensor(L[0][0:R, t0:t1], bank(2)[0:R, EXP * t0:EXP * t1].rearrange("p (t e) -> p t e", e=EXP),
                                     swb_b[0:R, :].unsqueeze(1).to_broadcast([R, t1 - t0, EXP]), ALU.add))
            done(v.tensor_reduce(rt[:, 0, :], L[0], AX.X, ALU.max))
            done(v.tensor_tensor(L[2], L[0], wide(0), ALU.subtract), "lg_ok")
            done(v.tensor_tensor(L[1], L[0], wide(0), ALU.is_equal))
            done(v.scalar_tensor_tensor(L[4], L[1], -float(EXP), expert_no, ALU.mult, ALU.add))
            dve.wait_ge(s["ex_ok"], 1)
            done(v.tensor_reduce(rt[:, 1, :], L[3], AX.X, ALU.add))
            done(v.reciprocal(rt[:, 2, :], rt[:, 1, :]), "p_col")
            v.tensor_copy(xs[:, :, 2 * D + 1], rt[:, 2, :]).then_inc(s["xf_ok"], 1)
            done(v.tensor_reduce(rt[:, 3, :], L[4], AX.X, ALU.min))
            for t0, t1, R in ((0, T - 1, P), (T - 1, T, LAST)):
                done(v.tensor_tensor(onehot[0:R, t0:t1, :], L[4][0:R, t0:t1],
                                     rt[0:R, 3, t0:t1].unsqueeze(2).to_broadcast([R, t1 - t0, EXP]), ALU.is_equal))

            def ties(t0, t1):
                for t in range(t0, t1):
                    R, lo, hi = rows(t), P * t, P * t + rows(t)
                    dve.wait_ge(s["prow_ok"], lo // 512 + 1)
                    v.scalar_tensor_tensor(tie[0:R, lo:hi], prow[0:R, lo:hi], rt[0:R, 2, t:t + 1], lower[0:R, 0:R],
                                           ALU.is_equal, ALU.mult).then_inc(s["tie_ok"], 1)

            def slots_of(t0, t1):
                for a, b, R in ((t0, min(t1, T - 1), P), (T - 1, T, LAST)):
                    if a < b <= t1:
                        done(v.tensor_tensor(L[5][0:R, a:b], bank(6 + (t0 > 0))[0:R, EXP * a:EXP * b].rearrange("p (t e) -> p t e", e=EXP),
                                             onehot[0:R, a:b, :], ALU.mult))
                r = rt[:, :, t0:t1]
                done(v.tensor_reduce(r[:, 4, :], L[5][:, t0:t1], AX.X, ALU.add))
                done(v.tensor_scalar(r[:, 5, :], r[:, 4, :], float(CAP), 1e6, ALU.is_ge, ALU.mult))
                done(v.tensor_tensor(r[:, 5, :], r[:, 5, :], r[:, 4, :], ALU.add))
                done(v.tensor_tensor(slot[:, t0:t1], r[:, 5, :], r[:, 6, :], ALU.add), "slot_ok")

            done(v.tensor_scalar(rt[:, 6, :], rt[:, 3, :], float(EXP), float(SLOTS), ALU.add, ALU.mult))
            n = 0
            for half in range(2):
                ties((0, TH)[half], (TH, T)[half])
                below = {}
                for kind, t, lo, hi in compares(half):
                    R, n = rows(t), n + 1
                    if kind == "tie":
                        dve.wait_ge(s["tie_ok"], t + 1)
                        dve.wait_ge(s["cmp_ok"], below[t])
                        ins = v.tensor_tensor(G[0:R, t, lo:hi], G[0:R, t, lo:hi], tie[0:R, lo:hi], ALU.add)
                    else:
                        if kind == "lt":
                            below[t] = n
                        ins = v.tensor_scalar(G[0:R, t, lo:hi], prow[0:R, lo:hi], rt[0:R, 2, t:t + 1], None,
                                              ALU.is_lt if kind == "lt" else ALU.is_le)
                    ins.then_inc(s["cmp_ok"], 1)
                dve.wait_ge(s["cnt_mm"], half + 1)
                slots_of((0, TH)[half], (TH, T)[half])
            done(v.tensor_scalar(rt[:, 7, :], rt[:, 4, :], float(CAP), None, ALU.is_ge))
            done(v.tensor_tensor(rt[:, 7, :], rt[:, 7, :], rt[:, 2, :], ALU.mult))
            for t in range(T):
                R = rows(t)
                v.scalar_tensor_tensor(obuf[0:R, t, :], xf[0:R, t, :], rt[0:R, 7, t:t + 1], h[0:R, t, :],
                                       ALU.mult, ALU.add).then_inc(s["out_ok"], 1)

            def keep_expert(e):
                dve.wait_ge(s["xeT_mm"], e + 1)
                if e >= 2:
                    dve.wait_ge(s["h_mm"], 3 * (e - 1))
                v.tensor_copy(xeT[0:DC, e % 2], bank(0)[0:DC, 0:2 * SLOTS].rearrange("p (c n) -> p c n", c=2)
                              ).then_inc(s["xeT_ok"], 1)

            keep_expert(0)
            dve.wait_ge(s["xe_in"], 16 * (EXP - 1))
            v.tensor_copy(whose, xe[0:HALF, :, :, 2 * D]).then_inc(s["whose_ok"], 1)
            keep_expert(1)
            dve.wait_ge(s["ffn_in2"], 48)
            for e in range(EXP):
                if e + 2 < EXP:
                    keep_expert(e + 2)
                dve.wait_ge(s["oe_mm"], e + 1)
                if e >= 2:
                    dve.wait_ge(s[("oe_out0", "oe_out1")[e % 2]], 32 * (e // 2))
                o = oe[0:HALF, e % 2]
                done(v.tensor_tensor(o, bank(1)[0:HALF, 0:2 * D].rearrange("p (a d) -> p a d", a=2),
                                     b2_s[0:HALF, e, :].unsqueeze(1).to_broadcast([HALF, 2, D]), ALU.add), "oe_read")
                for a in range(2):
                    v.scalar_tensor_tensor(o[:, a, :], o[:, a, :], xe[0:HALF, e, a, 2 * D + 1:2 * D + 2], xe[0:HALF, e, a, D:2 * D],
                                           ALU.mult, ALU.add).then_inc(s["oe_ok"], 1)


def constants():
    import numpy as np
    c = np.zeros((P, C_END), np.float32)
    p = np.arange(P)
    c[p, C_ID + p] = 1.0
    tok = np.arange(TOK)
    c[:, C_PAR:C_PAR + TOK] = ((p[:, None] // HD) % 2 == (tok[None, :] // N) % 2)
    for j in range(HQ):
        for g in range(HG):
            for k in range(3):
                c[32 * j + 3 * g + k, C_SEL + N * g:C_SEL + N * (g + 1)] = 1.0
    c[:, C_LOW:C_LOW + P] = p[:, None] < p[None, :]
    for t in range(T):
        b = np.minimum((P * t + p) // N, B - 1)
        c[:, C_BSEL + 2 * t] = (b == first_batch(t)) * PSCALE
        c[:, C_BSEL + 2 * t + 1] = (b != first_batch(t)) * PSCALE
    c[:, C_EXP:C_TOK] = np.tile(np.arange(EXP), T)[None, :]
    c[:, C_TOK:] = P * np.arange(T)[None, :] + p[:, None]
    return c


def kernel(x, txt, L0_tok_W_lin, L0_tok_b_lin, L0_attn_w_qkv, L0_attn_b_qkv, L0_attn_w_proj, L0_attn_b_proj,
           L0_ffn_switch_w, L0_ffn_switch_b, L0_ffn_w1, L0_ffn_b1, L0_ffn_w2, L0_ffn_b2):
    import numpy as np
    import concourse.bacc as bacc
    from concourse.bass_utils import run_bass_kernel_spmd

    hp = IMG // PATCH
    a = {}
    xs = np.asarray(x).reshape(B, CH, hp, PATCH, hp, PATCH).transpose(3, 5, 1, 0, 2, 4)
    a["x"] = xs.reshape(KC, P, B * NIMG).transpose(1, 0, 2)
    a["wlin"] = np.asarray(L0_tok_W_lin).T.reshape(KC, P, D).transpose(1, 0, 2)
    a["blin"] = np.asarray(L0_tok_b_lin)
    a["txt"] = np.asarray(txt)
    order = np.arange(D).reshape(HG, HQ, HD).transpose(1, 0, 2).reshape(-1)
    wq = np.asarray(L0_attn_w_qkv)
    bq = np.asarray(L0_attn_b_qkv)
    rows_ = np.concatenate([np.arange(2 * D), 2 * D + order])
    wq = np.concatenate([wq[rows_], np.asarray(L0_attn_w_proj)[:, order]], 0)
    a["wqkv"] = wq.reshape(8, DC, D).transpose(1, 0, 2)
    a["bqkv"] = bq[rows_]
    a["bproj"] = np.asarray(L0_attn_b_proj)
    a["sww"] = np.asarray(L0_ffn_switch_w).reshape(2, DC, EXP).transpose(1, 0, 2)
    a["swb"] = np.asarray(L0_ffn_switch_b)
    a["w1"] = np.asarray(L0_ffn_w1).reshape(EXP, 2, DC, F).transpose(2, 0, 1, 3)
    a["b1"] = np.asarray(L0_ffn_b1).reshape(EXP, FC, P).transpose(2, 0, 1)
    a["w2"] = np.asarray(L0_ffn_w2).reshape(EXP, FC, P, D).transpose(2, 0, 1, 3)
    a["b2"] = np.asarray(L0_ffn_b2)
    a["consts"] = constants()
    a = {k: np.ascontiguousarray(v) for k, v in a.items()}
    nc = bacc.Bacc("TRN2", target_bir_lowering=False, num_devices=1)
    ins = {k: nc.dram_tensor(k + "_dram", v.shape, mybir.dt.from_np(v.dtype), kind="ExternalInput").ap() for k, v in a.items()}
    out = nc.dram_tensor("out_dram", (TOK, D), mybir.dt.float32, kind="ExternalOutput").ap()
    fusion_kernel(nc, out=out, **ins)
    r = run_bass_kernel_spmd(nc, [{k + "_dram": v for k, v in a.items()}], core_ids=[0])
    return r.results[0]["out_dram"].reshape(B, N, D)
```
